# Optimizing a Trainium2 kernel written in Bass

```python
import numpy as np
import jax
import jax.numpy as jnp

def _softmax(x, axis=-1):
    return jax.nn.softmax(x, axis=axis)

def _gelu(x):
    return jax.nn.gelu(x, approximate=True)

def _silu(x):
    return jax.nn.silu(x)

def _sigmoid(x):
    return jax.nn.sigmoid(x)

def _layernorm(x, axis=-1, eps=1e-05):
    m = jnp.mean(x, axis=axis, keepdims=True)
    v = jnp.var(x, axis=axis, keepdims=True)
    return (x - m) / jnp.sqrt(v + eps)

def _scatter_add(tgt, idx, src, axis=0):
    return tgt.at[idx].add(src)

def _segment_sum(src, seg, n):
    return jax.ops.segment_sum(src, seg, n)
kernel_name = 'mk_adaln_d2_jaxref_r8_4f6504'

def setup_inputs(seed: int=0):
    np.random.seed(seed)
    _w = jnp.asarray

    def _L0_attn_setup():
        import jax, jax.numpy as jnp
        import numpy as np
        D_MODEL = 256
        NUM_HEADS = 16
        D_K = D_MODEL // NUM_HEADS
        SEQ = 256
        BATCH = 2
        THETA = 10000.0

        def _rope_tables(seq_len, d_k, theta, dtype):
            pos = jnp.arange(seq_len, dtype=dtype)[:, None]
            inv = theta ** (-(jnp.arange(0, d_k, 2, dtype=dtype) / d_k))
            ang = pos * inv
            sin = jnp.repeat(jnp.sin(ang), 2, axis=1)
            cos = jnp.repeat(jnp.cos(ang), 2, axis=1)
            return (sin, cos)

        def _apply_rope(x, sin, cos):
            xp = x.reshape(x.shape[:-1] + (x.shape[-1] // 2, 2))
            swapped = jnp.stack((-xp[..., 1], xp[..., 0]), axis=-1).reshape(x.shape)
            return x * cos + swapped * sin
        key = jax.random.key(seed)
        ks = jax.random.split(key, 5)
        s = 1.0 / np.sqrt(D_MODEL)
        return {'x': jax.random.normal(ks[0], (BATCH, SEQ, D_MODEL), jnp.float32), 'wq': jax.random.normal(ks[1], (D_MODEL, D_MODEL), jnp.float32) * s, 'wk': jax.random.normal(ks[2], (D_MODEL, D_MODEL), jnp.float32) * s, 'wv': jax.random.normal(ks[3], (D_MODEL, D_MODEL), jnp.float32) * s, 'wo': jax.random.normal(ks[4], (D_MODEL, D_MODEL), jnp.float32) * s}
    _L0_attn_in = _L0_attn_setup()

    def _L0_ffn_setup():
        import jax, jax.numpy as jnp
        import numpy as np
        D_IN = 256
        D_OUT = 256
        RANK = 16
        N_EXPERTS = 16
        MAX_EXPERTS = 32
        ROUTER_HID = 64
        TOPK = 2
        ALPHA = 1.0

        def _forward(x, W, bias, rw1, rb1, rw2, rb2, A, B, gates):
            lead = x.shape[:-1]
            x_flat = x.reshape(-1, D_IN)
            n = x_flat.shape[0]
            feat = jax.lax.stop_gradient(x_flat)
            h = jax.nn.silu(feat @ rw1.T + rb1)
            logits = (h @ rw2.T + rb2)[:, :N_EXPERTS] + gates[None, :]
            topv, topi = jax.lax.top_k(logits, TOPK)
            sm = jax.nn.softmax(topv, axis=-1)
            rows = jnp.arange(n)[:, None]
            coeff = jnp.zeros_like(logits).at[rows, topi].set(sm)
            base = x_flat @ W.T + bias
            xa = jnp.einsum('ni,eri->ner', x_flat, A)
            wxa = xa * coeff[:, :, None]
            delta = jnp.einsum('ner,eor->no', wxa, B)
            out = base + ALPHA * delta
            return out.reshape(*lead, D_OUT)
        key = jax.random.key(seed)
        ks = jax.random.split(key, 10)
        s = 0.02
        x = jax.random.normal(ks[0], (4, 512, D_IN), dtype=jnp.float32)
        W = jax.random.normal(ks[1], (D_OUT, D_IN), dtype=jnp.float32) * s
        bias = jax.random.normal(ks[2], (D_OUT,), dtype=jnp.float32) * s
        rw1 = jax.random.normal(ks[3], (ROUTER_HID, D_IN), dtype=jnp.float32) * s
        rb1 = jnp.zeros((ROUTER_HID,), dtype=jnp.float32)
        rw2 = jax.random.normal(ks[4], (MAX_EXPERTS, ROUTER_HID), dtype=jnp.float32) * s
        rb2 = jnp.zeros((MAX_EXPERTS,), dtype=jnp.float32)
        A = jax.random.normal(ks[5], (N_EXPERTS, RANK, D_IN), dtype=jnp.float32) * s
        B = jax.random.normal(ks[6], (N_EXPERTS, D_OUT, RANK), dtype=jnp.float32) * s
        gates = jnp.ones((N_EXPERTS,), dtype=jnp.float32)
        return {'x': x, 'W': W, 'bias': bias, 'rw1': rw1, 'rb1': rb1, 'rw2': rw2, 'rb2': rb2, 'A': A, 'B': B, 'gates': gates}
    _L0_ffn_in = _L0_ffn_setup()
    _L0_c = _w((lambda *s: np.random.randn(*s).astype(np.float32) * 0.05)(1, 256))
    _L0_wmod = _w((lambda *s: np.random.randn(*s).astype(np.float32) * 0.05)(256, 6 * 256) * 256 ** (-0.5))

    def _L1_attn_setup():
        import jax, jax.numpy as jnp
        import numpy as np
        BLOCK = 32
        key = jax.random.key(seed)
        ks = jax.random.split(key, 6)
        b, n, hid = (2, 512, 256)
        h, d = (16, 128)
        x = jax.random.normal(ks[0], (b, n, hid), dtype=jnp.float32)
        slope_rate = jax.random.uniform(ks[1], (h, 1, 1), dtype=jnp.float32)
        Wqkv = jax.random.normal(ks[2], (3 * h * d, hid), dtype=jnp.float32) * 0.02
        Wg = jax.random.normal(ks[3], (h * d, hid), dtype=jnp.float32) * 0.02
        norm_w = jnp.ones((h * d,), dtype=jnp.float32)
        Wo = jax.random.normal(ks[4], (hid, h * d), dtype=jnp.float32) * 0.02
        return {'x': x, 'slope_rate': slope_rate, 'Wqkv': Wqkv, 'Wg': Wg, 'norm_w': norm_w, 'Wo': Wo}
    _L1_attn_in = _L1_attn_setup()

    def _L1_ffn_setup():
        import jax, jax.numpy as jnp
        import numpy as np
        D_MODEL = 256
        D_EXPERT = 1024
        EPS = 1e-08

        def ternary_quant(w):
            scale = jnp.mean(jnp.abs(w)) + EPS
            q = jnp.clip(jnp.round(w / scale), -1.0, 1.0) * scale
            return w + jax.lax.stop_gradient(q - w)
        key = jax.random.key(seed)
        k_x, k_up, k_gate, k_down = jax.random.split(key, 4)
        std_in = 1.0 / np.sqrt(D_MODEL)
        std_exp = 1.0 / np.sqrt(D_EXPERT)
        return {'x': jax.random.normal(k_x, (4, 256, D_MODEL), dtype=jnp.float32), 'W_up': jax.random.normal(k_up, (D_EXPERT, D_MODEL), dtype=jnp.float32) * std_in, 'W_gate': jax.random.normal(k_gate, (D_EXPERT, D_MODEL), dtype=jnp.float32) * std_in, 'W_down': jax.random.normal(k_down, (D_MODEL, D_EXPERT), dtype=jnp.float32) * std_exp}
    _L1_ffn_in = _L1_ffn_setup()
    _L1_c = _w((lambda *s: np.random.randn(*s).astype(np.float32) * 0.05)(1, 256))
    _L1_wmod = _w((lambda *s: np.random.randn(*s).astype(np.float32) * 0.05)(256, 6 * 256) * 256 ** (-0.5))
    _d = {'L0_attn_x': _L0_attn_in['x'], 'L0_attn_wq': _L0_attn_in['wq'], 'L0_attn_wk': _L0_attn_in['wk'], 'L0_attn_wv': _L0_attn_in['wv'], 'L0_attn_wo': _L0_attn_in['wo'], 'L0_ffn_W': _L0_ffn_in['W'], 'L0_ffn_bias': _L0_ffn_in['bias'], 'L0_ffn_rw1': _L0_ffn_in['rw1'], 'L0_ffn_rb1': _L0_ffn_in['rb1'], 'L0_ffn_rw2': _L0_ffn_in['rw2'], 'L0_ffn_rb2': _L0_ffn_in['rb2'], 'L0_ffn_A': _L0_ffn_in['A'], 'L0_ffn_B': _L0_ffn_in['B'], 'L0_ffn_gates': _L0_ffn_in['gates'], 'L0_c': _L0_c, 'L0_wmod': _L0_wmod, 'L1_attn_slope_rate': _L1_attn_in['slope_rate'], 'L1_attn_Wqkv': _L1_attn_in['Wqkv'], 'L1_attn_Wg': _L1_attn_in['Wg'], 'L1_attn_norm_w': _L1_attn_in['norm_w'], 'L1_attn_Wo': _L1_attn_in['Wo'], 'L1_ffn_W_up': _L1_ffn_in['W_up'], 'L1_ffn_W_gate': _L1_ffn_in['W_gate'], 'L1_ffn_W_down': _L1_ffn_in['W_down'], 'L1_c': _L1_c, 'L1_wmod': _L1_wmod}
    _x0 = _d['L0_attn_x']
    _d['L0_attn_x'] = jax.random.normal(jax.random.fold_in(jax.random.key(seed), 1), (1, 2048, 256), dtype=_x0.dtype)
    del _x0
    return _d

def reference(L0_attn_x, L0_attn_wq, L0_attn_wk, L0_attn_wv, L0_attn_wo, L0_ffn_W, L0_ffn_bias, L0_ffn_rw1, L0_ffn_rb1, L0_ffn_rw2, L0_ffn_rb2, L0_ffn_A, L0_ffn_B, L0_ffn_gates, L0_c, L0_wmod, L1_attn_slope_rate, L1_attn_Wqkv, L1_attn_Wg, L1_attn_norm_w, L1_attn_Wo, L1_ffn_W_up, L1_ffn_W_gate, L1_ffn_W_down, L1_c, L1_wmod):

    def _L0_attn_ref(x, wq, wk, wv, wo):
        import jax, jax.numpy as jnp
        import numpy as np
        D_MODEL = 256
        NUM_HEADS = 16
        D_K = D_MODEL // NUM_HEADS
        SEQ = 256
        BATCH = 2
        THETA = 10000.0

        def _rope_tables(seq_len, d_k, theta, dtype):
            pos = jnp.arange(seq_len, dtype=dtype)[:, None]
            inv = theta ** (-(jnp.arange(0, d_k, 2, dtype=dtype) / d_k))
            ang = pos * inv
            sin = jnp.repeat(jnp.sin(ang), 2, axis=1)
            cos = jnp.repeat(jnp.cos(ang), 2, axis=1)
            return (sin, cos)

        def _apply_rope(x, sin, cos):
            xp = x.reshape(x.shape[:-1] + (x.shape[-1] // 2, 2))
            swapped = jnp.stack((-xp[..., 1], xp[..., 0]), axis=-1).reshape(x.shape)
            return x * cos + swapped * sin
        B, S, D = x.shape
        H, dk = (NUM_HEADS, D_K)
        q = jnp.einsum('bsd,hkd->bhsk', x, wq.reshape(H, dk, D))
        k = jnp.einsum('bsd,hkd->bhsk', x, wk.reshape(H, dk, D))
        v = jnp.einsum('bsd,hkd->bhsk', x, wv.reshape(H, dk, D))
        sin, cos = _rope_tables(S, dk, THETA, x.dtype)
        q = _apply_rope(q, sin, cos)
        k = _apply_rope(k, sin, cos)
        scores = jnp.einsum('bhqk,bhsk->bhqs', q, k) / jnp.sqrt(jnp.asarray(dk, x.dtype))
        causal = jnp.triu(jnp.ones((S, S), dtype=bool), k=1)
        scores = jnp.where(causal, -jnp.inf, scores)
        attn = jax.nn.softmax(scores, axis=-1)
        out = jnp.einsum('bhqs,bhsv->bqhv', attn, v).reshape(B, S, H * dk)
        return jnp.einsum('bsf,df->bsd', out, wo)

    def _L0_ffn_ref(x, W, bias, rw1, rb1, rw2, rb2, A, B, gates):
        import jax, jax.numpy as jnp
        import numpy as np
        D_IN = 256
        D_OUT = 256
        RANK = 16
        N_EXPERTS = 16
        MAX_EXPERTS = 32
        ROUTER_HID = 64
        TOPK = 2
        ALPHA = 1.0

        def _forward(x, W, bias, rw1, rb1, rw2, rb2, A, B, gates):
            lead = x.shape[:-1]
            x_flat = x.reshape(-1, D_IN)
            n = x_flat.shape[0]
            feat = jax.lax.stop_gradient(x_flat)
            h = jax.nn.silu(feat @ rw1.T + rb1)
            logits = (h @ rw2.T + rb2)[:, :N_EXPERTS] + gates[None, :]
            topv, topi = jax.lax.top_k(logits, TOPK)
            sm = jax.nn.softmax(topv, axis=-1)
            rows = jnp.arange(n)[:, None]
            coeff = jnp.zeros_like(logits).at[rows, topi].set(sm)
            base = x_flat @ W.T + bias
            xa = jnp.einsum('ni,eri->ner', x_flat, A)
            wxa = xa * coeff[:, :, None]
            delta = jnp.einsum('ner,eor->no', wxa, B)
            out = base + ALPHA * delta
            return out.reshape(*lead, D_OUT)
        return _forward(x, W, bias, rw1, rb1, rw2, rb2, A, B, gates)

    def _L1_attn_ref(x, slope_rate, Wqkv, Wg, norm_w, Wo):
        import jax, jax.numpy as jnp
        import numpy as np
        BLOCK = 32
        b, n, hid = x.shape
        h = slope_rate.shape[0]
        d = Wqkv.shape[0] // (3 * h)
        nb = n // BLOCK
        qkv = jax.nn.silu(x @ Wqkv.T).reshape(b, n, h, 3 * d)
        q, k, v = jnp.split(qkv, 3, axis=-1)
        q = q.transpose(0, 2, 1, 3)
        k = k.transpose(0, 2, 1, 3)
        v = v.transpose(0, 2, 1, 3)
        s = slope_rate.astype(jnp.float32)
        arr = jnp.arange(1, BLOCK + 1, dtype=jnp.float32)
        q_decay = jnp.exp(-s * arr[:, None])
        k_decay = jnp.exp(-s * (BLOCK - arr[:, None]))
        idx = arr[:, None] - arr[None, :]
        diag_decay = jnp.where(idx >= 0, jnp.exp(-s * idx), 0.0)
        block_decay = jnp.exp(-s * BLOCK)

        def chunk(t):
            return t.reshape(b, h, nb, BLOCK, d).transpose(2, 0, 1, 3, 4)
        qc, kc, vc = (chunk(q), chunk(k), chunk(v))

        def step(kv, qkv_blk):
            qi, ki, vi = qkv_blk
            out_nd = jnp.einsum('bhmd,bhde->bhme', qi * q_decay, kv)
            qk = jnp.einsum('bhmd,bhnd->bhmn', qi, ki) * diag_decay
            out_d = jnp.einsum('bhmn,bhne->bhme', qk, vi)
            kv_new = block_decay * kv + jnp.einsum('bhmd,bhme->bhde', ki * k_decay, vi)
            return (kv_new, out_nd + out_d)
        kv0 = jnp.zeros((b, h, d, d), dtype=jnp.float32)
        _, out_blocks = jax.lax.scan(step, kv0, (qc, kc, vc))
        out = out_blocks.transpose(1, 2, 0, 3, 4).reshape(b, h, n, d)
        out = out.transpose(0, 2, 1, 3).reshape(b, n, h * d)
        eps = jnp.finfo(jnp.float32).eps
        rms = jax.lax.rsqrt(jnp.mean(out * out, axis=-1, keepdims=True) + eps)
        out = out * rms * norm_w
        gate = jax.nn.sigmoid(x @ Wg.T)
        return gate * out @ Wo.T

    def _L1_ffn_ref(x, W_up, W_gate, W_down):
        import jax, jax.numpy as jnp
        import numpy as np
        D_MODEL = 256
        D_EXPERT = 1024
        EPS = 1e-08

        def ternary_quant(w):
            scale = jnp.mean(jnp.abs(w)) + EPS
            q = jnp.clip(jnp.round(w / scale), -1.0, 1.0) * scale
            return w + jax.lax.stop_gradient(q - w)
        wu = ternary_quant(W_up)
        wg = ternary_quant(W_gate)
        wd = ternary_quant(W_down)
        up = jnp.einsum('bsd,ed->bse', x, wu)
        gate = jnp.einsum('bsd,ed->bse', x, wg)
        hidden = jax.nn.silu(up) * gate
        return jnp.einsum('bse,de->bsd', hidden, wd)
    x = L0_attn_x
    mod = (_silu(L0_c) @ L0_wmod).reshape(L0_c.shape[0], 6, 1, -1)
    sa, ca, ga, sb, cb, gb = (mod[:, 0], mod[:, 1], mod[:, 2], mod[:, 3], mod[:, 4], mod[:, 5])
    ga = (2 * (ga >= 0) - 1) * jnp.maximum(jnp.abs(ga), 0.25)
    gb = (2 * (gb >= 0) - 1) * jnp.maximum(jnp.abs(gb), 0.25)
    h = _layernorm(x, axis=-1) * (1 + ca) + sa
    x = x + ga * _L0_attn_ref(h, L0_attn_wq, L0_attn_wk, L0_attn_wv, L0_attn_wo)
    h = _layernorm(x, axis=-1) * (1 + cb) + sb
    x = x + gb * _L0_ffn_ref(h, L0_ffn_W, L0_ffn_bias, L0_ffn_rw1, L0_ffn_rb1, L0_ffn_rw2, L0_ffn_rb2, L0_ffn_A, L0_ffn_B, L0_ffn_gates)
    mod = (_silu(L1_c) @ L1_wmod).reshape(L1_c.shape[0], 6, 1, -1)
    sa, ca, ga, sb, cb, gb = (mod[:, 0], mod[:, 1], mod[:, 2], mod[:, 3], mod[:, 4], mod[:, 5])
    ga = (2 * (ga >= 0) - 1) * jnp.maximum(jnp.abs(ga), 0.25)
    gb = (2 * (gb >= 0) - 1) * jnp.maximum(jnp.abs(gb), 0.25)
    h = _layernorm(x, axis=-1) * (1 + ca) + sa
    x = x + ga * _L1_attn_ref(h, L1_attn_slope_rate, L1_attn_Wqkv, L1_attn_Wg, L1_attn_norm_w, L1_attn_Wo)
    h = _layernorm(x, axis=-1) * (1 + cb) + sb
    x = x + gb * _L1_ffn_ref(h, L1_ffn_W_up, L1_ffn_W_gate, L1_ffn_W_down)
    return x

_drawn_inputs = setup_inputs


def setup_inputs(seed=0):
    import zlib

    import numpy as np

    out = dict(_drawn_inputs(seed))
    spreads = {'L0_ffn_rb1': (0.0, 0.8),
     'L0_ffn_rb2': (0.0, 0.8),
     'L0_ffn_gates': (1.0, 0.6),
     'L1_attn_norm_w': (1.0, 0.6)}
    factors = {'L0_ffn_bias': 8.0,
     'L0_ffn_rw1': 8.0,
     'L0_ffn_rw2': 8.0,
     'L0_ffn_A': 8.0,
     'L0_ffn_B': 8.0,
     'L1_attn_Wg': 3.088}
    for name, (base, spread) in spreads.items():
        noise = np.random.default_rng([zlib.crc32(name.encode()), seed]).standard_normal(out[name].shape)
        drawn = base * np.exp(spread * noise) if base else spread * noise
        out[name] = jnp.asarray(drawn.astype(out[name].dtype))
    for name, factor in factors.items():
        out[name] = (out[name] * factor).astype(out[name].dtype)
    return out
```

```python
from contextlib import ExitStack

import concourse.bass as bass
from concourse import mybir

F32 = mybir.dt.float32
BF16 = mybir.dt.bfloat16
U32 = mybir.dt.uint32
ALU = mybir.AluOpType
ACT = mybir.ActivationFunctionType
AX = mybir.AxisListType

P = 128
S = 2048
D = 256
KD = D // P
TILES = S // P
GT = 4
GROUPS = TILES // GT
GN = GT * P
LN_EPS = 1e-5

H0, DK = 16, 16
HG = 4
HGROUPS = H0 // HG
VW = 32
Q_PART = (0, 0, 1, 1, 0, 2)
K_PART = (0, 1, 0, 1, 2, 0)
TERMS = len(Q_PART) * DK
RHID, EXPERTS = 64, 16

H1, D1 = 16, 128
PAIRS = H1 // 2
F1 = H1 * D1
DE = 1024
KE = DE // P
RMS_EPS = 1.1920928955078125e-07


class Stage:

    def __init__(self, nc, ctx, stage, *names):
        self.nc = nc
        self.made = {n: ctx.enter_context(nc.semaphore(f"{stage}_{n}")) for n in names}

    def __getitem__(self, name):
        return self.made[name]

    def clear(self):
        for s in self.made.values():
            self.nc.gpsimd.sem_clear(s)
        self.nc.all_engine_barrier()


class Chain:

    def __init__(self, eng, sem):
        self.eng, self.sem, self.n = eng, sem, 0

    def did(self, ins):
        ins.then_inc(self.sem, 1)
        self.n += 1

    def settle(self):
        self.eng.wait_ge(self.sem, self.n)

    def link(self, ins):
        self.did(ins)
        self.settle()


LN_SEMS = ("ln_stats", "ln_std", "ln_xn", "ln_tr", "ln_ha", "ln_hv", "vec")


class Norm:

    def __init__(self, nc, ctx, name, ident, eps, banks):
        sb = lambda n, s: ctx.enter_context(nc.sbuf_tensor(f"{name}_{n}", s, F32))
        self.stats = sb("stats", [P, GT, 6])
        self.mv = sb("mv", [P, GT, 2])
        self.std = sb("std", [P, GT])
        self.rstd = sb("rstd", [P, GT])
        self.xn = sb("xn", [P, GT, D])
        self.ident, self.eps, self.banks = ident, eps, banks

    def vector(self, nc, v, chain, sem, x4):
        for t in range(GT):
            chain.did(nc.vector.bn_stats(self.stats[:, t, :], x4[:, t, :]))
        chain.settle()
        for t in range(GT):
            last = nc.vector.bn_aggr(self.mv[:, t, :], self.stats[:, t, :])
        last.then_inc(sem["ln_stats"], 1)
        v.wait_ge(sem["ln_std"], 1)
        chain.link(nc.vector.reciprocal(self.rstd[:], self.std[:]))
        for t in range(GT):
            last = nc.vector.tensor_scalar(self.xn[:, t, :], x4[:, t, :], self.mv[:, t, 0:1],
                                           self.rstd[:, t:t + 1], ALU.subtract, ALU.mult)
        last.then_inc(sem["ln_xn"], 1)

    def scalar_std(self, nc, a, sem):
        a.wait_ge(sem["ln_stats"], 1)
        nc.scalar.activation(self.std[:], self.mv[:, :, 1], ACT.Sqrt, bias=self.eps[:]).then_inc(sem["ln_std"], 1)

    def tensor(self, nc, pe, sem):
        pe.wait_ge(sem["ln_xn"], 1)
        for k in range(KD):
            for t in range(GT):
                last = nc.tensor.transpose(self.banks[k][:, t * P:(t + 1) * P],
                                           self.xn[:, t, k * P:(k + 1) * P], self.ident[:])
        last.then_inc(sem["ln_tr"], 1)

    def modulate(self, nc, a, v, sem, hT, scale1, shift):
        if a is not None:
            a.wait_ge(sem["ln_tr"], 1)
            nc.scalar.activation(hT[:, 0, :], self.banks[0][:], ACT.Identity, bias=shift[:, 0:1],
                                 scale=scale1[:, 0:1]).then_inc(sem["ln_ha"], 1)
        if v is not None:
            v.wait_ge(sem["ln_tr"], 1)
            nc.vector.tensor_scalar(hT[:, 1, :], self.banks[1][:], scale1[:, 1:2], shift[:, 1:2],
                                    ALU.mult, ALU.add).then_inc(sem["ln_hv"], 1)


def modulation(nc, ctx, bank, mods, gates, ins):
    with ExitStack() as c:
        sb = lambda n, s: c.enter_context(nc.sbuf_tensor(f"mod_{n}", s, F32))
        cT = sb("cT", [P, 2, KD])
        scT = sb("scT", [P, 2, KD])
        scb = sb("scb", [P, 2, KD, P])
        ones = sb("ones", [P, P])
        wm = sb("wm", [P, 2, KD, 6 * D])
        mag = sb("mag", [P, 2, 2, D])
        sgn = sb("sgn", [P, 2, 2, D])
        sem = Stage(nc, c, "mod", "load", "silu", "rep", "cols", "rows", "vec")
        with nc.Block() as block:
            @block.sync
            def _(sp):
                for l in range(2):
                    sp.dma_start(cT[:, l, :], ins[f"c{l}"]).then_inc(sem["load"], 16)
                    sp.dma_start(wm[:, l], ins[f"wmod{l}"]).then_inc(sem["load"], 16)

            @block.scalar
            def _(a):
                a.wait_ge(sem["load"], 64)
                nc.scalar.activation(scT[:], cT[:], ACT.Silu).then_inc(sem["silu"], 1)

            @block.tensor
            def _(pe):
                pe.wait_ge(sem["silu"], 1)
                for l in range(2):
                    for j in range(12):
                        for k in range(KD):
                            last = nc.tensor.matmul(bank[0][:, l * 12 + j:l * 12 + j + 1],
                                                    wm[:, l, k, j * P:(j + 1) * P], scT[:, l, k:k + 1],
                                                    start=(k == 0), stop=(k == KD - 1))
                last.then_inc(sem["cols"], 1)
                pe.wait_ge(sem["rep"], 1)
                for l in range(2):
                    for n, at in enumerate((2 * D, 5 * D)):
                        for k in range(KD):
                            last = nc.tensor.matmul(bank[1 + l][:, n * D:(n + 1) * D], scb[:, l, k, :],
                                                    wm[:, l, k, at:at + D], start=(k == 0), stop=(k == KD - 1))
                last.then_inc(sem["rows"], 1)

            @block.vector
            def _(v):
                chain = Chain(v, sem["vec"])
                chain.link(nc.vector.memset(ones[:], 1.0))
                v.wait_ge(sem["silu"], 1)
                for l in range(2):
                    for k in range(KD):
                        last = nc.vector.tensor_scalar(scb[:, l, k, :], ones[:], scT[:, l, k:k + 1], None, ALU.mult)
                last.then_inc(sem["rep"], 1)
                v.wait_ge(sem["cols"], 1)
                for l in range(2):
                    for part in range(2):
                        at = l * 12 + part * 6
                        nc.vector.tensor_copy(mods[:, l, part, 0, :], bank[0][:, at:at + 2])
                        nc.vector.tensor_scalar(mods[:, l, part, 1, :], bank[0][:, at + 2:at + 4], 1.0, None, ALU.add)
                v.wait_ge(sem["rows"], 1)
                for l in range(2):
                    g = bank[1 + l][:].rearrange("p (n d) -> p n d", n=2)
                    chain.link(nc.vector.tensor_copy(mag[:, l], g))
                    chain.link(nc.vector.scalar_tensor_tensor(mag[:, l], mag[:, l], -1.0, mag[:, l], ALU.mult, ALU.max))
                    chain.did(nc.vector.tensor_scalar(mag[:, l], mag[:, l], 0.25, None, ALU.max))
                    chain.did(nc.vector.tensor_scalar(sgn[:, l], g, 0.0, 2.0, ALU.is_ge, ALU.mult))
                chain.settle()
                nc.vector.scalar_tensor_tensor(gates[:], sgn[:], -1.0, mag[:], ALU.add, ALU.mult)
        sem.clear()


def rope_front(nc, bank, x, v_all, ident, eps, mods, parts_dram, ins):
    with ExitStack() as c:
        sb = lambda n, s, dt=F32: c.enter_context(nc.sbuf_tensor(f"rf_{n}", s, dt))
        norm = Norm(nc, c, "rf", ident, eps, bank[0:2])
        hT = sb("hT", [P, KD, GN])
        wqk = sb("wqk", [P, KD, 2 * D])
        wv = sb("wv", [P, KD, D])
        cos = sb("cos", [P, TILES, DK])
        sin = sb("sin", [P, TILES, DK])
        straight = sb("straight", [P, 2, 2 * D])
        crossed = sb("crossed", [P, 2, 2 * D])
        turned = sb("turned", [P, GT, 2 * D])
        part = sb("part", [P, 4, 3, GN], BF16)
        rest = sb("rest", [P, 4, GN])
        sem = Stage(nc, c, "rf", *LN_SEMS, "load", "qk", "v", "turned", "vcopy", "tr", "high", "rest", "parts",
                    "pool", "store")
        heads = 2 * D // DK
        pairs = lambda ap: ap.rearrange("p (h i two) -> p h i two", i=DK // 2, two=2)

        def table(t, g, n):
            row = t[:, bass.ds(g * GT + n, 1), :].rearrange("p one (i two) -> p one i two", two=2)
            return row.to_broadcast([P, heads, DK // 2, 2])

        with nc.Block() as block:
            @block.sync
            def _(sp):
                sp.dma_start(wqk[:], ins["wqk"]).then_inc(sem["load"], 16)
                sp.dma_start(wv[:], ins["wv"]).then_inc(sem["load"], 16)
                sp.dma_start(cos[:], ins["cos"]).then_inc(sem["load"], 16)
                sp.dma_start(sin[:], ins["sin"]).then_inc(sem["load"], 16)
                sp.wait_ge(sem["load"], 64)
        sem.clear()
        with nc.Fori(0, GROUPS) as g:
            with nc.Block() as block:
                @block.vector
                def _(v):
                    chain = Chain(v, sem["vec"])
                    norm.vector(nc, v, chain, sem, x[:, bass.ds(g * GT, GT), :])
                    norm.modulate(nc, None, v, sem, hT, mods[:, 0, 0, 1, :], mods[:, 0, 0, 0, :])
                    for t in range(GT):
                        v.wait_ge(sem["qk"], t + 1)
                        chain.did(nc.vector.tensor_tensor(pairs(straight[:, t % 2, :]), pairs(bank[2][:]),
                                                          table(cos, g, t), ALU.mult))
                        chain.link(nc.vector.tensor_tensor(pairs(crossed[:, t % 2, :]),
                                                           pairs(bank[2][:])[:, :, :, ::-1],
                                                           table(sin, g, t), ALU.mult))
                        nc.vector.tensor_tensor(turned[:, t, :], straight[:, t % 2, :], crossed[:, t % 2, :],
                                                ALU.add).then_inc(sem["turned"], 1)
                    for j in range(4):
                        v.wait_ge(sem["high"], j + 1)
                        nc.vector.tensor_tensor(rest[:, j, :], bank[4 + j][:], part[:, j, 0, :],
                                                ALU.subtract).then_inc(sem["rest"], 1)

                @block.scalar
                def _(a):
                    norm.scalar_std(nc, a, sem)
                    norm.modulate(nc, a, None, sem, hT, mods[:, 0, 0, 1, :], mods[:, 0, 0, 0, :])
                    for t in range(GT):
                        a.wait_ge(sem["v"], t + 1)
                        nc.scalar.copy(v_all[:, bass.ds(g * GT + t, 1), :],
                                       bank[3][:, 0:D].unsqueeze(1)).then_inc(sem["vcopy"], 1)
                    for j in range(4):
                        a.wait_ge(sem["tr"], j + 1)
                        nc.scalar.copy(part[:, j, 0, :], bank[4 + j][:]).then_inc(sem["high"], 1)

                @block.tensor
                def _(pe):
                    norm.tensor(nc, pe, sem)
                    pe.wait_ge(sem["ln_ha"], 1)
                    pe.wait_ge(sem["ln_hv"], 1)
                    for t in range(GT):
                        if t:
                            pe.wait_ge(sem["turned"], t)
                        for k in range(KD):
                            last = nc.tensor.matmul(bank[2][:], hT[:, k, t * P:(t + 1) * P], wqk[:, k, :],
                                                    start=(k == 0), stop=(k == KD - 1))
                        last.then_inc(sem["qk"], 1)
                        if t:
                            pe.wait_ge(sem["vcopy"], t)
                        for k in range(KD):
                            last = nc.tensor.matmul(bank[3][:, 0:D], hT[:, k, t * P:(t + 1) * P], wv[:, k, :],
                                                    start=(k == 0), stop=(k == KD - 1))
                        last.then_inc(sem["v"], 1)
                    pe.wait_ge(sem["turned"], GT)
                    for j in range(4):
                        for t in range(GT):
                            last = nc.tensor.transpose(bank[4 + j][:, t * P:(t + 1) * P],
                                                       turned[:, t, j * P:(j + 1) * P], ident[:])
                        last.then_inc(sem["tr"], 1)

                @block.gpsimd
                def _(gp):
                    chain = Chain(gp, sem["pool"])
                    for j in range(4):
                        gp.wait_ge(sem["rest"], j + 1)
                        chain.link(nc.gpsimd.tensor_copy(part[:, j, 1, :], rest[:, j, :]))
                        nc.gpsimd.tensor_tensor(part[:, j, 2, :], rest[:, j, :], part[:, j, 1, :],
                                                ALU.subtract).then_inc(sem["parts"], 1)

                @block.sync
                def _(sp):
                    for j in range(4):
                        sp.wait_ge(sem["parts"], j + 1)
                        half = (j % 2) * P
                        dst = parts_dram[j // 2, :, half:half + P, bass.ds(g * GN, GN)].rearrange("c p s -> p c s")
                        sp.dma_start(dst, part[:, j]).then_inc(sem["store"], 16)
                    sp.wait_ge(sem["store"], 64)
            sem.clear()


def rope_attention(nc, bank, v_all, attn, ident, parts_dram, ins):
    with ExitStack() as c:
        sb = lambda n, s, dt=F32: c.enter_context(nc.sbuf_tensor(f"ra_{n}", s, dt))
        kst = sb("kst", [P, HG, S], BF16)
        qst = sb("qst", [P, HG, S], BF16)
        vg = sb("vg", [P, TILES, HG, VW])
        prob = sb("prob", [P, 2, HG, GN])
        sums = sb("sums", [P, GN])
        pm = sb("pm", [P, GT * HG, GROUPS])
        negm = sb("negm", [P, 2, GT * HG])
        nrest = sb("nrest", [P, 2, GT * HG])
        mp = sb("mp", [P, GT * HG, VW], BF16)
        rec = sb("rec", [P, GT, HG])
        mask_f = sb("mask_f", [P, 2, P])
        mask = sb("mask", [P, 2, P], BF16)
        identb = sb("identb", [P, P], BF16)
        sem = Stage(nc, c, "ra", "load", "ready", "vg", "pm", "red", "neg", "mp", "trm", "shift", "sc", "exp",
                    "av", "avs", "trn", "norm", "vec", "pool")
        PM, ST, AV, TR = bank[0:2], (2, 4), bank[6], bank[7]
        TRb = TR[:].bitcast(BF16)

        def pieces(cq):
            return [(t * HG + h, h, t, p, GN if p < cq else P * (t + 1))
                    for t in range(GT) for h in range(HG) for p in range(cq + 1)]

        first_piece = [sum(len(pieces(j)) for j in range(cq)) for cq in range(GROUPS + 1)]
        first_block = [sum(GT * j + GT for j in range(cq)) for cq in range(GROUPS + 1)]

        with nc.Block() as block:
            @block.sync
            def _(sp):
                sp.dma_start(mask_f[:], ins["mask"]).then_inc(sem["load"], 16)

            @block.vector
            def _(v):
                nc.vector.memset(kst[TERMS:P, :, :], 1.0)
                nc.vector.memset(mp[:], 0.0)
                nc.vector.tensor_copy(identb[:], ident[:])
                chain = Chain(v, sem["vec"])
                chain.link(nc.vector.memset(vg[:], 0.0))
                nc.vector.memset(vg[:, :, :, DK:DK + 1], 1.0)
                v.wait_ge(sem["load"], 16)
                nc.vector.tensor_copy(mask[:], mask_f[:])
        sem.clear()

        with nc.Fori(0, HGROUPS) as g:
            with nc.Block() as block:
                @block.sync
                def _(sp):
                    for side, dst, order in ((0, qst, Q_PART), (1, kst, K_PART)):
                        for j, which in enumerate(order):
                            src = parts_dram[side, which, bass.ds(g * (HG * DK), HG * DK), :]
                            sp.dma_start(dst[j * DK:(j + 1) * DK, :, :],
                                         src.rearrange("(h r) s -> r h s", r=DK)).then_inc(sem["load"], 16)

                @block.gpsimd
                def _(gp):
                    chain = Chain(gp, sem["pool"])
                    src = v_all[:, :, bass.ds(g * (HG * DK), HG * DK)].rearrange("p t (h d) -> p t h d", h=HG)
                    nc.gpsimd.tensor_copy(vg[:, :, :, 0:DK], src).then_inc(sem["vg"], 1)
                    for cq in range(GROUPS):
                        gp.wait_ge(sem["neg"], cq + 1)
                        if cq:
                            gp.wait_ge(sem["trm"], cq)
                        m = negm[:, cq % 2, :]
                        r = nrest[:, cq % 2, :]
                        chain.link(nc.gpsimd.tensor_copy(mp[:, :, 0], m))
                        chain.link(nc.gpsimd.tensor_tensor(r, m, mp[:, :, 0], ALU.subtract))
                        chain.link(nc.gpsimd.tensor_copy(mp[:, :, 1], r))
                        nc.gpsimd.tensor_tensor(mp[:, :, 2], r, mp[:, :, 1], ALU.subtract).then_inc(sem["mp"], 1)

                @block.vector
                def _(v):
                    chain = Chain(v, sem["vec"])

                    def normalize(cq):
                        v.wait_ge(sem["trn"], cq + 1)
                        tr = TR[:].rearrange("p (t h w) -> p t h w", t=GT, h=HG)
                        chain.link(nc.vector.reciprocal(rec[:], tr[:, :, :, DK]))
                        dst = attn[:, cq * GT:(cq + 1) * GT, bass.ds(g * (HG * DK), HG * DK)]
                        nc.vector.tensor_tensor(dst.rearrange("p t (h d) -> p t h d", h=HG), tr[:, :, :, 0:DK],
                                                rec[:].unsqueeze(3).to_broadcast([P, GT, HG, DK]),
                                                ALU.mult).then_inc(sem["norm"], 1)

                    for cq in range(GROUPS):
                        todo = pieces(cq)
                        for i, (row, h, t, p, w) in enumerate(todo):
                            n = first_piece[cq] + i
                            v.wait_ge(sem["pm"], n + 1)
                            nc.vector.tensor_reduce(pm[:, row, p:p + 1], PM[n % 2][:, 0:w], AX.X,
                                                    ALU.max).then_inc(sem["red"], 1)
                            if cq >= 2 and i == len(todo) // 2:
                                normalize(cq - 2)
                        v.wait_ge(sem["red"], first_piece[cq + 1])
                        if cq >= 2:
                            v.wait_ge(sem["mp"], cq - 1)
                        nc.vector.tensor_reduce(negm[:, cq % 2, :], pm[:, :, 0:cq + 1], AX.X, ALU.max,
                                                negate=True).then_inc(sem["neg"], 1)
                    for cq in range(GROUPS - 2, GROUPS):
                        normalize(cq)

                @block.scalar
                def _(a):
                    e = 0
                    for cq in range(GROUPS):
                        a.wait_ge(sem["trm"], cq + 1)
                        for h in range(HG):
                            last = nc.scalar.copy(qst[TERMS:P, h, cq * GN:(cq + 1) * GN],
                                                  TRb[h * VW:(h + 1) * VW, 0:GN])
                        last.then_inc(sem["shift"], 1)
                        for kb in range(GT * (cq + 1)):
                            off = max(0, kb - GT * cq) * P
                            b = first_block[cq] + kb
                            for hp in range(2):
                                if b >= 2:
                                    a.wait_ge(sem["av"], b - 1)
                                a.wait_ge(sem["sc"], e + 1)
                                lo = ST[e % 2]
                                nc.scalar.activation(prob[:, b % 2, 2 * hp:2 * hp + 2, off:GN],
                                                     bank.whole[:, lo:lo + 2, off:GN], ACT.Exp,
                                                     scale=float(DK) ** -0.5).then_inc(sem["exp"], 1)
                                e += 1
                        a.wait_ge(sem["av"], first_block[cq + 1])
                        if cq:
                            a.wait_ge(sem["trn"], cq)
                        nc.scalar.copy(sums[:], AV[:]).then_inc(sem["avs"], 1)

                @block.tensor
                def _(pe):
                    pe.wait_ge(sem["load"], 16 * 2 * len(Q_PART))
                    state = {"n": 0, "e": 0}

                    def maxima(cq, todo):
                        for row, h, t, p, w in todo:
                            n = state["n"]
                            if n >= 2:
                                pe.wait_ge(sem["red"], n - 1)
                            q = qst[0:TERMS, h, cq * GN + t * P:cq * GN + (t + 1) * P]
                            last = nc.tensor.matmul(PM[n % 2][:, 0:w], q, kst[0:TERMS, h, p * GN:p * GN + w],
                                                    start=True, stop=(p < cq))
                            if p == cq:
                                last = nc.tensor.matmul(PM[n % 2][:, w - P:w], identb[:], mask[:, 0, :],
                                                        start=False, stop=True)
                            last.then_inc(sem["pm"], 1)
                            state["n"] += 1

                    def shift(cq):
                        pe.wait_ge(sem["mp"], cq + 1)
                        if cq >= 2:
                            pe.wait_ge(sem["norm"], cq - 1)
                        for t in range(GT):
                            last = nc.tensor.transpose(TRb[:, t * P:(t + 1) * P],
                                                       mp[:, t * HG:(t + 1) * HG, :].rearrange("p h w -> p (h w)"),
                                                       identb[:])
                        last.then_inc(sem["trm"], 1)

                    def turn_sums(cq):
                        pe.wait_ge(sem["avs"], cq + 1)
                        if cq + 1 < GROUPS:
                            pe.wait_ge(sem["shift"], cq + 2)
                        else:
                            pe.wait_ge(sem["norm"], cq)
                        for t in range(GT):
                            last = nc.tensor.transpose(TR[:, t * P:(t + 1) * P], sums[:, t * P:(t + 1) * P], ident[:])
                        last.then_inc(sem["trn"], 1)

                    def scores(cq, kb):
                        off = max(0, kb - GT * cq) * P
                        diagonal = kb >= GT * cq
                        for hp in range(2):
                            e = state["e"]
                            if e >= 2:
                                pe.wait_ge(sem["exp"], e - 1)
                            for h in (2 * hp, 2 * hp + 1):
                                out = bank[ST[e % 2] + h % 2]
                                last = nc.tensor.matmul(out[:, off:GN], kst[:, h, kb * P:(kb + 1) * P],
                                                        qst[:, h, cq * GN + off:(cq + 1) * GN],
                                                        start=True, stop=not diagonal)
                                if diagonal:
                                    last = nc.tensor.matmul(out[:, off:off + P], identb[:], mask[:, 1, :],
                                                            start=False, stop=True)
                            last.then_inc(sem["sc"], 1)
                            state["e"] += 1

                    def values(cq, kb):
                        off = max(0, kb - GT * cq) * P
                        b = first_block[cq] + kb
                        pe.wait_ge(sem["exp"], 2 * b + 2)
                        if kb == 0 and cq:
                            pe.wait_ge(sem["avs"], cq)
                        for h in range(HG):
                            last = nc.tensor.matmul(AV[h * VW:(h + 1) * VW, off:GN], vg[:, kb, h, :],
                                                    prob[:, b % 2, h, off:GN], start=(kb == 0),
                                                    stop=(kb == GT * (cq + 1) - 1), skip_group_check=True)
                        last.then_inc(sem["av"], 1)

                    maxima(0, pieces(0))
                    pe.wait_ge(sem["vg"], 1)
                    for cq in range(GROUPS):
                        shift(cq)
                        ahead = pieces(cq + 1) if cq + 1 < GROUPS else []
                        blocks, done = GT * (cq + 1), 0
                        pe.wait_ge(sem["shift"], cq + 1)
                        for kb in range(blocks + 1):
                            if kb < blocks:
                                scores(cq, kb)
                            if kb:
                                values(cq, kb - 1)
                            if kb == 1 and cq:
                                turn_sums(cq - 1)
                            upto = len(ahead) * min(kb + 1, blocks) // blocks
                            maxima(cq + 1, ahead[done:upto])
                            done = upto
                    turn_sums(GROUPS - 1)

            sem.clear()


def routed_ffn(nc, bank, x, attn, ident, eps, mods, gates, ins):
    with ExitStack() as c:
        sb = lambda n, s, dt=F32: c.enter_context(nc.sbuf_tensor(f"ff_{n}", s, dt))
        norm = Norm(nc, c, "ff", ident, eps, bank[0:2])
        hT = sb("hT", [P, KD, GN])
        stage = sb("stage", [P, GT, D])
        aT = sb("aT", [P, KD, GN])
        wo = sb("wo", [P, KD, D])
        wbase = sb("wbase", [P, KD, 2 * D])
        wexp = sb("wexp", [P, KD, D])
        rw1 = sb("rw1", [P, KD, RHID])
        rw2 = sb("rw2", [RHID, EXPERTS])
        rb1 = sb("rb1", [RHID, 1])
        rows = sb("rows", [1, 2, EXPERTS])
        brow = sb("brow", [1, EXPERTS])
        bias = sb("bias", [1, D])
        ones = sb("ones", [1, P])
        iota = sb("iota", [P, EXPERTS])
        sig = sb("sig", [RHID, GN])
        r1 = sb("r1", [RHID, GN])
        logit = sb("logit", [P, GT, EXPERTS])
        top = sb("top", [P, GT, 8])
        topi = sb("topi", [P, GT, 8], U32)
        topf = sb("topf", [P, GT, 2])
        gap = sb("gap", [P, 2, GT])
        sm = sb("sm", [P, 2, GT])
        coef = sb("coef", [P, 2, GT, EXPERTS])
        wxa = sb("wxa", [P, GT, D])
        wxaT = sb("wxaT", [P, KD, GN])
        upd = sb("upd", [P, GT, D])
        sem = Stage(nc, c, "ff", *LN_SEMS, "load", "stage", "atr", "aT", "y", "x1", "h1", "sig", "r1", "logit",
                    "gap", "sm", "base", "wxa", "wtr", "wxaT", "out")
        loads = (("wo", wo), ("wbase", wbase), ("wexp", wexp), ("rw1", rw1), ("rw2", rw2), ("rb1", rb1),
                 ("rows", rows), ("bias", bias), ("iota", iota))

        with nc.Block() as block:
            @block.sync
            def _(sp):
                for name, dst in loads:
                    sp.dma_start(dst[:], ins[name]).then_inc(sem["load"], 16)

            @block.vector
            def _(v):
                nc.vector.memset(ones[:], 1.0)
                v.wait_ge(sem["load"], 16 * len(loads))
                nc.vector.tensor_tensor(brow[:], rows[:, 0, :], rows[:, 1, :], ALU.add)
        sem.clear()

        with nc.Fori(0, GROUPS) as g:
            with nc.Block() as block:
                @block.scalar
                def _(a):
                    nc.scalar.copy(stage[:], attn[:, bass.ds(g * GT, GT), :]).then_inc(sem["stage"], 1)
                    a.wait_ge(sem["atr"], 1)
                    for k in range(KD):
                        last = nc.scalar.copy(aT[:, k, :], bank[k][:])
                    last.then_inc(sem["aT"], 1)
                    norm.scalar_std(nc, a, sem)
                    norm.modulate(nc, a, None, sem, hT, mods[:, 0, 1, 1, :], mods[:, 0, 1, 0, :])
                    a.wait_ge(sem["h1"], 1)
                    nc.scalar.activation(sig[:], bank[2][0:RHID, :], ACT.Sigmoid, bias=rb1[:]).then_inc(sem["sig"], 1)
                    a.wait_ge(sem["gap"], 1)
                    nc.scalar.activation(sm[:], gap[:], ACT.Sigmoid).then_inc(sem["sm"], 1)
                    a.wait_ge(sem["wtr"], 1)
                    for k in range(KD):
                        last = nc.scalar.copy(wxaT[:, k, :], bank[k][:])
                    last.then_inc(sem["wxaT"], 1)

                @block.tensor
                def _(pe):
                    pe.wait_ge(sem["stage"], 1)
                    for k in range(KD):
                        for t in range(GT):
                            last = nc.tensor.transpose(bank[k][:, t * P:(t + 1) * P],
                                                       stage[:, t, k * P:(k + 1) * P], ident[:])
                    last.then_inc(sem["atr"], 1)
                    pe.wait_ge(sem["aT"], 1)
                    for t in range(GT):
                        for k in range(KD):
                            last = nc.tensor.matmul(bank[4 + t][:, 0:D], aT[:, k, t * P:(t + 1) * P], wo[:, k, :],
                                                    start=(k == 0), stop=(k == KD - 1))
                        last.then_inc(sem["y"], 1)
                    norm.tensor(nc, pe, sem)
                    pe.wait_ge(sem["ln_ha"], 1)
                    pe.wait_ge(sem["ln_hv"], 1)
                    for k in range(KD):
                        last = nc.tensor.matmul(bank[2][0:RHID, :], rw1[:, k, :], hT[:, k, :],
                                                start=(k == 0), stop=(k == KD - 1))
                    last.then_inc(sem["h1"], 1)
                    pe.wait_ge(sem["x1"], GT)
                    for t in range(GT):
                        for k in range(KD):
                            last = nc.tensor.matmul(bank[4 + t][:], hT[:, k, t * P:(t + 1) * P], wbase[:, k, :],
                                                    start=(k == 0), stop=False, skip_group_check=True)
                        last = nc.tensor.matmul(bank[4 + t][:, 0:D], ones[:], bias[:], start=False, stop=False,
                                                skip_group_check=True)
                        last.then_inc(sem["base"], 1)
                    pe.wait_ge(sem["r1"], 1)
                    for t in range(GT):
                        out = bank[3][:, t * EXPERTS:(t + 1) * EXPERTS]
                        nc.tensor.matmul(out, r1[:, t * P:(t + 1) * P], rw2[:], start=True, stop=False)
                        last = nc.tensor.matmul(out, ones[:], brow[:], start=False, stop=True)
                    last.then_inc(sem["logit"], 1)
                    pe.wait_ge(sem["wxa"], GT)
                    for k in range(KD):
                        for t in range(GT):
                            last = nc.tensor.transpose(bank[k][:, t * P:(t + 1) * P],
                                                       wxa[:, t, k * P:(k + 1) * P], ident[:])
                    last.then_inc(sem["wtr"], 1)
                    pe.wait_ge(sem["wxaT"], 1)
                    for t in range(GT):
                        for k in range(KD):
                            last = nc.tensor.matmul(bank[4 + t][:, 0:D], wxaT[:, k, t * P:(t + 1) * P], wexp[:, k, :],
                                                    start=False, stop=(k == KD - 1), skip_group_check=True)
                        last.then_inc(sem["out"], 1)

                @block.vector
                def _(v):
                    chain = Chain(v, sem["vec"])
                    x4 = x[:, bass.ds(g * GT, GT), :]
                    for t in range(GT):
                        v.wait_ge(sem["y"], t + 1)
                        nc.vector.tensor_tensor(upd[:, t, :], bank[4 + t][:, 0:D], gates[:, 0, 0, :],
                                                ALU.mult).then_inc(sem["x1"], 1)
                    v.wait_ge(sem["x1"], GT)
                    chain.link(nc.vector.tensor_tensor(x4, x4, upd[:], ALU.add))
                    norm.vector(nc, v, chain, sem, x4)
                    norm.modulate(nc, None, v, sem, hT, mods[:, 0, 1, 1, :], mods[:, 0, 1, 0, :])
                    v.wait_ge(sem["sig"], 1)
                    nc.vector.scalar_tensor_tensor(r1[:], bank[2][0:RHID, :], rb1[:, 0:1], sig[:], ALU.add,
                                                   ALU.mult).then_inc(sem["r1"], 1)
                    v.wait_ge(sem["logit"], 1)
                    lg = bank[3][:, 0:GT * EXPERTS].rearrange("p (t e) -> p t e", t=GT)
                    chain.link(nc.vector.tensor_copy(logit[:], lg))
                    for t in range(GT):
                        chain.did(nc.vector.max(top[:, t, :], logit[:, t, :]))
                    chain.settle()
                    for t in range(GT):
                        chain.did(nc.vector.max_index(topi[:, t, :], top[:, t, :], logit[:, t, :]))
                    nc.vector.tensor_tensor(gap[:, 0, :], top[:, :, 0], top[:, :, 1], ALU.subtract)
                    nc.vector.tensor_tensor(gap[:, 1, :], top[:, :, 1], top[:, :, 0],
                                            ALU.subtract).then_inc(sem["gap"], 1)
                    chain.settle()
                    chain.link(nc.vector.tensor_copy(topf[:], topi[:, :, 0:2]))
                    v.wait_ge(sem["sm"], 1)
                    for t in range(GT):
                        for n in range(2):
                            chain.did(nc.vector.tensor_scalar(coef[:, n, t, :], iota[:], topf[:, t, n:n + 1],
                                                              sm[:, n, t:t + 1], ALU.is_equal, ALU.mult))
                    chain.settle()
                    chain.link(nc.vector.tensor_tensor(coef[:, 0], coef[:, 0], coef[:, 1], ALU.add))
                    for t in range(GT):
                        v.wait_ge(sem["base"], t + 1)
                        xa = bank[4 + t][:, D:2 * D].rearrange("p (e r) -> p e r", e=EXPERTS)
                        nc.vector.tensor_tensor(wxa[:, t, :].rearrange("p (e r) -> p e r", e=EXPERTS), xa,
                                                coef[:, 0, t, :].unsqueeze(2).to_broadcast([P, EXPERTS, D // EXPERTS]),
                                                ALU.mult).then_inc(sem["wxa"], 1)
                    for t in range(GT):
                        v.wait_ge(sem["out"], t + 1)
                        chain.did(nc.vector.tensor_tensor(upd[:, t, :], bank[4 + t][:, 0:D], gates[:, 0, 1, :],
                                                          ALU.mult))
                    chain.settle()
                    nc.vector.tensor_tensor(x4, x4, upd[:], ALU.add)
            sem.clear()


def decay_front(nc, bank, x, hT, ident, eps, mods):
    with ExitStack() as c:
        norm = Norm(nc, c, "df", ident, eps, bank[0:2])
        sem = Stage(nc, c, "df", *LN_SEMS)
        with nc.Fori(0, GROUPS) as g:
            h = hT[:, :, bass.ds(g * GN, GN)]
            with nc.Block() as block:
                @block.vector
                def _(v):
                    norm.vector(nc, v, Chain(v, sem["vec"]), sem, x[:, bass.ds(g * GT, GT), :])
                    norm.modulate(nc, None, v, sem, h, mods[:, 1, 0, 1, :], mods[:, 1, 0, 0, :])

                @block.scalar
                def _(a):
                    norm.scalar_std(nc, a, sem)
                    norm.modulate(nc, a, None, sem, h, mods[:, 1, 0, 1, :], mods[:, 1, 0, 0, :])

                @block.tensor
                def _(pe):
                    norm.tensor(nc, pe, sem)
            sem.clear()


def decay_attention(nc, bank, x, hT, ident, mods, gates, ins):
    with ExitStack() as c:
        sb = lambda n, s, dt=F32: c.enter_context(nc.sbuf_tensor(f"da_{n}", s, dt))
        w = sb("w", [P, KD, 8 * D1])
        wo = sb("wo", [P, 2, D])
        nw = sb("nw", [P, H1])
        slope = sb("slope", [P, H1])
        steps = sb("steps", [P, 4, P])
        dmask = sb("dmask", [P, 2, P])
        qdec = sb("qdec", [P, 2, P])
        kbdec = sb("kbdec", [P, 2, 2])
        small = sb("small", [P, 2, 2])
        qT = sb("qT", [P, 2, S])
        kT = sb("kT", [P, S])
        gT = sb("gT", [P, S])
        v = sb("v", [P, TILES, 2 * D1])
        ktok = sb("ktok", [P, TILES, D1])
        qd = sb("qd", [P, S])
        state = sb("state", [P, TILES, D1])
        smask = sb("smask", [P, 2, GT, P])
        oT = sb("oT", [P, 2, GN])
        sq = sb("sq", [P, GN])
        og = sb("og", [P, 2, S])
        ssum = sb("ssum", [P, S])
        yacc = sb("yacc", [P, TILES, D])
        ones = sb("ones", [P, 1])
        rms = sb("rms", [P, 2, TILES])
        reps = sb("reps", [P, 1])
        sem = Stage(nc, c, "da", "load", "small", "sneg", "dec", "dmask", "vec", "pool", "act", "proj", "evac", "ktr", "ktok",
                    "qd", "dl", "st", "sc", "sm", "o", "oT", "sq", "og", "y", "yadd", "ss", "rstd")
        PROJ, KTR, SC, DL, OB, YB = bank[0:2], bank[2], bank[3], bank[4], bank[5], bank[6:8]

        with nc.Block() as block:
            @block.sync
            def _(sp):
                sp.dma_start(nw[:], ins["nw"]).then_inc(sem["load"], 16)
                sp.dma_start(slope[:], ins["slope"]).then_inc(sem["load"], 16)
                sp.dma_start(steps[:], ins["steps"]).then_inc(sem["load"], 16)
                sp.wait_ge(sem["load"], 48)

            @block.vector
            def _(ve):
                nc.vector.memset(yacc[:], 0.0)
                nc.vector.memset(state[:, 0, :], 0.0)
                nc.vector.memset(ones[:], 1.0)
                nc.vector.memset(reps[:], RMS_EPS)

            @block.gpsimd
            def _(gp):
                nc.gpsimd.memset(ssum[:], 0.0)
        sem.clear()

        def wide(kind, h):
            return [(kind, h, j) for j in range(GROUPS)]

        first = wide("q", 0) + wide("k", 0) + [("v", 0, t) for t in range(0, TILES, 2)] + wide("g", 0)
        second = wide("q", 1)
        third = wide("k", 1)
        fourth = wide("g", 1)
        order = first + second + third + fourth
        nth = {item: i for i, item in enumerate(order)}
        column = {"q": 0, "k": 2, "g": 4}

        with nc.Fori(0, PAIRS) as pr:
            with nc.Block() as block:
                @block.sync
                def _(sp):
                    sp.dma_start(w[:], ins["wpair"][bass.ds(pr, 1)].rearrange("o p k n -> (o p) k n")).then_inc(sem["load"], 16)
                    sp.dma_start(wo[:], ins["wo1"][bass.ds(pr, 1)].rearrange("o p k n -> (o p) k n")).then_inc(sem["load"], 16)

                @block.scalar
                def _(a):
                    a.wait_ge(sem["sneg"], 1)
                    for h in range(2):
                        s = small[:, h, 0:1]
                        nc.scalar.activation(dmask[:, h, :], steps[:, 0, :], ACT.Exp, scale=s)
                        nc.scalar.activation(qdec[:, h, :], steps[:, 2, :], ACT.Exp, scale=s)
                        last = nc.scalar.activation(kbdec[:, h, :], steps[:, 3, 0:2], ACT.Exp, scale=s)
                    last.then_inc(sem["dec"], 1)

                    def drain(items):
                        for item in items:
                            kind, h, j = item
                            i = nth[item]
                            if item == ("k", 1, 0):
                                a.wait_ge(sem["ktr"], GROUPS)
                                a.wait_ge(sem["sc"], GROUPS)
                            if item == ("g", 1, 0):
                                a.wait_ge(sem["og"], GROUPS)
                            a.wait_ge(sem["proj"], i + 1)
                            src = PROJ[i % 2][:]
                            if kind == "v":
                                dst, f = v[:, j:j + 2, :].rearrange("p t n -> p (t n)"), ACT.Silu
                            else:
                                at = slice(j * GN, (j + 1) * GN)
                                dst = {"q": qT[:, h, at], "k": kT[:, at], "g": gT[:, at]}[kind]
                                f = ACT.Tanh if kind == "g" else ACT.Silu
                            nc.scalar.activation(dst, src, f, scale=0.5 if kind == "g" else 1.0).then_inc(sem["evac"], 1)

                    def outs(h):
                        for j in range(GROUPS):
                            n = h * GROUPS + j
                            a.wait_ge(sem["o"], n + 1)
                            if n >= 2:
                                a.wait_ge(sem["sq"], n - 1)
                                a.wait_ge(sem["og"], n - 1)
                            nc.scalar.copy(oT[:, n % 2, :], OB[:]).then_inc(sem["oT"], 1)

                    drain(first)
                    drain(second)
                    outs(0)
                    drain(third)
                    drain(fourth)
                    outs(1)

                @block.tensor
                def _(pe):
                    pe.wait_ge(sem["load"], 32)

                    def project(items):
                        for item in items:
                            kind, h, j = item
                            i = nth[item]
                            if i >= 2:
                                pe.wait_ge(sem["evac"], i - 1)
                            out = PROJ[i % 2]
                            if kind == "v":
                                for t in range(2):
                                    for k in range(KD):
                                        last = nc.tensor.matmul(out[:, t * 2 * D1:(t + 1) * 2 * D1],
                                                                hT[:, k, (j + t) * P:(j + t + 1) * P],
                                                                w[:, k, 6 * D1:8 * D1],
                                                                start=(k == 0), stop=(k == KD - 1))
                            else:
                                at = (column[kind] + h) * D1
                                for k in range(KD):
                                    last = nc.tensor.matmul(out[:], w[:, k, at:at + D1],
                                                            hT[:, k, j * GN:(j + 1) * GN],
                                                            start=(k == 0), stop=(k == KD - 1))
                            last.then_inc(sem["proj"], 1)

                    def turn_keys(h):
                        for j in range(GROUPS):
                            n = h * GROUPS + j
                            pe.wait_ge(sem["evac"], nth[("k", h, j)] + 1)
                            if n:
                                pe.wait_ge(sem["ktok"], n)
                            for t in range(GT):
                                b = j * GT + t
                                last = nc.tensor.transpose(KTR[:, t * P:(t + 1) * P], kT[:, b * P:(b + 1) * P], ident[:])
                            last.then_inc(sem["ktr"], 1)

                    def block_scores(h, j):
                        n = h * GROUPS + j
                        if n:
                            pe.wait_ge(sem["sm"], n)
                        for t in range(GT):
                            b = j * GT + t
                            last = nc.tensor.matmul(SC[:, t * P:(t + 1) * P], kT[:, b * P:(b + 1) * P],
                                                    qT[:, h, b * P:(b + 1) * P], start=True, stop=True)
                        last.then_inc(sem["sc"], 1)

                    def deltas(h, j):
                        n = h * GROUPS + j
                        pe.wait_ge(sem["ktok"], n + 1)
                        pe.wait_ge(sem["evac"], nth[("v", 0, TILES - 2)] + 1)
                        if n:
                            pe.wait_ge(sem["st"], h * (TILES - 1) + j * GT)
                        for b in range(j * GT, min(j * GT + GT, TILES - 1)):
                            t = b % GT
                            last = nc.tensor.matmul(DL[:, t * P:(t + 1) * P], ktok[:, b, :],
                                                    v[:, b, h * D1:(h + 1) * D1], start=True, stop=True)
                        last.then_inc(sem["dl"], 1)

                    def attend(h, j):
                        n = h * GROUPS + j
                        pe.wait_ge(sem["sm"], n + 1)
                        pe.wait_ge(sem["st"], h * (TILES - 1) + j * GT + GT - 1)
                        pe.wait_ge(sem["qd"], h + 1)
                        if n:
                            pe.wait_ge(sem["oT"], n)
                        for t in range(GT):
                            b = j * GT + t
                            out = OB[:, t * P:(t + 1) * P]
                            last = nc.tensor.matmul(out, v[:, b, h * D1:(h + 1) * D1], smask[:, n % 2, t, :],
                                                    start=True, stop=(b == 0))
                            if b:
                                last = nc.tensor.matmul(out, state[:, b, :], qd[:, b * P:(b + 1) * P],
                                                        start=False, stop=True)
                        last.then_inc(sem["o"], 1)

                    def head(h):
                        pe.wait_ge(sem["evac"], nth[("q", h, GROUPS - 1)] + 1)
                        for j in range(GROUPS + 1):
                            if j < GROUPS:
                                deltas(h, j)
                                block_scores(h, j)
                            if j:
                                attend(h, j - 1)

                    project(first)
                    turn_keys(0)
                    project(second)
                    head(0)
                    project(third)
                    turn_keys(1)
                    project(fourth)
                    head(1)
                    pe.wait_ge(sem["og"], 2 * GROUPS)
                    for t in range(TILES):
                        i = t // 2
                        if t % 2 == 0 and i >= 2:
                            pe.wait_ge(sem["yadd"], i - 1)
                        for h in range(2):
                            last = nc.tensor.matmul(YB[i % 2][:, (t % 2) * D:(t % 2 + 1) * D],
                                                    og[:, h, t * P:(t + 1) * P], wo[:, h, :],
                                                    start=(h == 0), stop=(h == 1))
                        if t % 2:
                            last.then_inc(sem["y"], 1)

                @block.gpsimd
                def _(gp):
                    chain = Chain(gp, sem["pool"])
                    nc.gpsimd.tensor_copy(small[:, :, 0], slope[:, bass.ds(pr * 2, 2)])
                    nc.gpsimd.tensor_copy(small[:, :, 1], nw[:, bass.ds(pr * 2, 2)]).then_inc(sem["small"], 1)

                    def decay_queries(h):
                        gp.wait_ge(sem["evac"], nth[("q", h, GROUPS - 1)] + 1)
                        gp.wait_ge(sem["dec"], 1)
                        if h:
                            gp.wait_ge(sem["o"], GROUPS)
                        nc.gpsimd.tensor_tensor(qd[:].rearrange("p (b m) -> p b m", m=P),
                                                qT[:, h, :].rearrange("p (b m) -> p b m", m=P),
                                                qdec[:, h, :].unsqueeze(1).to_broadcast([P, TILES, P]),
                                                ALU.mult).then_inc(sem["qd"], 1)

                    def squares(h):
                        for j in range(GROUPS):
                            n = h * GROUPS + j
                            gp.wait_ge(sem["oT"], n + 1)
                            if n:
                                gp.wait_ge(sem["sq"], n)
                            chain.link(nc.gpsimd.tensor_tensor(sq[:], oT[:, n % 2, :], oT[:, n % 2, :], ALU.mult))
                            at = ssum[:, j * GN:(j + 1) * GN]
                            nc.gpsimd.tensor_tensor(at, at, sq[:], ALU.add).then_inc(sem["sq"], 1)

                    decay_queries(0)
                    squares(0)
                    decay_queries(1)
                    squares(1)

                @block.vector
                def _(ve):
                    chain = Chain(ve, sem["vec"])
                    ve.wait_ge(sem["small"], 1)
                    chain.did(nc.vector.tensor_scalar(small[:, :, 1], small[:, :, 1], 0.5, None, ALU.mult))
                    nc.vector.tensor_scalar(small[:, :, 0], small[:, :, 0], -1.0, None, ALU.mult).then_inc(sem["sneg"], 1)
                    ve.wait_ge(sem["dec"], 1)
                    chain.link(nc.vector.tensor_tensor(dmask[:], dmask[:],
                                                       steps[:, 1:2, :].to_broadcast([P, 2, P]), ALU.mult))

                    def take_keys(h):
                        for j in range(GROUPS):
                            n = h * GROUPS + j
                            ve.wait_ge(sem["ktr"], n + 1)
                            if h and j == 0:
                                ve.wait_ge(sem["dl"], GROUPS)
                            nc.vector.tensor_scalar(ktok[:, j * GT:(j + 1) * GT, :].rearrange("p t d -> p (t d)"),
                                                    KTR[:], kbdec[:, h, 1:2], None, ALU.mult).then_inc(sem["ktok"], 1)

                    def states(h, j):
                        n = h * GROUPS + j
                        ve.wait_ge(sem["dl"], n + 1)
                        if h and j == 0:
                            ve.wait_ge(sem["o"], GROUPS)
                        for b in range(j * GT, min(j * GT + GT, TILES - 1)):
                            if b:
                                ve.wait_ge(sem["st"], h * (TILES - 1) + b)
                            nc.vector.scalar_tensor_tensor(state[:, b + 1, :], state[:, b, :], kbdec[:, h, 0:1],
                                                           DL[:, (b % GT) * P:(b % GT + 1) * P], ALU.mult,
                                                           ALU.add).then_inc(sem["st"], 1)

                    def mask_scores(h, j):
                        n = h * GROUPS + j
                        ve.wait_ge(sem["sc"], n + 1)
                        if n >= 2:
                            ve.wait_ge(sem["o"], n - 1)
                        nc.vector.tensor_tensor(smask[:, n % 2], SC[:].rearrange("p (t m) -> p t m", t=GT),
                                                dmask[:, h, :].unsqueeze(1).to_broadcast([P, GT, P]),
                                                ALU.mult).then_inc(sem["sm"], 1)

                    def gate(h, j):
                        n = h * GROUPS + j
                        if j == 0:
                            ve.wait_ge(sem["evac"], nth[("g", h, GROUPS - 1)] + 1)
                            at = gT[:]
                            chain.link(nc.vector.tensor_scalar(at, at, 1.0, small[:, h, 1:2], ALU.add, ALU.mult))
                        ve.wait_ge(sem["oT"], n + 1)
                        at = slice(j * GN, (j + 1) * GN)
                        nc.vector.tensor_tensor(og[:, h, at], oT[:, n % 2, :], gT[:, at], ALU.mult).then_inc(sem["og"], 1)

                    for h in range(2):
                        take_keys(h)
                        for j in range(GROUPS + 1):
                            if j < GROUPS:
                                states(h, j)
                                mask_scores(h, j)
                            if j:
                                gate(h, j - 1)
                    for i in range(TILES // 2):
                        ve.wait_ge(sem["y"], i + 1)
                        at = yacc[:, 2 * i:2 * i + 2, :].rearrange("p t n -> p (t n)")
                        nc.vector.tensor_tensor(at, at, YB[i % 2][:], ALU.add).then_inc(sem["yadd"], 1)
            sem.clear()

        with nc.Block() as block:
            @block.tensor
            def _(pe):
                for t in range(TILES):
                    last = nc.tensor.matmul(bank[0][:, t:t + 1], ssum[:, t * P:(t + 1) * P], ones[:], start=True, stop=True)
                last.then_inc(sem["ss"], 1)

            @block.scalar
            def _(a):
                a.wait_ge(sem["ss"], 1)
                nc.scalar.activation(rms[:, 0, :], bank[0][:, 0:TILES], ACT.Sqrt, bias=reps[:],
                                     scale=1.0 / F1).then_inc(sem["rstd"], 1)

            @block.vector
            def _(ve):
                chain = Chain(ve, sem["vec"])
                ve.wait_ge(sem["rstd"], 1)
                chain.link(nc.vector.reciprocal(rms[:, 1, :], rms[:, 0, :]))
                for t in range(TILES):
                    chain.did(nc.vector.scalar_tensor_tensor(yacc[:, t, :], yacc[:, t, :], rms[:, 1, t:t + 1],
                                                             gates[:, 1, 0, :], ALU.mult, ALU.mult))
                chain.settle()
                nc.vector.tensor_tensor(x[:], x[:], yacc[:], ALU.add)
        sem.clear()


def ternary_ffn(nc, bank, x, ident, eps, mods, gates, ins, out):
    with ExitStack() as c:
        sb = lambda n, s, dt=F32: c.enter_context(nc.sbuf_tensor(f"tf_{n}", s, dt))
        norm = Norm(nc, c, "tf", ident, eps, bank[0:2])
        hT = sb("hT", [P, KD, GN])
        raw = sb("raw", [P, 3, KD * DE])
        low = sb("low", [P, KD * DE])
        tern = sb("tern", [P, 3, KD * DE])
        asum = sb("asum", [P, 3])
        ones = sb("ones", [P, P])
        scale = sb("scale", [P, 3])
        half = sb("half", [P, 2, 3])
        hid = sb("hid", [P, KE, GN])
        act = sb("act", [P, 2, GN])
        upd = sb("upd", [P, GT, D])
        sem = Stage(nc, c, "tf", *LN_SEMS, "load", "abs", "sum", "up", "gate", "silu", "hid", "down", "store", "xdone")
        wu = tern[:, 0, :].rearrange("p (k n) -> p k n", k=KD)
        wg = tern[:, 1, :].rearrange("p (k n) -> p k n", k=KD)
        wd = tern[:, 2, :].rearrange("p (k n) -> p k n", k=KE)

        with nc.Block() as block:
            @block.sync
            def _(sp):
                for i, name in enumerate(("wup", "wgate", "wdown")):
                    sp.dma_start(raw[:, i, :], ins[name]).then_inc(sem["load"], 16)

            @block.vector
            def _(v):
                chain = Chain(v, sem["vec"])
                nc.vector.memset(ones[:], 1.0)
                v.wait_ge(sem["load"], 48)
                nc.vector.tensor_reduce(asum[:], raw[:], AX.X, ALU.add, apply_absolute_value=True).then_inc(sem["abs"], 1)
                v.wait_ge(sem["sum"], 1)
                chain.link(nc.vector.tensor_scalar(scale[:], bank[0][:, 0:3], 1.0 / (D * DE), 1e-8, ALU.mult, ALU.add))
                chain.did(nc.vector.tensor_scalar(half[:, 0, :], scale[:], 0.5, None, ALU.mult))
                chain.link(nc.vector.tensor_scalar(half[:, 1, :], scale[:], -0.5, None, ALU.mult))
                for i in range(3):
                    chain.did(nc.vector.tensor_scalar(low[:], raw[:, i, :], half[:, 1, i:i + 1], None, ALU.is_lt))
                    chain.settle()
                    chain.link(nc.vector.scalar_tensor_tensor(tern[:, i, :], raw[:, i, :], half[:, 0, i:i + 1], low[:],
                                                              ALU.is_gt, ALU.subtract))

            @block.tensor
            def _(pe):
                pe.wait_ge(sem["abs"], 1)
                nc.tensor.matmul(bank[0][:, 0:3], ones[:], asum[:], start=True, stop=True).then_inc(sem["sum"], 1)
        sem.clear()

        with nc.Fori(0, GROUPS) as g:
            with nc.Block() as block:
                @block.tensor
                def _(pe):
                    norm.tensor(nc, pe, sem)
                    pe.wait_ge(sem["ln_ha"], 1)
                    pe.wait_ge(sem["ln_hv"], 1)
                    for e in range(KE):
                        if e >= 2:
                            pe.wait_ge(sem["silu"], e - 1)
                        for k in range(KD):
                            last = nc.tensor.matmul(bank[2 + e % 2][:], wu[:, k, e * P:(e + 1) * P], hT[:, k, :],
                                                    start=(k == 0), stop=(k == KD - 1))
                        last.then_inc(sem["up"], 1)
                        if e >= 2:
                            pe.wait_ge(sem["hid"], e - 1)
                        for k in range(KD):
                            last = nc.tensor.matmul(bank[4 + e % 2][:], wg[:, k, e * P:(e + 1) * P], hT[:, k, :],
                                                    start=(k == 0), stop=(k == KD - 1))
                        last.then_inc(sem["gate"], 1)
                    pe.wait_ge(sem["hid"], KE)
                    for t in range(GT):
                        for e in range(KE):
                            last = nc.tensor.matmul(bank[6 + t // 2][:, (t % 2) * D:(t % 2 + 1) * D],
                                                    hid[:, e, t * P:(t + 1) * P], wd[:, e, :],
                                                    start=(e == 0), stop=(e == KE - 1))
                        if t % 2:
                            last.then_inc(sem["down"], 1)

                @block.scalar
                def _(a):
                    norm.scalar_std(nc, a, sem)
                    norm.modulate(nc, a, None, sem, hT, mods[:, 1, 1, 1, :], mods[:, 1, 1, 0, :])
                    for e in range(KE):
                        a.wait_ge(sem["up"], e + 1)
                        if e >= 2:
                            a.wait_ge(sem["hid"], e - 1)
                        nc.scalar.activation(act[:, e % 2, :], bank[2 + e % 2][:], ACT.Silu,
                                             scale=scale[:, 0:1]).then_inc(sem["silu"], 1)

                @block.vector
                def _(v):
                    chain = Chain(v, sem["vec"])
                    x4 = x[:, bass.ds(g * GT, GT), :]
                    norm.vector(nc, v, chain, sem, x4)
                    norm.modulate(nc, None, v, sem, hT, mods[:, 1, 1, 1, :], mods[:, 1, 1, 0, :])
                    for e in range(KE):
                        v.wait_ge(sem["silu"], e + 1)
                        v.wait_ge(sem["gate"], e + 1)
                        nc.vector.scalar_tensor_tensor(hid[:, e, :], bank[4 + e % 2][:], scale[:, 1:2],
                                                       act[:, e % 2, :], ALU.mult, ALU.mult).then_inc(sem["hid"], 1)
                    for i in range(GT // 2):
                        v.wait_ge(sem["down"], i + 1)
                        y = bank[6 + i][:].rearrange("p (t n) -> p t n", t=2)
                        chain.did(nc.vector.scalar_tensor_tensor(
                            upd[:, 2 * i:2 * i + 2, :], y, scale[:, 2:3],
                            gates[:, 1, 1:2, :].to_broadcast([P, 2, D]), ALU.mult, ALU.mult))
                    chain.settle()
                    nc.vector.tensor_tensor(x4, x4, upd[:], ALU.add).then_inc(sem["xdone"], 1)

                @block.sync
                def _(sp):
                    sp.wait_ge(sem["xdone"], 1)
                    sp.dma_start(out[:, bass.ds(g * GT, GT), :], x[:, bass.ds(g * GT, GT), :]).then_inc(sem["store"], 16)
                    sp.wait_ge(sem["store"], 16)
            sem.clear()


class Banks:

    def __init__(self, whole):
        self.whole = whole
        self.each = [whole[:, i, :] for i in range(8)]

    def __getitem__(self, i):
        return self.each[i]


def build(nc, ins, out, upto=99):
    parts_dram = nc.dram_tensor("qk_parts", [2, 3, D, S], BF16, kind="Internal").ap()
    with ExitStack() as ctx:
        sb = lambda n, s, dt=F32: ctx.enter_context(nc.sbuf_tensor(n, s, dt))
        bank = Banks(ctx.enter_context(nc.psum_tensor("psum", [P, 8, 512], F32)))
        x = sb("x", [P, TILES, D])
        ident = sb("ident", [P, P])
        eps = sb("eps", [P, 1])
        mods = sb("mods", [P, 2, 2, 2, KD])
        gates = sb("gates", [P, 2, 2, D])
        sem = Stage(nc, ctx, "top", "load")
        with nc.Block() as block:
            @block.sync
            def _(sp):
                sp.dma_start(x[:], ins["x"]).then_inc(sem["load"], 16)
                sp.dma_start(ident[:], ins["ident"]).then_inc(sem["load"], 16)
                sp.wait_ge(sem["load"], 32)

            @block.vector
            def _(v):
                nc.vector.memset(eps[:], LN_EPS)
        modulation(nc, ctx, bank, mods, gates, ins)
        with ExitStack() as c0:
            attn = c0.enter_context(nc.sbuf_tensor("attn", [P, TILES, D], F32))
            with nc.sbuf_tensor("v_all", [P, TILES, D], F32) as v_all:
                rope_front(nc, bank, x, v_all, ident, eps, mods, parts_dram, ins)
                rope_attention(nc, bank, v_all, attn, ident, parts_dram, ins)
            routed_ffn(nc, bank, x, attn, ident, eps, mods, gates, ins)
        with nc.sbuf_tensor("hT1", [P, KD, S], F32) as hT:
            decay_front(nc, bank, x, hT, ident, eps, mods)
            decay_attention(nc, bank, x, hT, ident, mods, gates, ins)
        ternary_ffn(nc, bank, x, ident, eps, mods, gates, ins, out)


def lay_out(i, np):
    kp = lambda a: np.ascontiguousarray(a.reshape(-1, P, a.shape[-1]).transpose(1, 0, 2))
    o = {}
    o["x"] = i["L0_attn_x"].reshape(TILES, P, D).transpose(1, 0, 2)
    o["ident"] = np.eye(P, dtype=np.float32)
    for l in range(2):
        o[f"c{l}"] = i[f"L{l}_c"].reshape(KD, P).T
        o[f"wmod{l}"] = kp(i[f"L{l}_wmod"])
    o["wqk"] = kp(np.concatenate([i["L0_attn_wq"].T, i["L0_attn_wk"].T], axis=1))
    o["wv"] = kp(i["L0_attn_wv"].T)
    pos = np.arange(S, dtype=np.float32)[:, None]
    inv = np.float32(10000.0) ** (-(np.arange(0, DK, 2, dtype=np.float32) / np.float32(DK)))
    ang = (pos * inv.astype(np.float32)).astype(np.float32)
    cos, sin = np.cos(ang), np.sin(ang)
    cos = np.stack([cos, cos], -1).reshape(TILES, P, DK)
    sin = np.stack([-sin, sin], -1).reshape(TILES, P, DK)
    o["cos"] = cos.transpose(1, 0, 2).astype(np.float32)
    o["sin"] = sin.transpose(1, 0, 2).astype(np.float32)
    r = np.arange(P)
    later = np.where(r[None, :] > r[:, None], np.float32(-1e30), np.float32(0))
    o["mask"] = np.stack([later, later.T], 1).astype(np.float32)
    o["wo"] = kp(i["L0_attn_wo"].T)
    a = i["L0_ffn_A"].reshape(D, D)
    o["wbase"] = kp(np.concatenate([i["L0_ffn_W"].T, a.T], axis=1))
    o["wexp"] = kp(i["L0_ffn_B"].transpose(0, 2, 1).reshape(D, D))
    o["rw1"] = kp(i["L0_ffn_rw1"].T)
    o["rw2"] = i["L0_ffn_rw2"][:EXPERTS].T
    o["rb1"] = i["L0_ffn_rb1"].reshape(RHID, 1)
    o["rows"] = np.stack([i["L0_ffn_rb2"][:EXPERTS], i["L0_ffn_gates"]]).reshape(1, 2, EXPERTS)
    o["bias"] = i["L0_ffn_bias"].reshape(1, D)
    o["iota"] = np.tile(np.arange(EXPERTS, dtype=np.float32), (P, 1))
    w = i["L1_attn_Wqkv"].reshape(PAIRS, 2, 3, D1, D)
    wg = i["L1_attn_Wg"].reshape(PAIRS, 2, D1, D)
    each = np.stack([w[:, 0, 0], w[:, 1, 0], w[:, 0, 1], w[:, 1, 1], wg[:, 0], wg[:, 1], w[:, 0, 2], w[:, 1, 2]], 1)
    each = each.reshape(PAIRS, 8 * D1, KD, P)
    o["wpair"] = each.transpose(0, 3, 2, 1)
    o["wo1"] = i["L1_attn_Wo"].reshape(D, PAIRS, 2, D1).transpose(1, 3, 2, 0)
    o["nw"] = i["L1_attn_norm_w"].reshape(H1, D1).T
    o["slope"] = np.tile(i["L1_attn_slope_rate"].reshape(1, H1), (P, 1))
    m, n = r[None, :], r[:, None]
    last = np.zeros((P, P), np.float32)
    last[:, 0] = P
    last[:, 1] = P - 1 - r
    o["steps"] = np.stack([np.maximum(m - n, 0), m >= n, np.broadcast_to(m + 1, (P, P)), last], 1).astype(np.float32)
    o["wup"] = kp(i["L1_ffn_W_up"].T).reshape(P, KD * DE)
    o["wgate"] = kp(i["L1_ffn_W_gate"].T).reshape(P, KD * DE)
    o["wdown"] = kp(i["L1_ffn_W_down"].T).reshape(P, KE * D)
    return {k: np.ascontiguousarray(a) for k, a in o.items()}


def kernel(**inputs):
    import numpy as np
    import concourse.bacc as bacc
    from concourse.bass_utils import run_bass_kernel_spmd

    arrays = lay_out({k: np.asarray(a) for k, a in inputs.items()}, np)
    nc = bacc.Bacc("TRN2", target_bir_lowering=False, num_devices=1)
    ins = {k: nc.dram_tensor(f"in_{k}", a.shape, mybir.dt.from_np(a.dtype), kind="ExternalInput").ap()
           for k, a in arrays.items()}
    out = nc.dram_tensor("out", [P, TILES, D], F32, kind="ExternalOutput").ap()
    build(nc, ins, out)
    r = run_bass_kernel_spmd(nc, [{f"in_{k}": a for k, a in arrays.items()}], core_ids=[0])
    return r.results[0]["out"].transpose(1, 0, 2).reshape(1, S, D)
```

```python
from contextlib import ExitStack

import concourse.bass as bass
from concourse import mybir

F32 = mybir.dt.float32
F32R = mybir.dt.float32r
BF16 = mybir.dt.bfloat16
U32 = mybir.dt.uint32
ALU = mybir.AluOpType
ACT = mybir.ActivationFunctionType
AX = mybir.AxisListType

P = 128
S = 2048
D = 256
KD = D // P
TILES = S // P
GT = 4
GROUPS = TILES // GT
GN = GT * P
LN_EPS = 1e-5

H0, DK = 16, 16
HG = 4
HGROUPS = H0 // HG
VW = 32
Q_PART = (0, 0, 1, 1, 0, 2)
K_PART = (0, 1, 0, 1, 2, 0)
TERMS = len(Q_PART) * DK
RHID, EXPERTS = 64, 16

H1, D1 = 16, 128
PAIRS = H1 // 2
F1 = H1 * D1
DE = 1024
KE = DE // P
RMS_EPS = 1.1920928955078125e-07


class Stage:

    def __init__(self, nc, ctx, stage, *names):
        self.nc = nc
        self.made = {n: ctx.enter_context(nc.semaphore(f"{stage}_{n}")) for n in names}

    def __getitem__(self, name):
        return self.made[name]

    def clear(self):
        for s in self.made.values():
            self.nc.gpsimd.sem_clear(s)
        self.nc.all_engine_barrier()


class Chain:

    def __init__(self, eng, sem):
        self.eng, self.sem, self.n = eng, sem, 0

    def did(self, ins):
        ins.then_inc(self.sem, 1)
        self.n += 1

    def settle(self):
        self.eng.wait_ge(self.sem, self.n)

    def link(self, ins):
        self.did(ins)
        self.settle()


def product(nc, out, a, b, start, stop):
    nc.tensor.matmul(out, a[0], b[0], start=start, stop=False)
    nc.tensor.matmul(out, a[0], b[1], start=False, stop=False)
    return nc.tensor.matmul(out, a[1], b[0], start=False, stop=stop)


LN_SEMS = ("ln_stats", "ln_std", "ln_xn", "ln_tr", "ln_ha", "ln_hv", "ln_hi", "ln_lo", "vec")


class Norm:

    def __init__(self, nc, ctx, name, ident, eps, banks):
        sb = lambda n, s: ctx.enter_context(nc.sbuf_tensor(f"{name}_{n}", s, F32))
        self.stats = sb("stats", [P, GT, 6])
        self.mv = sb("mv", [P, GT, 2])
        self.std = sb("std", [P, GT])
        self.rstd = sb("rstd", [P, GT])
        self.xn = sb("xn", [P, GT, D])
        self.ident, self.eps, self.banks = ident, eps, banks

    def vector(self, nc, v, chain, sem, x4):
        self.moments(nc, v, chain, sem, x4)
        self.normalize(nc, v, chain, sem, x4)

    def moments(self, nc, v, chain, sem, x4):
        for t in range(GT):
            chain.did(nc.vector.bn_stats(self.stats[:, t, :], x4[:, t, :]))
        chain.settle()
        for t in range(GT):
            last = nc.vector.bn_aggr(self.mv[:, t, :], self.stats[:, t, :])
        last.then_inc(sem["ln_stats"], 1)

    def normalize(self, nc, v, chain, sem, x4):
        v.wait_ge(sem["ln_std"], 1)
        chain.link(nc.vector.reciprocal(self.rstd[:], self.std[:]))
        for t in range(GT):
            last = nc.vector.tensor_scalar(self.xn[:, t, :], x4[:, t, :], self.mv[:, t, 0:1],
                                           self.rstd[:, t:t + 1], ALU.subtract, ALU.mult)
        last.then_inc(sem["ln_xn"], 1)

    def scalar_std(self, nc, a, sem):
        a.wait_ge(sem["ln_stats"], 1)
        nc.scalar.activation(self.std[:], self.mv[:, :, 1], ACT.Sqrt, bias=self.eps[:]).then_inc(sem["ln_std"], 1)

    def tensor(self, nc, pe, sem):
        pe.wait_ge(sem["ln_xn"], 1)
        for k in range(KD):
            for t in range(GT):
                last = nc.tensor.transpose(self.banks[k][:, t * P:(t + 1) * P],
                                           self.xn[:, t, k * P:(k + 1) * P], self.ident[:])
        last.then_inc(sem["ln_tr"], 1)

    def split(self, nc, a, v, sem, h, hi, lo):
        if a is not None:
            a.wait_ge(sem["ln_ha"], 1)
            nc.scalar.copy(hi[:, 0, :], h[:, 0, :]).then_inc(sem["ln_hi"], 1)
            a.wait_ge(sem["ln_hv"], 1)
            nc.scalar.copy(hi[:, 1, :], h[:, 1, :]).then_inc(sem["ln_hi"], 1)
        if v is not None:
            v.wait_ge(sem["ln_hv"], 1)
            for k in range(KD):
                v.wait_ge(sem["ln_hi"], k + 1)
                nc.vector.tensor_tensor(lo[:, k, :], h[:, k, :], hi[:, k, :].bitcast(F32),
                                        ALU.subtract).then_inc(sem["ln_lo"], 1)

    def modulate(self, nc, a, v, sem, hT, scale1, shift):
        if a is not None:
            a.wait_ge(sem["ln_tr"], 1)
            nc.scalar.activation(hT[:, 0, :], self.banks[0][:], ACT.Identity, bias=shift[:, 0:1],
                                 scale=scale1[:, 0:1]).then_inc(sem["ln_ha"], 1)
        if v is not None:
            v.wait_ge(sem["ln_tr"], 1)
            nc.vector.tensor_scalar(hT[:, 1, :], self.banks[1][:], scale1[:, 1:2], shift[:, 1:2],
                                    ALU.mult, ALU.add).then_inc(sem["ln_hv"], 1)


def modulation(nc, ctx, bank, mods, gates, ins):
    with ExitStack() as c:
        sb = lambda n, s: c.enter_context(nc.sbuf_tensor(f"mod_{n}", s, F32))
        cT = sb("cT", [P, 2, KD])
        scT = sb("scT", [P, 2, KD])
        scb = sb("scb", [P, 2, KD, P])
        ones = sb("ones", [P, P])
        wm = sb("wm", [P, 2, KD, 6 * D])
        mag = sb("mag", [P, 2, 2, D])
        sgn = sb("sgn", [P, 2, 2, D])
        sem = Stage(nc, c, "mod", "load", "silu", "rep", "cols", "rows", "vec")
        with nc.Block() as block:
            @block.sync
            def _(sp):
                for l in range(2):
                    sp.dma_start(cT[:, l, :], ins[f"c{l}"]).then_inc(sem["load"], 16)
                    sp.dma_start(wm[:, l], ins[f"wmod{l}"]).then_inc(sem["load"], 16)

            @block.scalar
            def _(a):
                a.wait_ge(sem["load"], 64)
                nc.scalar.activation(scT[:], cT[:], ACT.Silu).then_inc(sem["silu"], 1)

            @block.tensor
            def _(pe):
                pe.wait_ge(sem["silu"], 1)
                for l in range(2):
                    for j in range(12):
                        for k in range(KD):
                            last = nc.tensor.matmul(bank[0][:, l * 12 + j:l * 12 + j + 1],
                                                    wm[:, l, k, j * P:(j + 1) * P], scT[:, l, k:k + 1],
                                                    start=(k == 0), stop=(k == KD - 1))
                last.then_inc(sem["cols"], 1)
                pe.wait_ge(sem["rep"], 1)
                for l in range(2):
                    for n, at in enumerate((2 * D, 5 * D)):
                        for k in range(KD):
                            last = nc.tensor.matmul(bank[1 + l][:, n * D:(n + 1) * D], scb[:, l, k, :],
                                                    wm[:, l, k, at:at + D], start=(k == 0), stop=(k == KD - 1))
                last.then_inc(sem["rows"], 1)

            @block.vector
            def _(v):
                chain = Chain(v, sem["vec"])
                chain.link(nc.vector.memset(ones[:], 1.0))
                v.wait_ge(sem["silu"], 1)
                for l in range(2):
                    for k in range(KD):
                        last = nc.vector.tensor_scalar(scb[:, l, k, :], ones[:], scT[:, l, k:k + 1], None, ALU.mult)
                last.then_inc(sem["rep"], 1)
                v.wait_ge(sem["cols"], 1)
                for l in range(2):
                    for part in range(2):
                        at = l * 12 + part * 6
                        nc.vector.tensor_copy(mods[:, l, part, 0, :], bank[0][:, at:at + 2])
                        nc.vector.tensor_scalar(mods[:, l, part, 1, :], bank[0][:, at + 2:at + 4], 1.0, None, ALU.add)
                v.wait_ge(sem["rows"], 1)
                for l in range(2):
                    g = bank[1 + l][:].rearrange("p (n d) -> p n d", n=2)
                    chain.link(nc.vector.tensor_copy(mag[:, l], g))
                    chain.link(nc.vector.scalar_tensor_tensor(mag[:, l], mag[:, l], -1.0, mag[:, l], ALU.mult, ALU.max))
                    chain.did(nc.vector.tensor_scalar(mag[:, l], mag[:, l], 0.25, None, ALU.max))
                    chain.did(nc.vector.tensor_scalar(sgn[:, l], g, 0.0, 2.0, ALU.is_ge, ALU.mult))
                chain.settle()
                nc.vector.scalar_tensor_tensor(gates[:], sgn[:], -1.0, mag[:], ALU.add, ALU.mult)
        sem.clear()


def rope_front(nc, bank, x, v_all, ident, eps, mods, parts_dram, ins):
    with ExitStack() as c:
        sb = lambda n, s, dt=F32: c.enter_context(nc.sbuf_tensor(f"rf_{n}", s, dt))
        norm = Norm(nc, c, "rf", ident, eps, bank[0:2])
        hT = sb("hT", [P, KD, GN])
        wqk = sb("wqk", [P, KD, 2 * D])
        wv = sb("wv", [P, KD, D])
        cos = sb("cos", [P, TILES, DK])
        sin = sb("sin", [P, TILES, DK])
        straight = sb("straight", [P, 2, 2 * D])
        crossed = sb("crossed", [P, 2, 2 * D])
        turned = sb("turned", [P, GT, 2 * D])
        part = sb("part", [P, 4, 3, GN], BF16)
        rest = sb("rest", [P, 4, GN])
        sem = Stage(nc, c, "rf", *LN_SEMS, "load", "qk", "v", "turned", "vcopy", "tr", "high", "rest", "parts",
                    "pool", "store")
        heads = 2 * D // DK
        pairs = lambda ap: ap.rearrange("p (h i two) -> p h i two", i=DK // 2, two=2)

        def table(t, g, n):
            row = t[:, bass.ds(g * GT + n, 1), :].rearrange("p one (i two) -> p one i two", two=2)
            return row.to_broadcast([P, heads, DK // 2, 2])

        with nc.Block() as block:
            @block.sync
            def _(sp):
                sp.dma_start(wqk[:], ins["wqk"]).then_inc(sem["load"], 16)
                sp.dma_start(wv[:], ins["wv"]).then_inc(sem["load"], 16)
                sp.dma_start(cos[:], ins["cos"]).then_inc(sem["load"], 16)
                sp.dma_start(sin[:], ins["sin"]).then_inc(sem["load"], 16)
                sp.wait_ge(sem["load"], 64)
        sem.clear()
        with nc.Fori(0, GROUPS) as g:
            with nc.Block() as block:
                @block.vector
                def _(v):
                    chain = Chain(v, sem["vec"])
                    norm.vector(nc, v, chain, sem, x[:, bass.ds(g * GT, GT), :])
                    norm.modulate(nc, None, v, sem, hT, mods[:, 0, 0, 1, :], mods[:, 0, 0, 0, :])
                    for t in range(GT):
                        v.wait_ge(sem["qk"], t + 1)
                        chain.did(nc.vector.tensor_tensor(pairs(straight[:, t % 2, :]), pairs(bank[2][:]),
                                                          table(cos, g, t), ALU.mult))
                        chain.link(nc.vector.tensor_tensor(pairs(crossed[:, t % 2, :]),
                                                           pairs(bank[2][:])[:, :, :, ::-1],
                                                           table(sin, g, t), ALU.mult))
                        nc.vector.tensor_tensor(turned[:, t, :], straight[:, t % 2, :], crossed[:, t % 2, :],
                                                ALU.add).then_inc(sem["turned"], 1)
                    for j in range(4):
                        v.wait_ge(sem["high"], j + 1)
                        nc.vector.tensor_tensor(rest[:, j, :], bank[4 + j][:], part[:, j, 0, :],
                                                ALU.subtract).then_inc(sem["rest"], 1)

                @block.scalar
                def _(a):
                    norm.scalar_std(nc, a, sem)
                    norm.modulate(nc, a, None, sem, hT, mods[:, 0, 0, 1, :], mods[:, 0, 0, 0, :])
                    for t in range(GT):
                        a.wait_ge(sem["v"], t + 1)
                        nc.scalar.copy(v_all[:, bass.ds(g * GT + t, 1), :],
                                       bank[3][:, 0:D].unsqueeze(1)).then_inc(sem["vcopy"], 1)
                    for j in range(4):
                        a.wait_ge(sem["tr"], j + 1)
                        nc.scalar.copy(part[:, j, 0, :], bank[4 + j][:]).then_inc(sem["high"], 1)

                @block.tensor
                def _(pe):
                    norm.tensor(nc, pe, sem)
                    pe.wait_ge(sem["ln_ha"], 1)
                    pe.wait_ge(sem["ln_hv"], 1)
                    for t in range(GT):
                        if t:
                            pe.wait_ge(sem["turned"], t)
                        for k in range(KD):
                            last = nc.tensor.matmul(bank[2][:], hT[:, k, t * P:(t + 1) * P], wqk[:, k, :],
                                                    start=(k == 0), stop=(k == KD - 1))
                        last.then_inc(sem["qk"], 1)
                        if t:
                            pe.wait_ge(sem["vcopy"], t)
                        for k in range(KD):
                            last = nc.tensor.matmul(bank[3][:, 0:D], hT[:, k, t * P:(t + 1) * P], wv[:, k, :],
                                                    start=(k == 0), stop=(k == KD - 1))
                        last.then_inc(sem["v"], 1)
                    pe.wait_ge(sem["turned"], GT)
                    for j in range(4):
                        for t in range(GT):
                            last = nc.tensor.transpose(bank[4 + j][:, t * P:(t + 1) * P],
                                                       turned[:, t, j * P:(j + 1) * P], ident[:])
                        last.then_inc(sem["tr"], 1)

                @block.gpsimd
                def _(gp):
                    chain = Chain(gp, sem["pool"])
                    for j in range(4):
                        gp.wait_ge(sem["rest"], j + 1)
                        chain.link(nc.gpsimd.tensor_copy(part[:, j, 1, :], rest[:, j, :]))
                        nc.gpsimd.tensor_tensor(part[:, j, 2, :], rest[:, j, :], part[:, j, 1, :],
                                                ALU.subtract).then_inc(sem["parts"], 1)

                @block.sync
                def _(sp):
                    for j in range(4):
                        sp.wait_ge(sem["parts"], j + 1)
                        half = (j % 2) * P
                        dst = parts_dram[j // 2, :, half:half + P, bass.ds(g * GN, GN)].rearrange("c p s -> p c s")
                        sp.dma_start(dst, part[:, j]).then_inc(sem["store"], 16)
                    sp.wait_ge(sem["store"], 64)
            sem.clear()


def attention_order():
    order = []
    steps = [(0, 3), (1, 3), (0, 2), (1, 2), (0, 1), (0, 0), (1, 1), (1, 0)]
    maxima = [(s, piece) for s, (_, cq) in enumerate(steps) for piece in pieces(cq)]
    exps = [(s, kb, h) for s, (_, cq) in enumerate(steps) for kb in range(GT * (cq + 1)) for h in range(HG)]
    pe = dve = act = 0.0
    reduced, exped = [], []
    parts, rows = {}, {}
    m = e = shifted = 0
    while e < len(exps):
        s, kb, h = exps[e]
        if shifted < len(steps) and shifted <= s + 1 and parts.get(shifted, 1e9) <= max(pe, act if shifted > s else 0):
            order.append(("shift", shifted))
            pe += 0.3
            act = max(act, pe) + 2.0
            rows[shifted] = act
            shifted += 1
            continue
        can_m = m < len(maxima) and maxima[m][0] <= s + 3
        can_e = s in rows and (rows[s] <= pe or not can_m)
        if not can_e and not can_m:
            pe = max(pe, parts[shifted])
            continue
        at_m = max(pe, reduced[m - 3] if m >= 3 else 0.0)
        at_e = max(pe, exped[e - 3] if e >= 3 else 0.0)
        if can_m and (not can_e or (at_m <= at_e + 0.3 and dve <= act)):
            step, piece = maxima[m]
            order.append(("max", step, piece))
            pe = at_m + piece[4] / 2400
            dve = max(dve, pe + 0.1) + piece[4] / 960 + 0.07
            reduced.append(dve)
            m += 1
            if m == len(maxima) or maxima[m][0] != step:
                dve += 0.15
                parts[step] = dve + 1.5
        else:
            w = GN - max(0, kb - GT * steps[s][1]) * P
            order.append(("exp", s, kb, h))
            pe = max(at_e, rows[s]) + w / 2400
            act = max(act, pe + 0.1) + w / 1200 + 0.05
            exped.append(act)
            e += 1
            if h == HG - 1:
                pe = max(pe, exped[e - HG - 1] if e > HG else 0.0) + 0.85 * w / GN
                if kb == 1 and s:
                    order.append(("turn", s - 1))
                    pe, dve, act = pe + 0.25, dve + 0.5, act + 0.5
    return steps, order + [("turn", len(steps) - 1)]


def pieces(cq):
    return [(t * HG + h, h, t, p, GN if p < cq else P * (t + 1))
            for t in range(GT) for h in range(HG) for p in range(cq + 1)]


def rope_attention(nc, bank, v_all, attn, ident, parts_dram, ins):
    steps, order = attention_order()
    with ExitStack() as c:
        sb = lambda n, s, dt=F32: c.enter_context(nc.sbuf_tensor(f"ra_{n}", s, dt))
        kst = sb("kst", [P, 2, HG, S], BF16)
        qst = sb("qst", [P, 2, HG, S], BF16)
        vg = sb("vg", [P, 2, TILES, HG, VW])
        prob = sb("prob", [P, 2, HG, GN])
        sums = sb("sums", [P, GN])
        pm = sb("pm", [P, 2, GT * HG, GROUPS])
        negm = sb("negm", [P, len(steps), GT * HG])
        nrest = sb("nrest", [P, 2, GT * HG])
        mp = sb("mp", [P, len(steps), GT * HG, VW], BF16)
        rec = sb("rec", [P, GT, HG])
        mask_f = sb("mask_f", [P, 2, P])
        mask = sb("mask", [P, 2, P], BF16)
        identb = sb("identb", [P, P], BF16)
        sem = Stage(nc, c, "ra", "load", "next", "vg", "pm", "red", "neg", "mp", "trm", "shift", "sc", "exp",
                    "av", "avs", "trn", "norm", "vec", "pool")
        PM, ST, AV, TR = bank[0:3], bank[3:6], bank[6], bank[7]
        TRb = TR[:].bitcast(BF16)
        LOADS = 16 * 2 * len(Q_PART)

        first_piece = [sum(len(pieces(cq)) for _, cq in steps[:s]) for s in range(len(steps) + 1)]
        first_block = [sum(GT * (cq + 1) for _, cq in steps[:s]) for s in range(len(steps) + 1)]

        first_of_second = next(s for s, (gi, _) in enumerate(steps) if gi == 1)
        last_of_first = max(s for s, (gi, _) in enumerate(steps) if gi == 0)

        def load_stacks(sp, gi, group, done):
            for side, dst, parts in ((0, qst, Q_PART), (1, kst, K_PART)):
                for j, which in enumerate(parts):
                    src = parts_dram[side, which, bass.ds(group * (HG * DK), HG * DK), :]
                    sp.dma_start(dst[j * DK:(j + 1) * DK, gi, :, :],
                                 src.rearrange("(h r) s -> r h s", r=DK)).then_inc(done, 16)

        with nc.Block() as block:
            @block.sync
            def _(sp):
                sp.dma_start(mask_f[:], ins["mask"]).then_inc(sem["load"], 16)
                load_stacks(sp, 0, 0, sem["next"])
                sp.wait_ge(sem["next"], LOADS)

            @block.vector
            def _(v):
                nc.vector.memset(kst[TERMS:P, 0], 1.0)
                nc.vector.memset(mp[:], 0.0)
                nc.vector.tensor_copy(identb[:], ident[:])
                v.wait_ge(sem["load"], 16)
                nc.vector.tensor_copy(mask[:], mask_f[:])

            @block.gpsimd
            def _(gp):
                chain = Chain(gp, sem["pool"])
                chain.link(nc.gpsimd.memset(kst[TERMS:P, 1], 1.0))
                chain.link(nc.gpsimd.memset(vg[:], 0.0))
                nc.gpsimd.memset(vg[:, :, :, :, DK:DK + 1], 1.0)
        sem.clear()

        with nc.Fori(0, HGROUPS // 2) as turn:
            with nc.Block() as block:
                @block.sync
                def _(sp):
                    load_stacks(sp, 1, turn * 2 + 1, sem["load"])
                    sp.wait_ge(sem["av"], first_block[last_of_first + 1])
                    load_stacks(sp, 0, 2 - turn * 2, sem["next"])
                    sp.wait_ge(sem["next"], LOADS)

                @block.gpsimd
                def _(gp):
                    chain = Chain(gp, sem["pool"])
                    for gi in range(2):
                        src = v_all[:, :, bass.ds((turn * 2 + gi) * (HG * DK), HG * DK)]
                        last = nc.gpsimd.tensor_copy(vg[:, gi, :, :, 0:DK],
                                                     src.rearrange("p t (h d) -> p t h d", h=HG))
                    last.then_inc(sem["vg"], 1)
                    for s in range(len(steps)):
                        gp.wait_ge(sem["neg"], s + 1)
                        m, r, to = negm[:, s, :], nrest[:, s % 2, :], mp[:, s]
                        chain.link(nc.gpsimd.tensor_copy(to[:, :, 0], m))
                        chain.link(nc.gpsimd.tensor_tensor(r, m, to[:, :, 0], ALU.subtract))
                        chain.link(nc.gpsimd.tensor_copy(to[:, :, 1], r))
                        nc.gpsimd.tensor_tensor(to[:, :, 2], r, to[:, :, 1], ALU.subtract).then_inc(sem["mp"], 1)

                @block.vector
                def _(v):
                    chain = Chain(v, sem["vec"])

                    def normalize(s):
                        gi, cq = steps[s]
                        v.wait_ge(sem["trn"], s + 1)
                        tr = TR[:].rearrange("p (t h w) -> p t h w", t=GT, h=HG)
                        chain.link(nc.vector.reciprocal(rec[:], tr[:, :, :, DK]))
                        dst = attn[:, cq * GT:(cq + 1) * GT, bass.ds((turn * 2 + gi) * (HG * DK), HG * DK)]
                        nc.vector.tensor_tensor(dst.rearrange("p t (h d) -> p t h d", h=HG), tr[:, :, :, 0:DK],
                                                rec[:].unsqueeze(3).to_broadcast([P, GT, HG, DK]),
                                                ALU.mult).then_inc(sem["norm"], 1)

                    n, waiting = 0, None
                    for entry in order:
                        if entry[0] == "max":
                            s, (row, h, t, p, w) = entry[1:]
                            v.wait_ge(sem["pm"], n + 1)
                            nc.vector.tensor_reduce(pm[:, s % 2, row, p:p + 1], PM[n % 3][:, 0:w], AX.X,
                                                    ALU.max).then_inc(sem["red"], 1)
                            n += 1
                            if n == first_piece[s + 1]:
                                v.wait_ge(sem["red"], n)
                                nc.vector.tensor_reduce(negm[:, s, :], pm[:, s % 2, :, 0:steps[s][1] + 1], AX.X,
                                                        ALU.max, negate=True).then_inc(sem["neg"], 1)
                            if waiting is not None and n >= waiting[1]:
                                normalize(waiting[0])
                                waiting = None
                        if entry[0] == "turn":
                            if waiting is not None:
                                normalize(waiting[0])
                            waiting = (entry[1], n + 3)
                        if entry[0] == "shift" and waiting is not None:
                            normalize(waiting[0])
                            waiting = None
                    normalize(waiting[0])

                @block.scalar
                def _(a):
                    def take_sums(s):
                        a.wait_ge(sem["av"], first_block[s + 1])
                        if s:
                            a.wait_ge(sem["trn"], s)
                        nc.scalar.copy(sums[:], AV[:]).then_inc(sem["avs"], 1)

                    e = 0
                    for entry in order:
                        if entry[0] == "shift":
                            s = entry[1]
                            gi, cq = steps[s]
                            a.wait_ge(sem["trm"], s + 1)
                            for h in range(HG):
                                last = nc.scalar.copy(qst[TERMS:P, gi, h, cq * GN:(cq + 1) * GN],
                                                      TRb[h * VW:(h + 1) * VW, 0:GN])
                            last.then_inc(sem["shift"], 1)
                        if entry[0] == "exp":
                            s, kb, h = entry[1:]
                            gi, cq = steps[s]
                            off = max(0, kb - GT * cq) * P
                            b = first_block[s] + kb
                            if b >= 2 and h == 0:
                                a.wait_ge(sem["av"], b - 1)
                            a.wait_ge(sem["sc"], e + 1)
                            nc.scalar.activation(prob[:, b % 2, h, off:GN], ST[e % 3][:, off:GN], ACT.Exp,
                                                 scale=float(DK) ** -0.5).then_inc(sem["exp"], 1)
                            e += 1
                            if kb == 1 and s and h == HG - 1:
                                take_sums(s - 1)
                    take_sums(len(steps) - 1)

                @block.tensor
                def _(pe):
                    n = e = turned = shifted = 0

                    def values(s, kb):
                        gi, cq = steps[s]
                        off = max(0, kb - GT * cq) * P
                        b = first_block[s] + kb
                        pe.wait_ge(sem["exp"], HG * (b + 1))
                        if kb == 0 and s:
                            pe.wait_ge(sem["avs"], s)
                        for h in range(HG):
                            last = nc.tensor.matmul(AV[h * VW:(h + 1) * VW, off:GN], vg[:, gi, kb, h, :],
                                                    prob[:, b % 2, h, off:GN], start=(kb == 0),
                                                    stop=(kb == GT * (cq + 1) - 1), skip_group_check=True)
                        last.then_inc(sem["av"], 1)

                    pe.wait_ge(sem["vg"], 1)
                    behind = None
                    for entry in order:
                        s = entry[1]
                        gi, cq = steps[s]
                        if entry[0] == "max":
                            row, h, t, p, w = entry[2]
                            if n == first_piece[first_of_second]:
                                pe.wait_ge(sem["load"], LOADS)
                            if n >= 3:
                                pe.wait_ge(sem["red"], n - 2)
                            q = qst[0:TERMS, gi, h, cq * GN + t * P:cq * GN + (t + 1) * P]
                            last = nc.tensor.matmul(PM[n % 3][:, 0:w], q, kst[0:TERMS, gi, h, p * GN:p * GN + w],
                                                    start=True, stop=(p < cq))
                            if p == cq:
                                last = nc.tensor.matmul(PM[n % 3][:, w - P:w], identb[:], mask[:, 0, :],
                                                        start=False, stop=True)
                            last.then_inc(sem["pm"], 1)
                            n += 1
                        if entry[0] == "shift":
                            pe.wait_ge(sem["mp"], s + 1)
                            if turned:
                                pe.wait_ge(sem["norm"], turned)
                            for t in range(GT):
                                rows = mp[:, s, t * HG:(t + 1) * HG, :].rearrange("p h w -> p (h w)")
                                last = nc.tensor.transpose(TRb[:, t * P:(t + 1) * P], rows, identb[:])
                            last.then_inc(sem["trm"], 1)
                            shifted += 1
                        if entry[0] == "exp":
                            kb, h = entry[2:]
                            off = max(0, kb - GT * cq) * P
                            diagonal = kb >= GT * cq
                            if kb == 0 and h == 0:
                                pe.wait_ge(sem["shift"], s + 1)
                            if e >= 3:
                                pe.wait_ge(sem["exp"], e - 2)
                            last = nc.tensor.matmul(ST[e % 3][:, off:GN], kst[:, gi, h, kb * P:(kb + 1) * P],
                                                    qst[:, gi, h, cq * GN + off:(cq + 1) * GN],
                                                    start=True, stop=not diagonal)
                            if diagonal:
                                last = nc.tensor.matmul(ST[e % 3][:, off:off + P], identb[:], mask[:, 1, :],
                                                        start=False, stop=True)
                            last.then_inc(sem["sc"], 1)
                            e += 1
                            if h == HG - 1:
                                if behind is not None:
                                    values(*behind)
                                behind = (s, kb)
                        if entry[0] == "turn":
                            if s == len(steps) - 1:
                                values(*behind)
                            pe.wait_ge(sem["avs"], s + 1)
                            pe.wait_ge(sem["shift"], shifted)
                            if turned:
                                pe.wait_ge(sem["norm"], turned)
                            for t in range(GT):
                                last = nc.tensor.transpose(TR[:, t * P:(t + 1) * P], sums[:, t * P:(t + 1) * P],
                                                           ident[:])
                            last.then_inc(sem["trn"], 1)
                            turned += 1
            sem.clear()


def routed_ffn(nc, bank, x, attn, ident, eps, mods, gates, ins):
    with ExitStack() as c:
        sb = lambda n, s, dt=F32: c.enter_context(nc.sbuf_tensor(f"ff_{n}", s, dt))
        norm = Norm(nc, c, "ff", ident, eps, bank[0:2])
        hT = sb("hT", [P, KD, GN])
        stage = sb("stage", [P, GT, D])
        aT = sb("aT", [P, KD, GN])
        wo = sb("wo", [P, KD, D])
        wbase = sb("wbase", [P, KD, 2 * D])
        wexp = sb("wexp", [P, KD, D])
        rw1 = sb("rw1", [P, KD, RHID])
        rw2 = sb("rw2", [RHID, EXPERTS])
        rb1 = sb("rb1", [RHID, 1])
        rows = sb("rows", [1, 2, EXPERTS])
        brow = sb("brow", [1, EXPERTS])
        bias = sb("bias", [1, D])
        ones = sb("ones", [1, P])
        iota = sb("iota", [P, EXPERTS])
        sig = sb("sig", [RHID, GN])
        r1 = sb("r1", [RHID, GN])
        logit = sb("logit", [P, GT, EXPERTS])
        top = sb("top", [P, GT, 8])
        topi = sb("topi", [P, GT, 8], U32)
        topf = sb("topf", [P, GT, 2])
        gap = sb("gap", [P, 2, GT])
        sm = sb("sm", [P, 2, GT])
        coef = sb("coef", [P, 2, GT, EXPERTS])
        wxa = sb("wxa", [P, GT, D])
        wxaT = sb("wxaT", [P, KD, GN])
        upd = sb("upd", [P, GT, D])
        sem = Stage(nc, c, "ff", *LN_SEMS, "load", "stage", "atr", "aT", "y", "x1", "h1", "sig", "r1", "logit",
                    "gap", "sm", "base", "wxa", "wtr", "wxaT", "out")
        loads = (("wo", wo), ("wbase", wbase), ("wexp", wexp), ("rw1", rw1), ("rw2", rw2), ("rb1", rb1),
                 ("rows", rows), ("bias", bias), ("iota", iota))

        with nc.Block() as block:
            @block.sync
            def _(sp):
                for name, dst in loads:
                    sp.dma_start(dst[:], ins[name]).then_inc(sem["load"], 16)

            @block.vector
            def _(v):
                nc.vector.memset(ones[:], 1.0)
                v.wait_ge(sem["load"], 16 * len(loads))
                nc.vector.tensor_tensor(brow[:], rows[:, 0, :], rows[:, 1, :], ALU.add)
        sem.clear()

        with nc.Fori(0, GROUPS) as g:
            with nc.Block() as block:
                @block.scalar
                def _(a):
                    nc.scalar.copy(stage[:], attn[:, bass.ds(g * GT, GT), :]).then_inc(sem["stage"], 1)
                    a.wait_ge(sem["atr"], 1)
                    for k in range(KD):
                        last = nc.scalar.copy(aT[:, k, :], bank[k][:])
                    last.then_inc(sem["aT"], 1)
                    norm.scalar_std(nc, a, sem)
                    norm.modulate(nc, a, None, sem, hT, mods[:, 0, 1, 1, :], mods[:, 0, 1, 0, :])
                    a.wait_ge(sem["h1"], 1)
                    nc.scalar.activation(sig[:], bank[2][0:RHID, :], ACT.Sigmoid, bias=rb1[:]).then_inc(sem["sig"], 1)
                    a.wait_ge(sem["gap"], 1)
                    nc.scalar.activation(sm[:], gap[:], ACT.Sigmoid).then_inc(sem["sm"], 1)
                    a.wait_ge(sem["wtr"], 1)
                    for k in range(KD):
                        last = nc.scalar.copy(wxaT[:, k, :], bank[k][:])
                    last.then_inc(sem["wxaT"], 1)

                @block.tensor
                def _(pe):
                    pe.wait_ge(sem["stage"], 1)
                    for k in range(KD):
                        for t in range(GT):
                            last = nc.tensor.transpose(bank[k][:, t * P:(t + 1) * P],
                                                       stage[:, t, k * P:(k + 1) * P], ident[:])
                    last.then_inc(sem["atr"], 1)
                    pe.wait_ge(sem["aT"], 1)
                    for t in range(GT):
                        for k in range(KD):
                            last = nc.tensor.matmul(bank[4 + t][:, 0:D], aT[:, k, t * P:(t + 1) * P], wo[:, k, :],
                                                    start=(k == 0), stop=(k == KD - 1))
                        last.then_inc(sem["y"], 1)
                    norm.tensor(nc, pe, sem)
                    pe.wait_ge(sem["ln_ha"], 1)
                    pe.wait_ge(sem["ln_hv"], 1)
                    for k in range(KD):
                        last = nc.tensor.matmul(bank[2][0:RHID, :], rw1[:, k, :], hT[:, k, :],
                                                start=(k == 0), stop=(k == KD - 1))
                    last.then_inc(sem["h1"], 1)
                    pe.wait_ge(sem["x1"], GT)
                    for t in range(GT):
                        for k in range(KD):
                            last = nc.tensor.matmul(bank[4 + t][:], hT[:, k, t * P:(t + 1) * P], wbase[:, k, :],
                                                    start=(k == 0), stop=False, skip_group_check=True)
                        last = nc.tensor.matmul(bank[4 + t][:, 0:D], ones[:], bias[:], start=False, stop=False,
                                                skip_group_check=True)
                        last.then_inc(sem["base"], 1)
                    pe.wait_ge(sem["r1"], 1)
                    for t in range(GT):
                        out = bank[3][:, t * EXPERTS:(t + 1) * EXPERTS]
                        nc.tensor.matmul(out, r1[:, t * P:(t + 1) * P], rw2[:], start=True, stop=False)
                        last = nc.tensor.matmul(out, ones[:], brow[:], start=False, stop=True)
                    last.then_inc(sem["logit"], 1)
                    pe.wait_ge(sem["wxa"], GT)
                    for k in range(KD):
                        for t in range(GT):
                            last = nc.tensor.transpose(bank[k][:, t * P:(t + 1) * P],
                                                       wxa[:, t, k * P:(k + 1) * P], ident[:])
                    last.then_inc(sem["wtr"], 1)
                    pe.wait_ge(sem["wxaT"], 1)
                    for t in range(GT):
                        for k in range(KD):
                            last = nc.tensor.matmul(bank[4 + t][:, 0:D], wxaT[:, k, t * P:(t + 1) * P], wexp[:, k, :],
                                                    start=False, stop=(k == KD - 1), skip_group_check=True)
                        last.then_inc(sem["out"], 1)

                @block.vector
                def _(v):
                    chain = Chain(v, sem["vec"])
                    x4 = x[:, bass.ds(g * GT, GT), :]
                    for t in range(GT):
                        v.wait_ge(sem["y"], t + 1)
                        nc.vector.tensor_tensor(upd[:, t, :], bank[4 + t][:, 0:D], gates[:, 0, 0, :],
                                                ALU.mult).then_inc(sem["x1"], 1)
                    v.wait_ge(sem["x1"], GT)
                    chain.link(nc.vector.tensor_tensor(x4, x4, upd[:], ALU.add))
                    norm.vector(nc, v, chain, sem, x4)
                    norm.modulate(nc, None, v, sem, hT, mods[:, 0, 1, 1, :], mods[:, 0, 1, 0, :])
                    v.wait_ge(sem["sig"], 1)
                    nc.vector.scalar_tensor_tensor(r1[:], bank[2][0:RHID, :], rb1[:, 0:1], sig[:], ALU.add,
                                                   ALU.mult).then_inc(sem["r1"], 1)
                    v.wait_ge(sem["logit"], 1)
                    lg = bank[3][:, 0:GT * EXPERTS].rearrange("p (t e) -> p t e", t=GT)
                    chain.link(nc.vector.tensor_copy(logit[:], lg))
                    for t in range(GT):
                        chain.did(nc.vector.max(top[:, t, :], logit[:, t, :]))
                    chain.settle()
                    for t in range(GT):
                        chain.did(nc.vector.max_index(topi[:, t, :], top[:, t, :], logit[:, t, :]))
                    nc.vector.tensor_tensor(gap[:, 0, :], top[:, :, 0], top[:, :, 1], ALU.subtract)
                    nc.vector.tensor_tensor(gap[:, 1, :], top[:, :, 1], top[:, :, 0],
                                            ALU.subtract).then_inc(sem["gap"], 1)
                    chain.settle()
                    chain.link(nc.vector.tensor_copy(topf[:], topi[:, :, 0:2]))
                    v.wait_ge(sem["sm"], 1)
                    for t in range(GT):
                        for n in range(2):
                            chain.did(nc.vector.tensor_scalar(coef[:, n, t, :], iota[:], topf[:, t, n:n + 1],
                                                              sm[:, n, t:t + 1], ALU.is_equal, ALU.mult))
                    chain.settle()
                    chain.link(nc.vector.tensor_tensor(coef[:, 0], coef[:, 0], coef[:, 1], ALU.add))
                    for t in range(GT):
                        v.wait_ge(sem["base"], t + 1)
                        xa = bank[4 + t][:, D:2 * D].rearrange("p (e r) -> p e r", e=EXPERTS)
                        nc.vector.tensor_tensor(wxa[:, t, :].rearrange("p (e r) -> p e r", e=EXPERTS), xa,
                                                coef[:, 0, t, :].unsqueeze(2).to_broadcast([P, EXPERTS, D // EXPERTS]),
                                                ALU.mult).then_inc(sem["wxa"], 1)
                    for t in range(GT):
                        v.wait_ge(sem["out"], t + 1)
                        chain.did(nc.vector.tensor_tensor(upd[:, t, :], bank[4 + t][:, 0:D], gates[:, 0, 1, :],
                                                          ALU.mult))
                    chain.settle()
                    nc.vector.tensor_tensor(x4, x4, upd[:], ALU.add)
            sem.clear()


def decay_front(nc, bank, x, hT, ident, eps, mods, x_dram):
    with ExitStack() as c:
        norm = Norm(nc, c, "df", ident, eps, bank[0:2])
        h = c.enter_context(nc.sbuf_tensor("df_h", [P, KD, GN], F32))
        sem = Stage(nc, c, "df", *LN_SEMS, "save")
        with nc.Fori(0, GROUPS) as g:
            hi, lo = (part[:, :, bass.ds(g * GN, GN)] for part in hT)
            with nc.Block() as block:
                @block.vector
                def _(v):
                    norm.vector(nc, v, Chain(v, sem["vec"]), sem, x[:, bass.ds(g * GT, GT), :])
                    norm.modulate(nc, None, v, sem, h, mods[:, 1, 0, 1, :], mods[:, 1, 0, 0, :])
                    norm.split(nc, None, v, sem, h, hi, lo)

                @block.scalar
                def _(a):
                    norm.scalar_std(nc, a, sem)
                    norm.modulate(nc, a, None, sem, h, mods[:, 1, 0, 1, :], mods[:, 1, 0, 0, :])
                    norm.split(nc, a, None, sem, h, hi, lo)

                @block.tensor
                def _(pe):
                    norm.tensor(nc, pe, sem)

                @block.sync
                def _(sp):
                    sp.dma_start(x_dram[:, bass.ds(g * GT, GT), :], x[:, bass.ds(g * GT, GT), :])\
                      .then_inc(sem["save"], 16)
                    sp.wait_ge(sem["save"], 16)
            sem.clear()


def decay_attention(nc, bank, x, hT, mods, ident, gates, x_dram, ins):
    with ExitStack() as c:
        sb = lambda n, s, dt=F32: c.enter_context(nc.sbuf_tensor(f"da_{n}", s, dt))
        yacc = x
        raw = sb("raw", [P, KD, 8 * D1])
        w = [sb("wh", [P, KD, 8 * D1], F32R), sb("wl", [P, KD, 8 * D1], F32R)]
        wo_raw = sb("wo_raw", [P, 2, D])
        wo = [sb("woh", [P, 2, D], F32R), sb("wol", [P, 2, D], F32R)]
        nw = sb("nw", [P, H1])
        slope = sb("slope", [P, H1])
        steps = sb("steps", [P, 4, P])
        dmask = sb("dmask", [P, 2, P])
        qdec = sb("qdec", [P, 2, P])
        kbdec = sb("kbdec", [P, 2, 2])
        small = sb("small", [P, 2, 2])
        qT = sb("qT", [P, S])
        kT = sb("kT", [P, S])
        gT = sb("gT", [P, 2, GN])
        v = sb("v", [P, TILES, 2 * D1])
        ktok = sb("ktok", [P, TILES, D1])
        qd = sb("qd", [P, S])
        state = sb("state", [P, TILES, D1])
        smask = sb("smask", [P, 2, GT, P])
        oT = sb("oT", [P, 2, GN])
        sq = sb("sq", [P, 2, GN])
        og = sb("og", [P, 2, GN])
        ogs = [sb("ogh", [P, 2, S], F32R), sb("ogl", [P, 2, S], F32R)]
        ssum = sb("ssum", [P, S])
        ones = sb("ones", [P, 1])
        rms = sb("rms", [P, 2, TILES])
        reps = sb("reps", [P, 1])
        sem = Stage(nc, c, "da", "load", "next", "small", "sneg", "dec", "vec", "proj", "evac", "ktr",
                    "ktok", "qd", "dl", "st", "sc", "sm", "o", "oT", "sq", "ssum", "g", "og", "ogh", "ogl", "y", "yadd",
                    "ss", "rstd", "wh", "wl", "woh", "wol")
        PROJ, KTR, SC, DL, OB, YB = bank[0:2], bank[2], bank[3], bank[4], bank[5], bank[6:8]

        columns = {"v": slice(6 * D1, 8 * D1), "qk": slice(0, 4 * D1), "g": slice(4 * D1, 6 * D1)}

        def split_weights(kind, a=None, gp=None, ve=None):
            at = columns[kind]
            if a is not None:
                nc.scalar.copy(w[0][:, :, at], raw[:, :, at]).then_inc(sem["wh"], 1)
            if gp is not None:
                gp.wait_ge(sem["wh"], list(columns).index(kind) + 1)
                nc.gpsimd.tensor_tensor(w[1][:, :, at], raw[:, :, at], w[0][:, :, at].bitcast(F32),
                                        ALU.subtract).then_inc(sem["wl"], 1)
            if ve is not None:
                ve.wait_ge(sem["wh"], list(columns).index(kind) + 1)
                nc.vector.tensor_tensor(w[1][:, :, at], raw[:, :, at], w[0][:, :, at].bitcast(F32),
                                        ALU.subtract).then_inc(sem["wl"], 1)

        def add_squares(n, eng, ops):
            at = slice(n % GROUPS * GN, (n % GROUPS + 1) * GN)
            eng.wait_ge(sem["sq"], n + 1)
            ops.tensor_tensor(ssum[:, at], ssum[:, at], sq[:, n % 2, :], ALU.add).then_inc(sem["ssum"], 1)

        def load_pair(sp, pair, done):
            sp.dma_start(raw[:], ins["wpair"][bass.ds(pair, 1)].rearrange("o p k n -> (o p) k n")).then_inc(done, 16)

        with nc.Block() as block:
            @block.sync
            def _(sp):
                sp.dma_start(nw[:], ins["nw"]).then_inc(sem["load"], 16)
                sp.dma_start(slope[:], ins["slope"]).then_inc(sem["load"], 16)
                sp.dma_start(steps[:], ins["steps"]).then_inc(sem["load"], 16)
                load_pair(sp, 0, sem["next"])
                sp.wait_ge(sem["load"], 48)

            @block.vector
            def _(ve):
                nc.vector.memset(yacc[:], 0.0)
                nc.vector.memset(state[:, 0, :], 0.0)
                nc.vector.memset(ones[:], 1.0)
                nc.vector.memset(reps[:], RMS_EPS)
                for part in (*wo, *ogs):
                    nc.vector.memset(part[:].bitcast(F32), 0.0)

            @block.scalar
            def _(a):
                a.wait_ge(sem["next"], 16)
                for kind in columns:
                    split_weights(kind, a=a)

            @block.gpsimd
            def _(gp):
                nc.gpsimd.memset(ssum[:], 0.0)
                for kind in columns:
                    split_weights(kind, gp=gp)
        sem.clear()

        def wide(kind, h):
            return [(kind, h, j) for j in range(GROUPS)]

        values = [("v", 0, t) for t in range(0, TILES, 2)]
        items = wide("k", 0) + wide("q", 0) + values + wide("g", 0) + wide("k", 1) + wide("q", 1) + wide("g", 1)
        nth = {item: i for i, item in enumerate(items)}
        column = {"q": 0, "k": 2, "g": 4}

        def share(pe):
            for i in range(TILES // 2):
                if i >= 2:
                    pe.wait_ge(sem["yadd"], i - 1)
                for t in (2 * i, 2 * i + 1):
                    for h in range(2):
                        last = product(nc, YB[i % 2][:, (t % 2) * D:(t % 2 + 1) * D],
                                       [part[:, h, t * P:(t + 1) * P] for part in ogs],
                                       [part[:, h, :] for part in wo], h == 0, h == 1)
                last.then_inc(sem["y"], 1)
                yield

        def add_share(ve, i):
            ve.wait_ge(sem["y"], i + 1)
            at = yacc[:, 2 * i:2 * i + 2, :].rearrange("p t n -> p (t n)")
            nc.vector.tensor_tensor(at, at, YB[i % 2][:], ALU.add).then_inc(sem["yadd"], 1)

        with nc.Fori(0, PAIRS) as pr:
            with nc.Block() as block:
                @block.sync
                def _(sp):
                    load_pair(sp, (pr + 1) % PAIRS, sem["next"])
                    sp.dma_start(wo_raw[:], ins["wo1"][bass.ds(pr, 1)].rearrange("o p k n -> (o p) k n"))\
                      .then_inc(sem["load"], 16)
                    sp.wait_ge(sem["next"], 16)

                @block.scalar
                def _(a):
                    a.wait_ge(sem["sneg"], 1)
                    for h in range(2):
                        s = small[:, h, 0:1]
                        nc.scalar.activation(dmask[:, h, :], steps[:, 0, :], ACT.Exp, scale=s)
                        nc.scalar.activation(qdec[:, h, :], steps[:, 2, :], ACT.Exp, scale=s)
                        last = nc.scalar.activation(kbdec[:, h, :], steps[:, 3, 0:2], ACT.Exp, scale=s)
                    last.then_inc(sem["dec"], 1)

                    def drain(some):
                        for item in some:
                            kind, h, j = item
                            i = nth[item]
                            if item == ("k", 1, 0):
                                a.wait_ge(sem["ktr"], GROUPS)
                                a.wait_ge(sem["sc"], GROUPS)
                            if item == ("q", 1, 0):
                                a.wait_ge(sem["qd"], GROUPS)
                            n = h * GROUPS + j
                            if kind == "g" and n >= 2:
                                a.wait_ge(sem["og"], n - 1)
                            a.wait_ge(sem["proj"], i + 1)
                            src = PROJ[i % 2][:]
                            if kind == "v":
                                dst = v[:, j:j + 2, :].rearrange("p t n -> p (t n)")
                            else:
                                at = slice(j * GN, (j + 1) * GN)
                                dst = {"q": qT[:, at], "k": kT[:, at], "g": gT[:, n % 2, :]}[kind]
                            f, scale = (ACT.Tanh, 0.5) if kind == "g" else (ACT.Silu, 1.0)
                            nc.scalar.activation(dst, src, f, scale=scale).then_inc(sem["evac"], 1)

                    def head(h):
                        for j in range(GROUPS + 2):
                            if j < GROUPS:
                                drain([("g", h, j)])
                            if 1 <= j <= GROUPS:
                                n = h * GROUPS + j - 1
                                a.wait_ge(sem["o"], n + 1)
                                if n >= 2:
                                    a.wait_ge(sem["og"], n - 1)
                                nc.scalar.copy(oT[:, n % 2, :], OB[:]).then_inc(sem["oT"], 1)
                                if n >= 2:
                                    a.wait_ge(sem["ssum"], n - 1)
                                a.wait_ge(sem["oT"], n + 1)
                                nc.scalar.activation(sq[:, n % 2, :], oT[:, n % 2, :], ACT.Square).then_inc(sem["sq"], 1)
                            if h and j == GROUPS:
                                split_weights("g", a=a)
                            if j >= 2:
                                n = h * GROUPS + j - 2
                                a.wait_ge(sem["og"], n + 1)
                                if n == 0:
                                    a.wait_ge(sem["y"], TILES // 2)
                                nc.scalar.copy(ogs[0][:, h, (j - 2) * GN:(j - 1) * GN],
                                               og[:, n % 2, :]).then_inc(sem["ogh"], 1)

                    drain(wide("k", 0) + wide("q", 0) + values)
                    a.wait_ge(sem["next"], 16)
                    split_weights("v", a=a)
                    head(0)
                    drain(wide("k", 1) + wide("q", 1))
                    split_weights("qk", a=a)
                    a.wait_ge(sem["load"], 16)
                    nc.scalar.copy(wo[0][:], wo_raw[:]).then_inc(sem["woh"], 1)
                    head(1)

                @block.tensor
                def _(pe):
                    def project(item):
                        kind, h, j = item
                        i = nth[item]
                        if i >= 2:
                            pe.wait_ge(sem["evac"], i - 1)
                        out = PROJ[i % 2]
                        if kind == "v":
                            for t in range(2):
                                for k in range(KD):
                                    last = product(nc, out[:, t * 2 * D1:(t + 1) * 2 * D1],
                                                   [part[:, k, (j + t) * P:(j + t + 1) * P] for part in hT],
                                                   [part[:, k, 6 * D1:8 * D1] for part in w], k == 0, k == KD - 1)
                        else:
                            at = (column[kind] + h) * D1
                            for k in range(KD):
                                last = product(nc, out[:], [part[:, k, at:at + D1] for part in w],
                                               [part[:, k, j * GN:(j + 1) * GN] for part in hT], k == 0, k == KD - 1)
                        last.then_inc(sem["proj"], 1)

                    def turn_keys(h, j):
                        n = h * GROUPS + j
                        pe.wait_ge(sem["evac"], nth[("k", h, j)] + 1)
                        if n:
                            pe.wait_ge(sem["ktok"], n)
                        for t in range(GT):
                            b = j * GT + t
                            last = nc.tensor.transpose(KTR[:, t * P:(t + 1) * P], kT[:, b * P:(b + 1) * P], ident[:])
                        last.then_inc(sem["ktr"], 1)

                    def block_scores(h, j):
                        n = h * GROUPS + j
                        pe.wait_ge(sem["evac"], nth[("q", h, j)] + 1)
                        if n:
                            pe.wait_ge(sem["sm"], n)
                        for t in range(GT):
                            b = j * GT + t
                            last = nc.tensor.matmul(SC[:, t * P:(t + 1) * P], kT[:, b * P:(b + 1) * P],
                                                    qT[:, b * P:(b + 1) * P], start=True, stop=True)
                        last.then_inc(sem["sc"], 1)

                    def deltas(h, j):
                        n = h * GROUPS + j
                        pe.wait_ge(sem["ktok"], n + 1)
                        pe.wait_ge(sem["evac"], nth[values[-1]] + 1)
                        if n:
                            pe.wait_ge(sem["st"], h * (TILES - 1) + j * GT)
                        for b in range(j * GT, min(j * GT + GT, TILES - 1)):
                            t = b % GT
                            last = nc.tensor.matmul(DL[:, t * P:(t + 1) * P], ktok[:, b, :],
                                                    v[:, b, h * D1:(h + 1) * D1], start=True, stop=True)
                        last.then_inc(sem["dl"], 1)

                    def attend(h, j):
                        n = h * GROUPS + j
                        pe.wait_ge(sem["sm"], n + 1)
                        pe.wait_ge(sem["st"], h * (TILES - 1) + j * GT + GT - 1)
                        pe.wait_ge(sem["qd"], n + 1)
                        if n:
                            pe.wait_ge(sem["oT"], n)
                        for t in range(GT):
                            b = j * GT + t
                            out = OB[:, t * P:(t + 1) * P]
                            last = nc.tensor.matmul(out, v[:, b, h * D1:(h + 1) * D1], smask[:, n % 2, t, :],
                                                    start=True, stop=(b == 0))
                            if b:
                                last = nc.tensor.matmul(out, state[:, b, :], qd[:, b * P:(b + 1) * P],
                                                        start=False, stop=True)
                        last.then_inc(sem["o"], 1)

                    def head(h):
                        for j in range(GROUPS + 1):
                            if j < GROUPS:
                                deltas(h, j)
                                block_scores(h, j)
                                project(("g", h, j))
                            if j:
                                attend(h, j - 1)

                    before = share(pe)
                    for item in wide("k", 0) + wide("q", 0):
                        project(item)
                        next(before)
                    for i, item in enumerate(values):
                        project(item)
                        if i % 2:
                            turn_keys(0, i // 2)
                    head(0)
                    for item in wide("k", 1):
                        project(item)
                    for j, item in enumerate(wide("q", 1)):
                        project(item)
                        turn_keys(1, j)
                    head(1)

                @block.gpsimd
                def _(gp):
                    nc.gpsimd.tensor_copy(small[:, :, 0], slope[:, bass.ds(pr * 2, 2)])
                    nc.gpsimd.tensor_copy(small[:, :, 1], nw[:, bass.ds(pr * 2, 2)]).then_inc(sem["small"], 1)

                    def decay_queries(h):
                        gp.wait_ge(sem["dec"], 1)
                        for j in range(GROUPS):
                            gp.wait_ge(sem["evac"], nth[("q", h, j)] + 1)
                            if h:
                                gp.wait_ge(sem["o"], j + 1)
                            at = slice(j * GN, (j + 1) * GN)
                            nc.gpsimd.tensor_tensor(qd[:, at].rearrange("p (b m) -> p b m", m=P),
                                                    qT[:, at].rearrange("p (b m) -> p b m", m=P),
                                                    qdec[:, h, :].unsqueeze(1).to_broadcast([P, GT, P]),
                                                    ALU.mult).then_inc(sem["qd"], 1)

                    def outs(h):
                        for j in range(GROUPS):
                            n = h * GROUPS + j
                            at = slice(j * GN, (j + 1) * GN)
                            if n < 2 * GROUPS - 1:
                                if n >= GROUPS:
                                    gp.wait_ge(sem["ssum"], n - GROUPS + 1)
                                add_squares(n, gp, nc.gpsimd)
                            gp.wait_ge(sem["ogh"], n + 1)
                            nc.gpsimd.tensor_tensor(ogs[1][:, h, at], og[:, n % 2, :], ogs[0][:, h, at].bitcast(F32),
                                                    ALU.subtract).then_inc(sem["ogl"], 1)

                    decay_queries(0)
                    split_weights("v", gp=gp)
                    outs(0)
                    decay_queries(1)
                    split_weights("qk", gp=gp)
                    gp.wait_ge(sem["woh"], 1)
                    gp.wait_ge(sem["y"], TILES // 2)
                    nc.gpsimd.tensor_tensor(wo[1][:], wo_raw[:], wo[0][:].bitcast(F32),
                                            ALU.subtract).then_inc(sem["wol"], 1)
                    outs(1)

                @block.vector
                def _(ve):
                    chain = Chain(ve, sem["vec"])
                    ve.wait_ge(sem["small"], 1)
                    chain.did(nc.vector.tensor_scalar(small[:, :, 1], small[:, :, 1], 0.5, None, ALU.mult))
                    nc.vector.tensor_scalar(small[:, :, 0], small[:, :, 0], -1.0, None, ALU.mult).then_inc(sem["sneg"], 1)
                    ve.wait_ge(sem["dec"], 1)
                    chain.link(nc.vector.tensor_tensor(dmask[:], dmask[:],
                                                       steps[:, 1:2, :].to_broadcast([P, 2, P]), ALU.mult))

                    def take_keys(h):
                        for j in range(GROUPS):
                            n = h * GROUPS + j
                            ve.wait_ge(sem["ktr"], n + 1)
                            if h and j == 0:
                                ve.wait_ge(sem["dl"], GROUPS)
                            nc.vector.tensor_scalar(ktok[:, j * GT:(j + 1) * GT, :].rearrange("p t d -> p (t d)"),
                                                    KTR[:], kbdec[:, h, 1:2], None, ALU.mult).then_inc(sem["ktok"], 1)

                    def states(h, j):
                        ve.wait_ge(sem["dl"], h * GROUPS + j + 1)
                        if h and j == 0:
                            ve.wait_ge(sem["o"], GROUPS)
                        for b in range(j * GT, min(j * GT + GT, TILES - 1)):
                            if b:
                                ve.wait_ge(sem["st"], h * (TILES - 1) + b)
                            nc.vector.scalar_tensor_tensor(state[:, b + 1, :], state[:, b, :], kbdec[:, h, 0:1],
                                                           DL[:, (b % GT) * P:(b % GT + 1) * P], ALU.mult,
                                                           ALU.add).then_inc(sem["st"], 1)

                    def mask_scores(h, j):
                        n = h * GROUPS + j
                        ve.wait_ge(sem["sc"], n + 1)
                        if n >= 2:
                            ve.wait_ge(sem["o"], n - 1)
                        nc.vector.tensor_tensor(smask[:, n % 2], SC[:].rearrange("p (t m) -> p t m", t=GT),
                                                dmask[:, h, :].unsqueeze(1).to_broadcast([P, GT, P]),
                                                ALU.mult).then_inc(sem["sm"], 1)

                    def weigh_gate(h, j):
                        n = h * GROUPS + j
                        ve.wait_ge(sem["evac"], nth[("g", h, j)] + 1)
                        at = gT[:, n % 2, :]
                        nc.vector.tensor_scalar(at, at, 1.0, small[:, h, 1:2], ALU.add, ALU.mult).then_inc(sem["g"], 1)

                    def gate(h, j):
                        n = h * GROUPS + j
                        ve.wait_ge(sem["g"], n + 1)
                        ve.wait_ge(sem["oT"], n + 1)
                        if n >= 2:
                            ve.wait_ge(sem["ogl"], n - 1)
                        nc.vector.tensor_tensor(og[:, n % 2, :], oT[:, n % 2, :], gT[:, n % 2, :],
                                                ALU.mult).then_inc(sem["og"], 1)

                    for i in range(TILES // 2):
                        add_share(ve, i)
                    for h in range(2):
                        take_keys(h)
                        for j in range(GROUPS + 1):
                            if j < GROUPS:
                                states(h, j)
                                mask_scores(h, j)
                                weigh_gate(h, j)
                            if j:
                                gate(h, j - 1)
                    split_weights("g", ve=ve)
                    ve.wait_ge(sem["ssum"], 2 * GROUPS - 1)
                    add_squares(2 * GROUPS - 1, ve, nc.vector)
            sem.clear()

        with nc.Block() as block:
            @block.tensor
            def _(pe):
                for t in range(TILES):
                    last = nc.tensor.matmul(bank[0][:, t:t + 1], ssum[:, t * P:(t + 1) * P], ones[:], start=True, stop=True)
                last.then_inc(sem["ss"], 1)
                for _ in share(pe):
                    pass

            @block.sync
            def _(sp):
                sp.dma_start(v[:], x_dram).then_inc(sem["load"], 16)

            @block.scalar
            def _(a):
                a.wait_ge(sem["ss"], 1)
                nc.scalar.activation(rms[:, 0, :], bank[0][:, 0:TILES], ACT.Sqrt, bias=reps[:],
                                     scale=1.0 / F1).then_inc(sem["rstd"], 1)

            @block.vector
            def _(ve):
                chain = Chain(ve, sem["vec"])
                ve.wait_ge(sem["rstd"], 1)
                chain.link(nc.vector.reciprocal(rms[:, 1, :], rms[:, 0, :]))
                for i in range(TILES // 2):
                    add_share(ve, i)
                    ve.wait_ge(sem["yadd"], i + 1)
                    for t in (2 * i, 2 * i + 1):
                        chain.did(nc.vector.scalar_tensor_tensor(yacc[:, t, :], yacc[:, t, :], rms[:, 1, t:t + 1],
                                                                 gates[:, 1, 0, :], ALU.mult, ALU.mult))
                chain.settle()
                ve.wait_ge(sem["load"], 16)
                nc.vector.tensor_tensor(x[:], yacc[:], v[:], ALU.add)
        sem.clear()


def ternary_ffn(nc, bank, x, ident, eps, mods, gates, ins, out):
    with ExitStack() as c:
        sb = lambda n, s, dt=F32: c.enter_context(nc.sbuf_tensor(f"tf_{n}", s, dt))
        norm = Norm(nc, c, "tf", ident, eps, bank[0:2])
        h = sb("h", [P, KD, GN])
        hT = [sb("hh", [P, KD, S], F32R), sb("hl", [P, KD, S], F32R)]
        raw = sb("raw", [P, 3, KD * DE])
        low = sb("low", [P, 3, KD * DE])
        tern = sb("tern", [P, 3, KD * DE], F32R)
        asum = sb("asum", [P, 3])
        ones = sb("ones", [P, P])
        scale = sb("scale", [P, 3])
        half = sb("half", [P, 2, 3])
        hid = sb("hid", [P, 2, GN])
        hids = [sb("hidh", [P, KE, GN], F32R), sb("hidl", [P, KE, GN], F32R)]
        act = sb("act", [P, 2, GN])
        upd = sb("upd", [P, GT, D])
        sem = Stage(nc, c, "tf", *LN_SEMS, "load", "load2", "load3", "abs", "sum", "half", "low", "up", "gate", "silu",
                    "hid", "hidh", "hidl", "down", "store", "xdone")
        wu = tern[:, 0, :].rearrange("p (k n) -> p k n", k=KD)
        wg = tern[:, 1, :].rearrange("p (k n) -> p k n", k=KD)
        wd = tern[:, 2, :].rearrange("p (k n) -> p k n", k=KE)
        loaded = ("load", "load2", "load3")
        rows = lambda g: x[:, bass.ds(g * GT, GT), :]
        parts = lambda g: [part[:, :, bass.ds(g * GN, GN)] for part in hT]
        factor, shift = mods[:, 1, 1, 1, :], mods[:, 1, 1, 0, :]

        with nc.Block() as block:
            @block.sync
            def _(sp):
                for i, name in enumerate(("wup", "wgate", "wdown")):
                    sp.dma_start(raw[:, i, :], ins[name]).then_inc(sem[loaded[i]], 16)

            @block.scalar
            def _(a):
                norm.scalar_std(nc, a, sem)
                norm.modulate(nc, a, None, sem, h, factor, shift)
                norm.split(nc, a, None, sem, h, *parts(0))

            @block.vector
            def _(v):
                chain = Chain(v, sem["vec"])
                nc.vector.memset(ones[:], 1.0)
                norm.vector(nc, v, chain, sem, rows(0))
                for i in range(3):
                    v.wait_ge(sem[loaded[i]], 16)
                    nc.vector.tensor_reduce(asum[:, i:i + 1], raw[:, i, :], AX.X, ALU.add,
                                            apply_absolute_value=True).then_inc(sem["abs"], 1)
                    if i == 0:
                        norm.modulate(nc, None, v, sem, h, factor, shift)
                norm.split(nc, None, v, sem, h, *parts(0))
                v.wait_ge(sem["sum"], 1)
                chain.link(nc.vector.tensor_scalar(scale[:], bank[2][:, 0:3], 1.0 / (D * DE), 1e-8, ALU.mult, ALU.add))
                nc.vector.tensor_scalar(half[:, 0, :], scale[:], 0.5, None, ALU.mult).then_inc(sem["half"], 1)
                nc.vector.tensor_scalar(half[:, 1, :], scale[:], -0.5, None, ALU.mult).then_inc(sem["half"], 1)
                v.wait_ge(sem["half"], 2)
                for i in range(2):
                    chain.link(nc.vector.tensor_scalar(low[:, i, :], raw[:, i, :], half[:, 1, i:i + 1], None, ALU.is_lt))
                    nc.vector.scalar_tensor_tensor(tern[:, i, :], raw[:, i, :], half[:, 0, i:i + 1], low[:, i, :],
                                                   ALU.is_gt, ALU.subtract)
                v.wait_ge(sem["low"], 1)
                nc.vector.scalar_tensor_tensor(tern[:, 2, :], raw[:, 2, :], half[:, 0, 2:3], low[:, 2, :],
                                               ALU.is_gt, ALU.subtract)

            @block.gpsimd
            def _(gp):
                gp.wait_ge(sem["half"], 2)
                gp.wait_ge(sem["load3"], 16)
                nc.gpsimd.tensor_scalar(low[:, 2, :], raw[:, 2, :], half[:, 1, 2:3], None, ALU.is_lt)\
                  .then_inc(sem["low"], 1)

            @block.tensor
            def _(pe):
                norm.tensor(nc, pe, sem)
                pe.wait_ge(sem["abs"], 3)
                nc.tensor.matmul(bank[2][:, 0:3], ones[:], asum[:], start=True, stop=True).then_inc(sem["sum"], 1)
        sem.clear()

        def finish(v, chain, g):
            for i in range(GT // 2):
                y = bank[6 + i][:].rearrange("p (t n) -> p t n", t=2)
                chain.did(nc.vector.scalar_tensor_tensor(
                    upd[:, 2 * i:2 * i + 2, :], y, scale[:, 2:3],
                    gates[:, 1, 1:2, :].to_broadcast([P, 2, D]), ALU.mult, ALU.mult))
            chain.settle()
            nc.vector.tensor_tensor(rows(g), rows(g), upd[:], ALU.add).then_inc(sem["xdone"], 1)

        def store(sp, g):
            sp.wait_ge(sem["xdone"], 1)
            sp.dma_start(out[:, bass.ds(g * GT, GT), :], rows(g)).then_inc(sem["store"], 16)
            sp.wait_ge(sem["store"], 16)

        def turn(g, first=False, last=False):
            with nc.Block() as block:
                @block.tensor
                def _(pe):
                    high, low_ = parts(g)
                    for e in range(KE):
                        for w, banks, done, used in ((wu, bank[2:4], "up", "silu"), (wg, bank[4:6], "gate", "hid")):
                            if e >= 2:
                                pe.wait_ge(sem[used], e - 1)
                            for k in range(KD):
                                nc.tensor.matmul(banks[e % 2][:], w[:, k, e * P:(e + 1) * P], high[:, k, :],
                                                 start=(k == 0), stop=False)
                                mm = nc.tensor.matmul(banks[e % 2][:], w[:, k, e * P:(e + 1) * P], low_[:, k, :],
                                                      start=False, stop=(k == KD - 1))
                            mm.then_inc(sem[done], 1)
                        if e == 4 and not last:
                            norm.tensor(nc, pe, sem)
                    if not first:
                        pe.wait_ge(sem["xdone"], 1)
                    for t in range(GT):
                        at = bank[6 + t // 2][:, (t % 2) * D:(t % 2 + 1) * D]
                        for e in range(KE):
                            if t == 0:
                                pe.wait_ge(sem["hidh"], e + 1)
                                pe.wait_ge(sem["hidl"], e + 1)
                            for part in hids:
                                mm = nc.tensor.matmul(at, part[:, e, t * P:(t + 1) * P], wd[:, e, :],
                                                      start=(e == 0 and part is hids[0]),
                                                      stop=(e == KE - 1 and part is hids[1]))
                    mm.then_inc(sem["down"], 1)

                @block.scalar
                def _(a):
                    for e in range(KE + 1):
                        if e < KE:
                            a.wait_ge(sem["up"], e + 1)
                            if e >= 2:
                                a.wait_ge(sem["hid"], e - 1)
                            nc.scalar.activation(act[:, e % 2, :], bank[2 + e % 2][:], ACT.Silu,
                                                 scale=scale[:, 0:1]).then_inc(sem["silu"], 1)
                        if e:
                            a.wait_ge(sem["hid"], e)
                            nc.scalar.copy(hids[0][:, e - 1, :], hid[:, (e - 1) % 2, :]).then_inc(sem["hidh"], 1)
                        if e == 1 and not last:
                            norm.scalar_std(nc, a, sem)
                        if e == 5 and not last:
                            norm.modulate(nc, a, None, sem, h, factor, shift)
                        if e == 6 and not last:
                            norm.split(nc, a, None, sem, h, *parts(g + 1))

                @block.gpsimd
                def _(gp):
                    for e in range(KE):
                        gp.wait_ge(sem["hidh"], e + 1)
                        nc.gpsimd.tensor_tensor(hids[1][:, e, :], hid[:, e % 2, :], hids[0][:, e, :].bitcast(F32),
                                                ALU.subtract).then_inc(sem["hidl"], 1)

                @block.vector
                def _(v):
                    chain = Chain(v, sem["vec"])
                    for e in range(KE):
                        v.wait_ge(sem["silu"], e + 1)
                        v.wait_ge(sem["gate"], e + 1)
                        if e >= 2:
                            v.wait_ge(sem["hidl"], e - 1)
                        nc.vector.scalar_tensor_tensor(hid[:, e % 2, :], bank[4 + e % 2][:], scale[:, 1:2],
                                                       act[:, e % 2, :], ALU.mult, ALU.mult).then_inc(sem["hid"], 1)
                        if e == 0 and not last:
                            norm.moments(nc, v, chain, sem, rows(g + 1))
                        if e == 1 and not last:
                            norm.normalize(nc, v, chain, sem, rows(g + 1))
                        if e == 2 and not first:
                            finish(v, chain, g - 1)
                        if e == 5 and not last:
                            norm.modulate(nc, None, v, sem, h, factor, shift)
                    if not last:
                        norm.split(nc, None, v, sem, h, *parts(g + 1))

                if not first:
                    @block.sync
                    def _(sp):
                        store(sp, g - 1)
            sem.clear()

        turn(0, first=True)
        with nc.Fori(1, GROUPS - 1) as g:
            turn(g)
        turn(GROUPS - 1, last=True)
        with nc.Block() as block:
            @block.vector
            def _(v):
                finish(v, Chain(v, sem["vec"]), GROUPS - 1)

            @block.sync
            def _(sp):
                store(sp, GROUPS - 1)
        sem.clear()


class Banks:

    def __init__(self, whole):
        self.whole = whole
        self.each = [whole[:, i, :] for i in range(8)]

    def __getitem__(self, i):
        return self.each[i]


def build(nc, ins, out, upto=99):
    parts_dram = nc.dram_tensor("qk_parts", [2, 3, D, S], BF16, kind="Internal").ap()
    x_dram = nc.dram_tensor("x_saved", [P, TILES, D], F32, kind="Internal").ap()
    with ExitStack() as ctx:
        sb = lambda n, s, dt=F32: ctx.enter_context(nc.sbuf_tensor(n, s, dt))
        bank = Banks(ctx.enter_context(nc.psum_tensor("psum", [P, 8, 512], F32)))
        x = sb("x", [P, TILES, D])
        ident = sb("ident", [P, P])
        eps = sb("eps", [P, 1])
        mods = sb("mods", [P, 2, 2, 2, KD])
        gates = sb("gates", [P, 2, 2, D])
        sem = Stage(nc, ctx, "top", "load")
        with nc.Block() as block:
            @block.sync
            def _(sp):
                sp.dma_start(x[:], ins["x"]).then_inc(sem["load"], 16)
                sp.dma_start(ident[:], ins["ident"]).then_inc(sem["load"], 16)
                sp.wait_ge(sem["load"], 32)

            @block.vector
            def _(v):
                nc.vector.memset(eps[:], LN_EPS)
        modulation(nc, ctx, bank, mods, gates, ins)
        with ExitStack() as c0:
            attn = c0.enter_context(nc.sbuf_tensor("attn", [P, TILES, D], F32))
            with nc.sbuf_tensor("v_all", [P, TILES, D], F32) as v_all:
                rope_front(nc, bank, x, v_all, ident, eps, mods, parts_dram, ins)
                rope_attention(nc, bank, v_all, attn, ident, parts_dram, ins)
            routed_ffn(nc, bank, x, attn, ident, eps, mods, gates, ins)
        with nc.sbuf_tensor("h1h", [P, KD, S], F32R) as high, nc.sbuf_tensor("h1l", [P, KD, S], F32R) as low:
            decay_front(nc, bank, x, (high, low), ident, eps, mods, x_dram)
            decay_attention(nc, bank, x, (high, low), mods, ident, gates, x_dram, ins)
        ternary_ffn(nc, bank, x, ident, eps, mods, gates, ins, out)


def lay_out(i, np):
    kp = lambda a: np.ascontiguousarray(a.reshape(-1, P, a.shape[-1]).transpose(1, 0, 2))
    o = {}
    o["x"] = i["L0_attn_x"].reshape(TILES, P, D).transpose(1, 0, 2)
    o["ident"] = np.eye(P, dtype=np.float32)
    for l in range(2):
        o[f"c{l}"] = i[f"L{l}_c"].reshape(KD, P).T
        o[f"wmod{l}"] = kp(i[f"L{l}_wmod"])
    o["wqk"] = kp(np.concatenate([i["L0_attn_wq"].T, i["L0_attn_wk"].T], axis=1))
    o["wv"] = kp(i["L0_attn_wv"].T)
    pos = np.arange(S, dtype=np.float32)[:, None]
    inv = np.float32(10000.0) ** (-(np.arange(0, DK, 2, dtype=np.float32) / np.float32(DK)))
    ang = (pos * inv.astype(np.float32)).astype(np.float32)
    cos, sin = np.cos(ang), np.sin(ang)
    cos = np.stack([cos, cos], -1).reshape(TILES, P, DK)
    sin = np.stack([-sin, sin], -1).reshape(TILES, P, DK)
    o["cos"] = cos.transpose(1, 0, 2).astype(np.float32)
    o["sin"] = sin.transpose(1, 0, 2).astype(np.float32)
    r = np.arange(P)
    later = np.where(r[None, :] > r[:, None], np.float32(-1e30), np.float32(0))
    o["mask"] = np.stack([later, later.T], 1).astype(np.float32)
    o["wo"] = kp(i["L0_attn_wo"].T)
    a = i["L0_ffn_A"].reshape(D, D)
    o["wbase"] = kp(np.concatenate([i["L0_ffn_W"].T, a.T], axis=1))
    o["wexp"] = kp(i["L0_ffn_B"].transpose(0, 2, 1).reshape(D, D))
    o["rw1"] = kp(i["L0_ffn_rw1"].T)
    o["rw2"] = i["L0_ffn_rw2"][:EXPERTS].T
    o["rb1"] = i["L0_ffn_rb1"].reshape(RHID, 1)
    o["rows"] = np.stack([i["L0_ffn_rb2"][:EXPERTS], i["L0_ffn_gates"]]).reshape(1, 2, EXPERTS)
    o["bias"] = i["L0_ffn_bias"].reshape(1, D)
    o["iota"] = np.tile(np.arange(EXPERTS, dtype=np.float32), (P, 1))
    w = i["L1_attn_Wqkv"].reshape(PAIRS, 2, 3, D1, D)
    wg = i["L1_attn_Wg"].reshape(PAIRS, 2, D1, D)
    each = np.stack([w[:, 0, 0], w[:, 1, 0], w[:, 0, 1], w[:, 1, 1], wg[:, 0], wg[:, 1], w[:, 0, 2], w[:, 1, 2]], 1)
    each = each.reshape(PAIRS, 8 * D1, KD, P)
    o["wpair"] = each.transpose(0, 3, 2, 1)
    o["wo1"] = i["L1_attn_Wo"].reshape(D, PAIRS, 2, D1).transpose(1, 3, 2, 0)
    o["nw"] = i["L1_attn_norm_w"].reshape(H1, D1).T
    o["slope"] = np.tile(i["L1_attn_slope_rate"].reshape(1, H1), (P, 1))
    m, n = r[None, :], r[:, None]
    last = np.zeros((P, P), np.float32)
    last[:, 0] = P
    last[:, 1] = P - 1 - r
    o["steps"] = np.stack([np.maximum(m - n, 0), m >= n, np.broadcast_to(m + 1, (P, P)), last], 1).astype(np.float32)
    o["wup"] = kp(i["L1_ffn_W_up"].T).reshape(P, KD * DE)
    o["wgate"] = kp(i["L1_ffn_W_gate"].T).reshape(P, KD * DE)
    o["wdown"] = kp(i["L1_ffn_W_down"].T).reshape(P, KE * D)
    return {k: np.ascontiguousarray(a) for k, a in o.items()}


def kernel(**inputs):
    import numpy as np
    import concourse.bacc as bacc
    from concourse.bass_utils import run_bass_kernel_spmd

    arrays = lay_out({k: np.asarray(a) for k, a in inputs.items()}, np)
    nc = bacc.Bacc("TRN2", target_bir_lowering=False, num_devices=1)
    ins = {k: nc.dram_tensor(f"in_{k}", a.shape, mybir.dt.from_np(a.dtype), kind="ExternalInput").ap()
           for k, a in arrays.items()}
    out = nc.dram_tensor("out", [P, TILES, D], F32, kind="ExternalOutput").ap()
    build(nc, ins, out)
    r = run_bass_kernel_spmd(nc, [{f"in_{k}": a for k, a in arrays.items()}], core_ids=[0])
    return r.results[0]["out"].transpose(1, 0, 2).reshape(1, S, D)
```

```python
from contextlib import ExitStack

import concourse.bass as bass
from concourse import mybir

F32 = mybir.dt.float32
F32R = mybir.dt.float32r
BF16 = mybir.dt.bfloat16
U32 = mybir.dt.uint32
ALU = mybir.AluOpType
ACT = mybir.ActivationFunctionType
AX = mybir.AxisListType

P = 128
S = 2048
D = 256
KD = D // P
TILES = S // P
GT = 4
GROUPS = TILES // GT
GN = GT * P
LN_EPS = 1e-5

H0, DK = 16, 16
HG = 4
HGROUPS = H0 // HG
VW = 32
Q_PART = (0, 0, 1, 1, 0, 2)
K_PART = (0, 1, 0, 1, 2, 0)
TERMS = len(Q_PART) * DK
RHID, EXPERTS = 64, 16

H1, D1 = 16, 128
PAIRS = H1 // 2
F1 = H1 * D1
DE = 1024
KE = DE // P
RMS_EPS = 1.1920928955078125e-07


class Stage:

    def __init__(self, nc, ctx, stage, *names):
        self.nc = nc
        self.made = {n: ctx.enter_context(nc.semaphore(f"{stage}_{n}")) for n in names}

    def __getitem__(self, name):
        return self.made[name]

    def clear(self):
        numbers = sorted(s.num for s in self.made.values())
        first = 0
        for i, n in enumerate(numbers):
            if i + 1 == len(numbers) or numbers[i + 1] != n + 1:
                self.nc.gpsimd.sem_clear(range(numbers[first], n + 1))
                first = i + 1
        self.nc.all_engine_barrier()


class Chain:

    def __init__(self, eng, sem):
        self.eng, self.sem, self.n = eng, sem, 0

    def did(self, ins):
        ins.then_inc(self.sem, 1)
        self.n += 1

    def settle(self):
        self.eng.wait_ge(self.sem, self.n)

    def link(self, ins):
        self.did(ins)
        self.settle()


def product(nc, out, a, b, start, stop):
    nc.tensor.matmul(out, a[0], b[0], start=start, stop=False)
    nc.tensor.matmul(out, a[0], b[1], start=False, stop=False)
    return nc.tensor.matmul(out, a[1], b[0], start=False, stop=stop)


LN_SEMS = ("ln_stats", "ln_std", "ln_xn", "ln_tr", "ln_ha", "ln_hv", "ln_hi", "vec")


class Norm:

    def __init__(self, nc, ctx, name, ident, eps, banks, before=0):
        sb = lambda n, s: ctx.enter_context(nc.sbuf_tensor(f"{name}_{n}", s, F32))
        self.stats = sb("stats", [P, GT, 6])
        self.mv = sb("mv", [P, GT, 2])
        self.std = sb("std", [P, GT])
        self.rstd = sb("rstd", [P, GT])
        self.xn = sb("xn", [P, GT, D])
        self.ident, self.eps, self.banks = ident, eps, banks
        self.nth = before + 1

    def vector(self, nc, v, chain, sem, x4):
        self.moments(nc, v, chain, sem, x4)
        self.normalize(nc, v, chain, sem, x4)

    def moments(self, nc, v, chain, sem, x4):
        for t in range(GT):
            chain.did(nc.vector.bn_stats(self.stats[:, t, :], x4[:, t, :]))
        chain.settle()
        for t in range(GT):
            last = nc.vector.bn_aggr(self.mv[:, t, :], self.stats[:, t, :])
        last.then_inc(sem["ln_stats"], 1)

    def normalize(self, nc, v, chain, sem, x4):
        v.wait_ge(sem["ln_std"], self.nth)
        chain.link(nc.vector.reciprocal(self.rstd[:], self.std[:]))
        for t in range(GT):
            last = nc.vector.tensor_scalar(self.xn[:, t, :], x4[:, t, :], self.mv[:, t, 0:1],
                                           self.rstd[:, t:t + 1], ALU.subtract, ALU.mult)
        last.then_inc(sem["ln_xn"], 1)

    def scalar_std(self, nc, a, sem):
        a.wait_ge(sem["ln_stats"], self.nth)
        nc.scalar.activation(self.std[:], self.mv[:, :, 1], ACT.Sqrt, bias=self.eps[:]).then_inc(sem["ln_std"], 1)

    def tensor(self, nc, pe, sem):
        pe.wait_ge(sem["ln_xn"], self.nth)
        for k in range(KD):
            for t in range(GT):
                last = nc.tensor.transpose(self.banks[k][:, t * P:(t + 1) * P],
                                           self.xn[:, t, k * P:(k + 1) * P], self.ident[:])
        last.then_inc(sem["ln_tr"], 1)

    def split(self, nc, a, v, sem, h, hi, lo):
        if a is not None:
            a.wait_ge(sem["ln_ha"], self.nth)
            nc.scalar.copy(hi[:, 0, :], h[:, 0, :]).then_inc(sem["ln_hi"], 1)
            a.wait_ge(sem["ln_hv"], self.nth)
            nc.scalar.copy(hi[:, 1, :], h[:, 1, :]).then_inc(sem["ln_hi"], 1)
        if v is not None:
            v.wait_ge(sem["ln_hv"], self.nth)
            for k in range(KD):
                v.wait_ge(sem["ln_hi"], KD * (self.nth - 1) + k + 1)
                nc.vector.tensor_tensor(lo[:, k, :], h[:, k, :], hi[:, k, :].bitcast(F32),
                                        ALU.subtract)

    def modulate(self, nc, a, v, sem, hT, scale1, shift):
        if a is not None:
            a.wait_ge(sem["ln_tr"], self.nth)
            nc.scalar.activation(hT[:, 0, :], self.banks[0][:], ACT.Identity, bias=shift[:, 0:1],
                                 scale=scale1[:, 0:1]).then_inc(sem["ln_ha"], 1)
        if v is not None:
            v.wait_ge(sem["ln_tr"], self.nth)
            nc.vector.tensor_scalar(hT[:, 1, :], self.banks[1][:], scale1[:, 1:2], shift[:, 1:2],
                                    ALU.mult, ALU.add).then_inc(sem["ln_hv"], 1)


def modulation(nc, bank, x, ident, eps, mods, gates, ins):
    with ExitStack() as c:
        sb = lambda n, s: c.enter_context(nc.sbuf_tensor(f"mod_{n}", s, F32))
        cT = sb("cT", [P, 2, KD])
        scT = sb("scT", [P, 2, KD])
        scb = sb("scb", [P, 2, KD, P])
        ones = sb("ones", [P, P])
        wm = sb("wm", [P, 2, KD, 6 * D])
        own = sb("own", [P, 2, 2 * 2 * KD, P])
        mag = sb("mag", [P, 2, 2, D])
        sgn = sb("sgn", [P, 2, 2, D])
        sem = Stage(nc, c, "mod", "c", "wm0", "wm1", "ident", "x", "silu", "rep", "row", "signed", "abs", "vec")
        gate_at = ((1, 0), (2, D))
        own_at = ((0, 0, 4), (1, D, 2), (2, 0, 2))

        with nc.Block() as block:
            @block.sync
            def _(sp):
                for l in range(2):
                    sp.dma_start(cT[:, l, :], ins[f"c{l}"]).then_inc(sem["c"], 16)
                for l in range(2):
                    sp.dma_start(wm[:, l], ins[f"wmod{l}"]).then_inc(sem[f"wm{l}"], 16)
                    if l == 0:
                        sp.dma_start(ident[:], ins["ident"]).then_inc(sem["ident"], 16)
                sp.dma_start(x[:], ins["x"]).then_inc(sem["x"], 16)
                sp.wait_ge(sem["x"], 16)

            @block.scalar
            def _(a):
                a.wait_ge(sem["c"], 32)
                nc.scalar.activation(scT[:], cT[:], ACT.Silu).then_inc(sem["silu"], 1)
                for l in range(2):
                    a.wait_ge(sem["signed"], l + 1)
                    for n, (b, at) in enumerate(gate_at):
                        last = nc.scalar.activation(mag[:, l, n, :], bank[3 * l + b][:, at:at + D], ACT.Abs, scale=2.0)
                last.then_inc(sem["abs"], 1)

            @block.tensor
            def _(pe):
                pe.wait_ge(sem["rep"], 1)
                for l in range(2):
                    pe.wait_ge(sem[f"wm{l}"], 16)
                    for b in range(3):
                        for k in range(KD):
                            mm = nc.tensor.matmul(bank[3 * l + b][:], scb[:, l, k, :],
                                                  wm[:, l, k, b * 2 * D:(b + 1) * 2 * D],
                                                  start=(k == 0), stop=(k == KD - 1))
                        mm.then_inc(sem["row"], 1)

            @block.vector
            def _(v):
                chain = Chain(v, sem["vec"])
                nc.vector.memset(eps[:], LN_EPS)
                chain.link(nc.vector.memset(ones[:], 1.0))
                v.wait_ge(sem["silu"], 1)
                for l in range(2):
                    for k in range(KD):
                        last = nc.vector.tensor_scalar(scb[:, l, k, :], ones[:], scT[:, l, k:k + 1], None, ALU.mult)
                last.then_inc(sem["rep"], 1)
                v.wait_ge(sem["ident"], 16)
                for l in range(2):
                    done = 0
                    for b, at, blocks in own_at:
                        v.wait_ge(sem["row"], 3 * l + b + 1)
                        src = bank[3 * l + b][:, at:at + blocks * P].rearrange("p (n q) -> p n q", q=P)
                        chain.did(nc.vector.tensor_tensor(own[:, l, done:done + blocks, :], src,
                                                          ident[:].unsqueeze(1).to_broadcast([P, blocks, P]), ALU.mult))
                        done += blocks
                    for n, (b, at) in enumerate(gate_at):
                        last = nc.vector.tensor_scalar(sgn[:, l, n, :], bank[3 * l + b][:, at:at + D], 0.0, 0.5,
                                                       ALU.is_ge, ALU.subtract)
                    last.then_inc(sem["signed"], 1)
                    chain.settle()
                    chain.link(nc.vector.tensor_reduce(mods[:, l].rearrange("p a b k -> p (a b k)"), own[:, l], AX.X,
                                                       ALU.add))
                    nc.vector.tensor_scalar(mods[:, l, :, 1, :], mods[:, l, :, 1, :], 1.0, None, ALU.add)
                v.wait_ge(sem["abs"], 1)
                v.wait_ge(sem["signed"], 2)
                nc.vector.scalar_tensor_tensor(gates[:], mag[:], 0.5, sgn[:], ALU.max, ALU.mult)
        sem.clear()


def rope_front(nc, bank, x, v_all, ident, eps, mods, parts_dram, ins):
    with ExitStack() as c:
        sb = lambda n, s, dt=F32: c.enter_context(nc.sbuf_tensor(f"rf_{n}", s, dt))
        norm = Norm(nc, c, "rf", ident, eps, bank[0:2])
        hT = sb("hT", [P, KD, GN])
        wqk = sb("wqk", [P, KD, 2 * D])
        wv = sb("wv", [P, KD, D])
        cos = sb("cos", [P, TILES, DK])
        sin = sb("sin", [P, TILES, DK])
        straight = sb("straight", [P, 2, 2 * D])
        crossed = sb("crossed", [P, 2, 2 * D])
        turned = sb("turned", [P, GT, 2 * D])
        part = sb("part", [P, 4, 3, GN], BF16)
        rest = sb("rest", [P, 4, GN])
        sem = Stage(nc, c, "rf", *LN_SEMS, "load", "qk", "v", "turned", "vcopy", "high", "rest", "middle",
                    "parts", "store")
        heads = 2 * D // DK
        pairs = lambda ap: ap.rearrange("p (h i two) -> p h i two", i=DK // 2, two=2)

        def table(t, g, n):
            row = t[:, bass.ds(g * GT + n, 1), :].rearrange("p one (i two) -> p one i two", two=2)
            return row.to_broadcast([P, heads, DK // 2, 2])

        rows = lambda g: x[:, bass.ds(g * GT, GT), :]
        factor, shift = mods[:, 0, 0, 1, :], mods[:, 0, 0, 0, :]

        with nc.Block() as block:
            @block.sync
            def _(sp):
                sp.dma_start(wqk[:], ins["wqk"]).then_inc(sem["load"], 16)
                sp.dma_start(wv[:], ins["wv"]).then_inc(sem["load"], 16)
                sp.dma_start(cos[:], ins["cos"]).then_inc(sem["load"], 16)
                sp.dma_start(sin[:], ins["sin"]).then_inc(sem["load"], 16)
                sp.wait_ge(sem["load"], 64)

            @block.vector
            def _(v):
                norm.vector(nc, v, Chain(v, sem["vec"]), sem, rows(0))
                norm.modulate(nc, None, v, sem, hT, factor, shift)

            @block.scalar
            def _(a):
                norm.scalar_std(nc, a, sem)
                norm.modulate(nc, a, None, sem, hT, factor, shift)

            @block.tensor
            def _(pe):
                norm.tensor(nc, pe, sem)
        sem.clear()

        def high_part(a, j):
            nc.scalar.copy(part[:, j, 0, :], bank[4 + j][:]).then_inc(sem["high"], 1)

        def middle_part(a, j):
            a.wait_ge(sem["rest"], j + 1)
            nc.scalar.copy(part[:, j, 1, :], rest[:, j, :]).then_inc(sem["middle"], 1)

        def rests(v):
            for j in range(4):
                v.wait_ge(sem["high"], j + 1)
                nc.vector.tensor_tensor(rest[:, j, :], bank[4 + j][:], part[:, j, 0, :],
                                        ALU.subtract).then_inc(sem["rest"], 1)

        def low_parts(gp):
            for j in range(4):
                gp.wait_ge(sem["middle"], j + 1)
                nc.gpsimd.tensor_tensor(part[:, j, 2, :], rest[:, j, :], part[:, j, 1, :],
                                        ALU.subtract).then_inc(sem["parts"], 1)

        def store_parts(sp, g):
            for j in range(4):
                sp.wait_ge(sem["parts"], j + 1)
                half = (j % 2) * P
                dst = parts_dram[j // 2, :, half:half + P, bass.ds(g * GN, GN)].rearrange("c p s -> p c s")
                sp.dma_start(dst, part[:, j]).then_inc(sem["store"], 16)
            sp.wait_ge(sem["store"], 64)

        def all_parts(a):
            for j in range(5):
                if j < 4:
                    high_part(a, j)
                if j:
                    middle_part(a, j - 1)

        def turn(g, first=False, last=False):
            with nc.Block() as block:
                @block.vector
                def _(v):
                    chain = Chain(v, sem["vec"])
                    if not first:
                        rests(v)
                    for t in range(GT):
                        v.wait_ge(sem["qk"], t + 1)
                        chain.did(nc.vector.tensor_tensor(pairs(straight[:, t % 2, :]), pairs(bank[2 + t % 2][:]),
                                                          table(cos, g, t), ALU.mult))
                        chain.link(nc.vector.tensor_tensor(pairs(crossed[:, t % 2, :]),
                                                           pairs(bank[2 + t % 2][:])[:, :, :, ::-1],
                                                           table(sin, g, t), ALU.mult))
                        nc.vector.tensor_tensor(turned[:, t, :], straight[:, t % 2, :], crossed[:, t % 2, :],
                                                ALU.add).then_inc(sem["turned"], 1)
                        if t == 1 and not last:
                            norm.moments(nc, v, chain, sem, rows(g + 1))
                        if t == 2 and not last:
                            norm.normalize(nc, v, chain, sem, rows(g + 1))
                    if not last:
                        norm.modulate(nc, None, v, sem, hT, factor, shift)

                @block.scalar
                def _(a):
                    if not first:
                        all_parts(a)
                    for i in range(GT // 2):
                        if i == 1 and not last:
                            norm.scalar_std(nc, a, sem)
                        a.wait_ge(sem["v"], i + 1)
                        nc.scalar.copy(v_all[:, bass.ds(g * GT + 2 * i, 2), :],
                                       bank[i][:].rearrange("p (t n) -> p t n", t=2)).then_inc(sem["vcopy"], 1)
                    if not last:
                        norm.modulate(nc, a, None, sem, hT, factor, shift)

                @block.tensor
                def _(pe):
                    def turn_tile(t):
                        pe.wait_ge(sem["turned"], t + 1)
                        for j in range(4):
                            nc.tensor.transpose(bank[4 + j][:, t * P:(t + 1) * P],
                                                turned[:, t, j * P:(j + 1) * P], ident[:])

                    for i in range(GT // 2):
                        for t in (2 * i, 2 * i + 1):
                            if i:
                                turn_tile(t - 2)
                            for k in range(KD):
                                mm = nc.tensor.matmul(bank[2 + t % 2][:], hT[:, k, t * P:(t + 1) * P], wqk[:, k, :],
                                                      start=(k == 0), stop=(k == KD - 1))
                            mm.then_inc(sem["qk"], 1)
                        for t in (2 * i, 2 * i + 1):
                            for k in range(KD):
                                mm = nc.tensor.matmul(bank[i][:, (t % 2) * D:(t % 2 + 1) * D],
                                                      hT[:, k, t * P:(t + 1) * P], wv[:, k, :],
                                                      start=(k == 0), stop=(k == KD - 1))
                        mm.then_inc(sem["v"], 1)
                        if i == 0 and not first:
                            pe.wait_ge(sem["rest"], 4)
                    turn_tile(2)
                    if not last:
                        pe.wait_ge(sem["vcopy"], GT // 2)
                        norm.tensor(nc, pe, sem)
                    turn_tile(3)

                if not first:
                    @block.gpsimd
                    def _(gp):
                        low_parts(gp)

                    @block.sync
                    def _(sp):
                        store_parts(sp, g - 1)
            sem.clear()

        turn(0, first=True)
        with nc.Fori(1, GROUPS - 1) as g:
            turn(g)
        turn(GROUPS - 1, last=True)
        with nc.Block() as block:
            @block.vector
            def _(v):
                rests(v)

            @block.scalar
            def _(a):
                all_parts(a)

            @block.gpsimd
            def _(gp):
                low_parts(gp)

            @block.sync
            def _(sp):
                store_parts(sp, GROUPS - 1)
        sem.clear()


def attention_order():
    order = []
    steps = [(0, 3), (1, 3), (0, 2), (0, 1), (1, 2), (0, 0), (1, 1), (1, 0)]
    maxima = [(s, piece) for s, (_, cq) in enumerate(steps) for piece in pieces(cq)]
    exps = [(s, kb, h) for s, (_, cq) in enumerate(steps) for kb in range(GT * (cq + 1)) for h in range(HG)]
    pe = dve = act = 0.0
    reduced, exped = [], []
    parts, rows = {}, {}
    m = e = shifted = 0
    while e < len(exps):
        s, kb, h = exps[e]
        if shifted < len(steps) and shifted <= s + 1 and parts.get(shifted, 1e9) <= max(pe, act if shifted > s else 0):
            order.append(("shift", shifted))
            pe += 0.3
            act = max(act, pe) + 2.0
            rows[shifted] = act
            shifted += 1
            continue
        can_m = m < len(maxima) and maxima[m][0] <= s + 2
        can_e = s in rows and (rows[s] <= pe or not can_m)
        if not can_e and not can_m:
            pe = parts[shifted] if shifted in parts and parts[shifted] > pe else pe + 0.5
            continue
        at_m = max(pe, reduced[m - 3] if m >= 3 else 0.0)
        at_e = max(pe, exped[e - 3] if e >= 3 else 0.0)
        if can_m and (not can_e or (at_m <= at_e + 0.3 and dve <= act)):
            step, piece = maxima[m]
            order.append(("max", step, piece))
            pe = at_m + piece[4] / 2400
            dve = max(dve, pe + 0.1) + piece[4] / 960 + 0.07
            reduced.append(dve)
            m += 1
            if m == len(maxima) or maxima[m][0] != step:
                dve += 0.15
                parts[step] = dve + 1.5
        else:
            w = GN - max(0, kb - GT * steps[s][1]) * P
            order.append(("exp", s, kb, h))
            pe = max(at_e, rows[s]) + w / 2400
            act = max(act, pe + 0.2) + w / 1050 + 0.1
            exped.append(act)
            e += 1
            if h == HG - 1:
                pe = max(pe, exped[e - HG - 1] if e > HG else 0.0) + 0.85 * w / GN
                if kb == 1 and s:
                    order.append(("turn", s - 1))
                    pe, dve, act = pe + 0.25, dve + 0.5, act + 0.5
                if e == len(exps):
                    order.append(("turn", s))
    return steps, order


def last_of_first(steps):
    return max(s for s, (gi, _) in enumerate(steps) if gi == 0)


def pieces(cq):
    return [(t * HG + h, h, t, p, GN if p < cq else P * (t + 1))
            for t in range(GT) for h in range(HG) for p in range(cq + 1)]


def rope_attention(nc, bank, v_all, attn, ident, parts_dram, ins):
    steps, order = attention_order()
    with ExitStack() as c:
        sb = lambda n, s, dt=F32: c.enter_context(nc.sbuf_tensor(f"ra_{n}", s, dt))
        kst = sb("kst", [P, 2, HG, S], BF16)
        qst = sb("qst", [P, 2, HG, S], BF16)
        vg = sb("vg", [P, 2, TILES, HG, VW])
        prob = sb("prob", [P, 2, HG, GN])
        sums = sb("sums", [P, GN])
        pm = sb("pm", [P, 2, GT * HG, GROUPS])
        negm = sb("negm", [P, len(steps), GT * HG])
        nrest = sb("nrest", [P, 2, GT * HG])
        mp = sb("mp", [P, len(steps), GT * HG, VW], BF16)
        rec = sb("rec", [P, GT, HG])
        mask_f = sb("mask_f", [P, P])
        mask = sb("mask", [P, P], BF16)
        identb = sb("identb", [P, P], BF16)
        sem = Stage(nc, c, "ra", "load", "next", "vg", "cut", "pm", "red", "neg", "mp", "trm", "shift", "sc", "exp",
                    "av", "avs", "trn", "norm", "vec", "pool")
        PM, ST, AV, TR = bank[0:3], bank[3:6], bank[6], bank[7]
        TRb = TR[:].bitcast(BF16)
        LOADS = 16 * 2 * len(Q_PART)

        first_piece = [sum(len(pieces(cq)) for _, cq in steps[:s]) for s in range(len(steps) + 1)]
        first_block = [sum(GT * (cq + 1) for _, cq in steps[:s]) for s in range(len(steps) + 1)]

        first_of_second = next(s for s, (gi, _) in enumerate(steps) if gi == 1)
        first_done = first_block[last_of_first(steps) + 1]

        def load_stacks(sp, gi, group, done):
            for side, dst, parts in ((0, qst, Q_PART), (1, kst, K_PART)):
                for j, which in enumerate(parts):
                    src = parts_dram[side, which, bass.ds(group * (HG * DK), HG * DK), :]
                    sp.dma_start(dst[j * DK:(j + 1) * DK, gi, :, :],
                                 src.rearrange("(h r) s -> r h s", r=DK)).then_inc(done, 16)

        def take_values(gi, group):
            src = v_all[:, :, bass.ds(group * (HG * DK), HG * DK)]
            nc.gpsimd.tensor_copy(vg[:, gi, :, :, 0:DK], src.rearrange("p t (h d) -> p t h d", h=HG))\
              .then_inc(sem["vg"], 1)

        def maxima_parts(gp, chain, s):
            gp.wait_ge(sem["neg"], s + 1)
            m, r, to = negm[:, s, :], nrest[:, s % 2, :], mp[:, s]
            chain.link(nc.gpsimd.tensor_copy(to[:, :, 0], m))
            chain.link(nc.gpsimd.tensor_tensor(r, m, to[:, :, 0], ALU.subtract))
            chain.link(nc.gpsimd.tensor_copy(to[:, :, 1], r))
            nc.gpsimd.tensor_tensor(to[:, :, 2], r, to[:, :, 1], ALU.subtract).then_inc(sem["mp"], 1)

        def reduce_piece(v, s, piece, n, last):
            row, h, t, p, w = piece
            v.wait_ge(sem["pm"], n + 1)
            nc.vector.tensor_reduce(pm[:, s % 2, row, p:p + 1], PM[n % 3][:, 0:w], AX.X,
                                    ALU.max).then_inc(sem["red"], 1)
            if last:
                v.wait_ge(sem["red"], n + 1)
                nc.vector.tensor_reduce(negm[:, s, :], pm[:, s % 2, :, 0:steps[s][1] + 1], AX.X,
                                        ALU.max, negate=True).then_inc(sem["neg"], 1)

        def score_piece(pe, s, piece, n):
            row, h, t, p, w = piece
            gi, cq = steps[s]
            if n >= 3:
                pe.wait_ge(sem["red"], n - 2)
            q = qst[0:TERMS, gi, h, cq * GN + t * P:cq * GN + (t + 1) * P]
            last = nc.tensor.matmul(PM[n % 3][:, 0:w], q, kst[0:TERMS, gi, h, p * GN:p * GN + w],
                                    start=True, stop=(p < cq))
            if p == cq:
                last = nc.tensor.matmul(PM[n % 3][:, w - P:w], identb[:], mask[:], start=False, stop=True)
            last.then_inc(sem["pm"], 1)

        def turn_maxima(pe, s):
            pe.wait_ge(sem["mp"], s + 1)
            for t in range(GT):
                rows = mp[:, s, t * HG:(t + 1) * HG, :].rearrange("p h w -> p (h w)")
                last = nc.tensor.transpose(TRb[:, t * P:(t + 1) * P], rows, identb[:])
            last.then_inc(sem["trm"], 1)

        def shift_rows(a, s):
            gi, cq = steps[s]
            a.wait_ge(sem["trm"], s + 1)
            for h in range(HG):
                last = nc.scalar.copy(qst[TERMS:P, gi, h, cq * GN:(cq + 1) * GN], TRb[h * VW:(h + 1) * VW, 0:GN])
            last.then_inc(sem["shift"], 1)

        with nc.Block() as block:
            @block.sync
            def _(sp):
                sp.dma_start(mask_f[:], ins["mask"]).then_inc(sem["load"], 16)
                load_stacks(sp, 0, 0, sem["next"])
                sp.wait_ge(sem["next"], LOADS)

            @block.vector
            def _(v):
                nc.vector.tensor_copy(identb[:], ident[:])
                nc.vector.memset(mp[:], 0.0)
                nc.vector.memset(kst[TERMS:P, 0], 1.0)
                v.wait_ge(sem["load"], 16)
                nc.vector.tensor_copy(mask[:], mask_f[:])

            @block.gpsimd
            def _(gp):
                chain = Chain(gp, sem["pool"])
                chain.link(nc.gpsimd.memset(kst[TERMS:P, 1], 1.0))
                chain.link(nc.gpsimd.memset(vg[:], 0.0))
                chain.link(nc.gpsimd.memset(vg[:, :, :, :, DK:DK + 1], 1.0))
        sem.clear()

        with nc.Fori(0, HGROUPS // 2) as turn:
            with nc.Block() as block:
                @block.sync
                def _(sp):
                    load_stacks(sp, 1, turn * 2 + 1, sem["load"])
                    sp.wait_ge(sem["av"], first_done)
                    load_stacks(sp, 0, 2 - turn * 2, sem["next"])
                    sp.wait_ge(sem["next"], LOADS)

                @block.gpsimd
                def _(gp):
                    chain = Chain(gp, sem["pool"])
                    take_values(0, turn * 2)
                    take_values(1, turn * 2 + 1)
                    n = 0
                    for entry in order:
                        if entry[0] == "max":
                            n += 1
                            if n == first_piece[entry[1] + 1]:
                                maxima_parts(gp, chain, entry[1])
                        if entry[0] == "exp" and entry[3] == HG - 1:
                            s, kb = entry[1:3]
                            b, at = first_block[s] + kb, (kb - GT * steps[s][1]) * P
                            if at >= 0:
                                gp.wait_ge(sem["exp"], HG * (b + 1))
                                some = prob[:, b % 2, :, at:at + P]
                                nc.gpsimd.affine_select(out=some, in_=some, pattern=[[0, HG], [1, P]], base=0,
                                                        channel_multiplier=-1, compare_op=ALU.is_ge,
                                                        fill=0.0).then_inc(sem["cut"], 1)

                @block.vector
                def _(v):
                    chain = Chain(v, sem["vec"])

                    def normalize(s):
                        gi, cq = steps[s]
                        v.wait_ge(sem["trn"], s + 1)
                        tr = TR[:].rearrange("p (t h w) -> p t h w", t=GT, h=HG)
                        chain.link(nc.vector.reciprocal(rec[:], tr[:, :, :, DK]))
                        dst = attn[:, cq * GT:(cq + 1) * GT, bass.ds((turn * 2 + gi) * (HG * DK), HG * DK)]
                        nc.vector.tensor_tensor(dst.rearrange("p t (h d) -> p t h d", h=HG), tr[:, :, :, 0:DK],
                                                rec[:].unsqueeze(3).to_broadcast([P, GT, HG, DK]),
                                                ALU.mult).then_inc(sem["norm"], 1)

                    n, waiting = 0, None
                    for entry in order:
                        if entry[0] == "max":
                            s, piece = entry[1:]
                            reduce_piece(v, s, piece, n, n + 1 == first_piece[s + 1])
                            n += 1
                            if waiting is not None and n >= waiting[1]:
                                normalize(waiting[0])
                                waiting = None
                        if entry[0] == "turn":
                            if waiting is not None:
                                normalize(waiting[0])
                            waiting = (entry[1], n + 3)
                        if entry[0] == "shift" and waiting is not None:
                            normalize(waiting[0])
                            waiting = None
                    if waiting is not None:
                        normalize(waiting[0])

                @block.scalar
                def _(a):
                    def take_sums(s):
                        a.wait_ge(sem["av"], first_block[s + 1])
                        if s:
                            a.wait_ge(sem["trn"], s)
                        nc.scalar.copy(sums[:], AV[:]).then_inc(sem["avs"], 1)

                    e = 0
                    for entry in order:
                        if entry[0] == "shift":
                            shift_rows(a, entry[1])
                        if entry[0] == "exp":
                            s, kb, h = entry[1:]
                            gi, cq = steps[s]
                            off = max(0, kb - GT * cq) * P
                            b = first_block[s] + kb
                            if b >= 2 and h == 0:
                                a.wait_ge(sem["av"], b - 1)
                            a.wait_ge(sem["sc"], e + 1)
                            nc.scalar.activation(prob[:, b % 2, h, off:GN], ST[e % 3][:, off:GN], ACT.Exp,
                                                 scale=float(DK) ** -0.5).then_inc(sem["exp"], 1)
                            e += 1
                            if kb == 1 and s and h == 1:
                                take_sums(s - 1)
                        if entry == ("turn", len(steps) - 1):
                            take_sums(len(steps) - 1)

                @block.tensor
                def _(pe):
                    n = e = turned = shifted = 0

                    def values(s, kb):
                        gi, cq = steps[s]
                        off = max(0, kb - GT * cq) * P
                        b = first_block[s] + kb
                        pe.wait_ge(sem["exp"], HG * (b + 1))
                        if kb >= GT * cq:
                            pe.wait_ge(sem["cut"], GT * s + kb - GT * cq + 1)
                        if kb == 0:
                            pe.wait_ge(sem["vg"], gi + 1)
                        if kb == 0 and s:
                            pe.wait_ge(sem["avs"], s)
                        for h in range(HG):
                            last = nc.tensor.matmul(AV[h * VW:(h + 1) * VW, off:GN], vg[:, gi, kb, h, :],
                                                    prob[:, b % 2, h, off:GN], start=(kb == 0),
                                                    stop=(kb == GT * (cq + 1) - 1), skip_group_check=True)
                        last.then_inc(sem["av"], 1)

                    behind = None
                    for entry in order:
                        s = entry[1]
                        gi, cq = steps[s]
                        if entry[0] == "max":
                            if s == first_of_second and entry[2] == pieces(cq)[0]:
                                pe.wait_ge(sem["load"], LOADS)
                            score_piece(pe, s, entry[2], n)
                            n += 1
                        if entry[0] == "shift":
                            if turned:
                                pe.wait_ge(sem["norm"], turned)
                            turn_maxima(pe, s)
                            shifted += 1
                        if entry[0] == "exp":
                            kb, h = entry[2:]
                            off = max(0, kb - GT * cq) * P
                            if kb == 0 and h == 0:
                                pe.wait_ge(sem["shift"], s + 1)
                            if e >= 3:
                                pe.wait_ge(sem["exp"], e - 2)
                            last = nc.tensor.matmul(ST[e % 3][:, off:GN], kst[:, gi, h, kb * P:(kb + 1) * P],
                                                    qst[:, gi, h, cq * GN + off:(cq + 1) * GN],
                                                    start=True, stop=True)
                            last.then_inc(sem["sc"], 1)
                            e += 1
                            if h == HG - 1:
                                if behind is not None:
                                    values(*behind)
                                behind = (s, kb)
                        if entry[0] == "turn":
                            if s == len(steps) - 1:
                                values(*behind)
                            pe.wait_ge(sem["avs"], s + 1)
                            pe.wait_ge(sem["shift"], shifted)
                            if turned:
                                pe.wait_ge(sem["norm"], turned)
                            for t in range(GT):
                                last = nc.tensor.transpose(TR[:, t * P:(t + 1) * P], sums[:, t * P:(t + 1) * P],
                                                           ident[:])
                            last.then_inc(sem["trn"], 1)
                            turned += 1
            sem.clear()


def routed_ffn(nc, bank, x, attn, ident, eps, mods, gates, ins):
    with ExitStack() as c:
        sb = lambda n, s, dt=F32: c.enter_context(nc.sbuf_tensor(f"ff_{n}", s, dt))
        norm = Norm(nc, c, "ff", ident, eps, bank[0:2])
        hT = sb("hT", [P, KD, GN])
        stage = sb("stage", [P, GT, D])
        aT = sb("aT", [P, KD, GN])
        wo = sb("wo", [P, KD, D])
        wbase = sb("wbase", [P, KD, 2 * D])
        wexp = sb("wexp", [P, KD, D])
        rw1 = sb("rw1", [P, KD, RHID])
        rw2 = sb("rw2", [RHID, EXPERTS])
        rb1 = sb("rb1", [RHID, 1])
        vrows = sb("rows", [1, 2, EXPERTS])
        brow = sb("brow", [1, EXPERTS])
        bias = sb("bias", [1, D])
        gbias = sb("gbias", [P, D])
        res = sb("res", [P, GT, D])
        ones = sb("ones", [1, P])
        iota = sb("iota", [P, EXPERTS])
        sig = sb("sig", [RHID, GN])
        r1 = sb("r1", [RHID, GN])
        logit = sb("logit", [P, GT, EXPERTS])
        top = sb("top", [P, GT, 8])
        topi = sb("topi", [P, GT, 8], U32)
        topf = sb("topf", [P, GT, 2])
        gap = sb("gap", [P, 2, GT])
        sm = sb("sm", [P, 2, GT])
        coef = sb("coef", [P, 2, GT, EXPERTS])
        wxa = sb("wxa", [P, GT, D])
        wxaT = sb("wxaT", [P, KD, GN])
        upd = sb("upd", [P, GT, D])
        sem = Stage(nc, c, "ff", *LN_SEMS, "wo", "load", "stage", "atr", "aT", "y", "h1", "sig", "r1", "logit",
                    "gap", "sm", "base", "wxa", "wtr", "wxaT", "res", "ones", "bias")
        loads = (("wbase", wbase), ("wexp", wexp), ("rw1", rw1), ("rw2", rw2), ("rb1", rb1),
                 ("rows", vrows), ("bias", bias), ("iota", iota))

        rows = lambda g: x[:, bass.ds(g * GT, GT), :]
        two = lambda ap: ap.rearrange("p (t n) -> p t n", t=2)

        def take_attention(a, g):
            nc.scalar.copy(stage[:], attn[:, bass.ds(g * GT, GT), :]).then_inc(sem["stage"], 1)

        def turn_attention(pe):
            pe.wait_ge(sem["stage"], 1)
            for k in range(KD):
                for t in range(GT):
                    last = nc.tensor.transpose(bank[k][:, t * P:(t + 1) * P],
                                               stage[:, t, k * P:(k + 1) * P], ident[:])
                last.then_inc(sem["atr"], 1)

        def copy_attention(a):
            for k in range(KD):
                a.wait_ge(sem["atr"], k + 1)
                nc.scalar.copy(aT[:, k, :], bank[k][:]).then_inc(sem["aT"], 1)

        def project_out(pe):
            pe.wait_ge(sem["aT"], KD)
            for t in range(GT):
                for k in range(KD):
                    last = nc.tensor.matmul(bank[t // 2][:, (t % 2) * D:(t % 2 + 1) * D],
                                            aT[:, k, t * P:(t + 1) * P], wo[:, k, :],
                                            start=(k == 0), stop=(k == KD - 1))
                if t % 2:
                    last.then_inc(sem["y"], 1)

        def add_attention(v, chain, g):
            for i in range(GT // 2):
                v.wait_ge(sem["y"], i + 1)
                chain.did(nc.vector.tensor_tensor(upd[:, 2 * i:2 * i + 2, :], two(bank[i][:]),
                                                  gates[:, 0, 0:1, :].to_broadcast([P, 2, D]), ALU.mult))
            chain.settle()
            chain.link(nc.vector.tensor_tensor(rows(g), rows(g), upd[:], ALU.add))
            norm.moments(nc, v, chain, sem, rows(g))

        factor, shift = mods[:, 0, 1, 1, :], mods[:, 0, 1, 0, :]

        with nc.Block() as block:
            @block.sync
            def _(sp):
                sp.dma_start(wo[:], ins["wo"]).then_inc(sem["wo"], 16)
                for name, dst in loads:
                    sp.dma_start(dst[:], ins[name]).then_inc(sem["load"], 16)

            @block.scalar
            def _(a):
                take_attention(a, 0)
                copy_attention(a)
                norm.scalar_std(nc, a, sem)
                norm.modulate(nc, a, None, sem, hT, factor, shift)

            @block.tensor
            def _(pe):
                turn_attention(pe)
                pe.wait_ge(sem["wo"], 16)
                project_out(pe)
                norm.tensor(nc, pe, sem)
                pe.wait_ge(sem["load"], 16 * len(loads))
                pe.wait_ge(sem["ones"], 1)
                nc.tensor.matmul(bank[2][:, 0:D], ones[:], bias[:], start=True, stop=True).then_inc(sem["bias"], 1)

            @block.vector
            def _(v):
                chain = Chain(v, sem["vec"])
                nc.vector.memset(ones[:], 1.0).then_inc(sem["ones"], 1)
                add_attention(v, chain, 0)
                norm.normalize(nc, v, chain, sem, rows(0))
                norm.modulate(nc, None, v, sem, hT, factor, shift)
                v.wait_ge(sem["load"], 16 * len(loads))
                nc.vector.tensor_tensor(brow[:], vrows[:, 0, :], vrows[:, 1, :], ALU.add)
                v.wait_ge(sem["bias"], 1)
                nc.vector.tensor_tensor(gbias[:], bank[2][:, 0:D], gates[:, 0, 1, :], ALU.mult)
        sem.clear()

        def take_result(v):
            for t in range(GT):
                nc.vector.tensor_tensor(res[:, t, :], bank[4 + t][:, 0:D], gates[:, 0, 1, :],
                                        ALU.mult).then_inc(sem["res"], 1)

        def finish(v, chain, g):
            v.wait_ge(sem["res"], GT)
            chain.link(nc.vector.tensor_tensor(res[:], res[:], gbias[:].unsqueeze(1).to_broadcast([P, GT, D]),
                                               ALU.add))
            nc.vector.tensor_tensor(rows(g), rows(g), res[:], ALU.add)

        def turn(g, first=False, last=False):
            with nc.Block() as block:
                @block.scalar
                def _(a):
                    if not last:
                        take_attention(a, g + 1)
                    a.wait_ge(sem["h1"], 1)
                    nc.scalar.activation(sig[:], bank[2][0:RHID, :], ACT.Sigmoid, bias=rb1[:]).then_inc(sem["sig"], 1)
                    if not last:
                        copy_attention(a)
                    a.wait_ge(sem["gap"], 1)
                    nc.scalar.activation(sm[:], gap[:], ACT.Sigmoid).then_inc(sem["sm"], 1)
                    if not last:
                        norm.scalar_std(nc, a, sem)
                    for k in range(KD):
                        a.wait_ge(sem["wtr"], k + 1)
                        nc.scalar.copy(wxaT[:, k, :], bank[2 + k][:]).then_inc(sem["wxaT"], 1)
                    if not last:
                        norm.modulate(nc, a, None, sem, hT, factor, shift)

                @block.tensor
                def _(pe):
                    def base(t):
                        for k in range(KD):
                            mm = nc.tensor.matmul(bank[4 + t][:], hT[:, k, t * P:(t + 1) * P], wbase[:, k, :],
                                                  start=(k == 0), stop=False, skip_group_check=True)
                        mm.then_inc(sem["base"], 1)

                    for k in range(KD):
                        mm = nc.tensor.matmul(bank[2][0:RHID, :], rw1[:, k, :], hT[:, k, :],
                                              start=(k == 0), stop=(k == KD - 1))
                    mm.then_inc(sem["h1"], 1)
                    if not last:
                        turn_attention(pe)
                    if not first:
                        pe.wait_ge(sem["res"], GT)
                    base(0)
                    pe.wait_ge(sem["r1"], 1)
                    for t in range(GT):
                        to = bank[3][:, t * EXPERTS:(t + 1) * EXPERTS]
                        nc.tensor.matmul(to, r1[:, t * P:(t + 1) * P], rw2[:], start=True, stop=False)
                        mm = nc.tensor.matmul(to, ones[:], brow[:], start=False, stop=True)
                    mm.then_inc(sem["logit"], 1)
                    if not last:
                        project_out(pe)
                    for t in range(1, GT):
                        base(t)
                    pe.wait_ge(sem["wxa"], GT)
                    for k in range(KD):
                        for t in range(GT):
                            mm = nc.tensor.transpose(bank[2 + k][:, t * P:(t + 1) * P],
                                                     wxa[:, t, k * P:(k + 1) * P], ident[:])
                        mm.then_inc(sem["wtr"], 1)
                    if not last:
                        norm.tensor(nc, pe, sem)
                    pe.wait_ge(sem["wxaT"], KD)
                    for t in range(GT):
                        for k in range(KD):
                            nc.tensor.matmul(bank[4 + t][:, 0:D], wxaT[:, k, t * P:(t + 1) * P], wexp[:, k, :],
                                             start=False, stop=(k == KD - 1), skip_group_check=True)

                @block.vector
                def _(v):
                    chain = Chain(v, sem["vec"])
                    if not first:
                        take_result(v)
                    v.wait_ge(sem["sig"], 1)
                    nc.vector.scalar_tensor_tensor(r1[:], bank[2][0:RHID, :], rb1[:, 0:1], sig[:], ALU.add,
                                                   ALU.mult).then_inc(sem["r1"], 1)
                    if not first:
                        finish(v, chain, g - 1)
                    v.wait_ge(sem["logit"], 1)
                    lg = bank[3][:, 0:GT * EXPERTS].rearrange("p (t e) -> p t e", t=GT)
                    chain.link(nc.vector.tensor_copy(logit[:], lg))
                    for t in range(GT):
                        chain.did(nc.vector.max(top[:, t, :], logit[:, t, :]))
                    chain.settle()
                    for t in range(GT):
                        chain.did(nc.vector.max_index(topi[:, t, :], top[:, t, :], logit[:, t, :]))
                    nc.vector.tensor_tensor(gap[:, 0, :], top[:, :, 0], top[:, :, 1], ALU.subtract)
                    nc.vector.tensor_tensor(gap[:, 1, :], top[:, :, 1], top[:, :, 0],
                                            ALU.subtract).then_inc(sem["gap"], 1)
                    chain.settle()
                    chain.link(nc.vector.tensor_copy(topf[:], topi[:, :, 0:2]))
                    v.wait_ge(sem["sm"], 1)
                    for t in range(GT):
                        for n in range(2):
                            chain.did(nc.vector.tensor_scalar(coef[:, n, t, :], iota[:], topf[:, t, n:n + 1],
                                                              sm[:, n, t:t + 1], ALU.is_equal, ALU.mult))
                    chain.settle()
                    chain.link(nc.vector.tensor_tensor(coef[:, 0], coef[:, 0], coef[:, 1], ALU.add))
                    if not last:
                        add_attention(v, chain, g + 1)
                    for t in range(GT):
                        v.wait_ge(sem["base"], t + 1)
                        xa = bank[4 + t][:, D:2 * D].rearrange("p (e r) -> p e r", e=EXPERTS)
                        nc.vector.tensor_tensor(wxa[:, t, :].rearrange("p (e r) -> p e r", e=EXPERTS), xa,
                                                coef[:, 0, t, :].unsqueeze(2).to_broadcast([P, EXPERTS, D // EXPERTS]),
                                                ALU.mult).then_inc(sem["wxa"], 1)
                    if not last:
                        norm.normalize(nc, v, chain, sem, rows(g + 1))
                        norm.modulate(nc, None, v, sem, hT, factor, shift)
            sem.clear()

        turn(0, first=True)
        with nc.Fori(1, GROUPS - 1) as g:
            turn(g)
        turn(GROUPS - 1, last=True)
        with nc.Block() as block:
            @block.vector
            def _(v):
                take_result(v)
                finish(v, Chain(v, sem["vec"]), GROUPS - 1)
        sem.clear()


def decay_front(nc, bank, x, hT, first, ident, eps, mods, x_dram, ins):
    with ExitStack() as c:
        norms = [Norm(nc, c, f"df{g}", ident, eps, bank[2 * g:2 * g + 2], before=g) for g in range(GROUPS)]
        h = c.enter_context(nc.sbuf_tensor("df_h", [P, GROUPS, KD, GN], F32))
        saves = [f"save{g}" for g in range(GROUPS)]
        sem = Stage(nc, c, "df", *LN_SEMS, *saves, "load")
        factor, shift = mods[:, 1, 0, 1, :], mods[:, 1, 0, 0, :]
        rows = [x[:, g * GT:(g + 1) * GT, :] for g in range(GROUPS)]
        parts = [[part[:, :, g * GN:(g + 1) * GN] for part in hT] for g in range(GROUPS)]
        with nc.Block() as block:
            @block.vector
            def _(v):
                chain = Chain(v, sem["vec"])
                for g in range(GROUPS + 3):
                    if g < GROUPS:
                        norms[g].moments(nc, v, chain, sem, rows[g])
                    if 1 <= g <= GROUPS:
                        norms[g - 1].normalize(nc, v, chain, sem, rows[g - 1])
                    if 2 <= g <= GROUPS + 1:
                        norms[g - 2].modulate(nc, None, v, sem, h[:, g - 2], factor, shift)
                    if g >= 3:
                        norms[g - 3].split(nc, None, v, sem, h[:, g - 3], *parts[g - 3])

            @block.scalar
            def _(a):
                for g in range(GROUPS + 2):
                    if g < GROUPS:
                        norms[g].scalar_std(nc, a, sem)
                    if g >= 2:
                        norms[g - 2].modulate(nc, a, None, sem, h[:, g - 2], factor, shift)
                        norms[g - 2].split(nc, a, None, sem, h[:, g - 2], *parts[g - 2])

            @block.tensor
            def _(pe):
                for norm in norms:
                    norm.tensor(nc, pe, sem)

            @block.sync
            def _(sp):
                raw, nw, slope, steps = first
                sp.dma_start(raw[:], ins["wpair"][0]).then_inc(sem["load"], 16)
                sp.dma_start(nw[:], ins["nw"]).then_inc(sem["load"], 16)
                sp.dma_start(slope[:], ins["slope"]).then_inc(sem["load"], 16)
                sp.dma_start(steps[:], ins["steps"]).then_inc(sem["load"], 16)
                for g, save in enumerate(saves):
                    sp.dma_start(x_dram[:, g * GT:(g + 1) * GT, :], rows[g]).then_inc(sem[save], 16)
                for save in saves:
                    sp.wait_ge(sem[save], 16)
                sp.wait_ge(sem["load"], 64)

            @block.gpsimd
            def _(gp):
                for g, save in enumerate(saves):
                    gp.wait_ge(sem[save], 16)
                    gp.wait_ge(sem["ln_xn"], g + 1)
                    nc.gpsimd.memset(rows[g], 0.0)
        sem.clear()


def decay_attention(nc, bank, x, hT, first, ident, gates, x_dram, ins):
    with ExitStack() as c:
        sb = lambda n, s, dt=F32: c.enter_context(nc.sbuf_tensor(f"da_{n}", s, dt))
        yacc = x
        raw, nw, slope, steps = first
        w = [sb("wh", [P, KD, 8 * D1], F32R), sb("wl", [P, KD, 8 * D1], F32R)]
        wo_raw = sb("wo_raw", [P, 2, D])
        wo = [sb("woh", [P, 2, D], F32R), sb("wol", [P, 2, D], F32R)]
        dmask = sb("dmask", [P, 2, P])
        qdec = sb("qdec", [P, 2, P])
        kbdec = sb("kbdec", [P, 2, 2])
        small = sb("small", [P, 2, 2])
        qT = sb("qT", [P, S])
        kT = sb("kT", [P, S])
        gT = sb("gT", [P, 2, GN])
        v = sb("v", [P, TILES, 2 * D1])
        ktok = sb("ktok", [P, TILES, D1])
        qd = sb("qd", [P, S])
        state = sb("state", [P, TILES, D1])
        smask = sb("smask", [P, 2, GT, P])
        oT = sb("oT", [P, 2, GN])
        sq = sb("sq", [P, 2, GN])
        og = sb("og", [P, 2, GN])
        ogs = [sb("ogh", [P, 2, S], F32R), sb("ogl", [P, 2, S], F32R)]
        ssum = sb("ssum", [P, S])
        ones = sb("ones", [P, 1])
        rms = sb("rms", [P, 2, TILES])
        reps = sb("reps", [P, 1])
        sem = Stage(nc, c, "da", "load", "next", "small", "sneg", "dec", "vec", "proj", "evac", "ktr",
                    "ktok", "qd", "dl", "st", "sc", "sm", "o", "oT", "sq", "ssum", "g", "og", "ogh", "ogl", "y", "yadd",
                    "ss", "rstd", "wh", "woh", "wol")
        PROJ, KTR, SC, DL, YB = bank[0:2], bank[2], bank[3], bank[4], bank[6:8]
        OB = bank[5], KTR

        AT_ONCE = 4
        SHARES = [*range(AT_ONCE, TILES // 2), *range(AT_ONCE)]
        LATE = TILES // 2 - AT_ONCE

        columns = {"v": slice(6 * D1, 8 * D1), "qk": slice(0, 4 * D1), "g": slice(4 * D1, 6 * D1)}

        def split_weights(kind, a=None, gp=None, ve=None):
            at = columns[kind]
            if a is not None:
                nc.scalar.copy(w[0][:, :, at], raw[:, :, at]).then_inc(sem["wh"], 1)
            if gp is not None:
                gp.wait_ge(sem["wh"], list(columns).index(kind) + 1)
                nc.gpsimd.tensor_tensor(w[1][:, :, at], raw[:, :, at], w[0][:, :, at].bitcast(F32),
                                        ALU.subtract)
            if ve is not None:
                ve.wait_ge(sem["wh"], list(columns).index(kind) + 1)
                nc.vector.tensor_tensor(w[1][:, :, at], raw[:, :, at], w[0][:, :, at].bitcast(F32),
                                        ALU.subtract)

        def add_squares(n, eng, ops):
            at = slice(n % GROUPS * GN, (n % GROUPS + 1) * GN)
            eng.wait_ge(sem["sq"], n + 1)
            ops.tensor_tensor(ssum[:, at], ssum[:, at], sq[:, n % 2, :], ALU.add).then_inc(sem["ssum"], 1)

        def load_pair(sp, pair, done):
            sp.dma_start(raw[:], ins["wpair"][bass.ds(pair, 1)].rearrange("o p k n -> (o p) k n")).then_inc(done, 16)

        with nc.Block() as block:
            @block.vector
            def _(ve):
                nc.vector.memset(state[:, 0, :], 0.0)
                nc.vector.memset(ones[:], 1.0)
                nc.vector.memset(reps[:], RMS_EPS)
                for part in (wo[0][:], wo[1][:], ogs[0][:, :, 2 * AT_ONCE * P:]):
                    nc.vector.memset(part.bitcast(F32), 0.0)
                split_weights("qk", ve=ve)

            @block.scalar
            def _(a):
                for kind in columns:
                    split_weights(kind, a=a)

            @block.gpsimd
            def _(gp):
                nc.gpsimd.memset(ssum[:], 0.0)
                nc.gpsimd.memset(ogs[1][:, :, 2 * AT_ONCE * P:].bitcast(F32), 0.0)
                split_weights("v", gp=gp)
                split_weights("g", gp=gp)
        sem.clear()

        def wide(kind, h):
            return [(kind, h, j) for j in range(GROUPS)]

        values = [("v", 0, t) for t in range(0, TILES, 2)]
        items = wide("k", 0) + wide("q", 0) + values + wide("g", 0) + wide("k", 1) + wide("q", 1) + wide("g", 1)
        nth = {item: i for i, item in enumerate(items)}
        column = {"q": 0, "k": 2, "g": 4}

        def share(pe, which):
            for m in which:
                if m >= 2:
                    pe.wait_ge(sem["yadd"], m - 1)
                for t in (2 * SHARES[m], 2 * SHARES[m] + 1):
                    for h in range(2):
                        last = product(nc, YB[m % 2][:, (t % 2) * D:(t % 2 + 1) * D],
                                       [part[:, h, t * P:(t + 1) * P] for part in ogs],
                                       [part[:, h, :] for part in wo], h == 0, h == 1)
                last.then_inc(sem["y"], 1)
                yield

        def add_share(ve, m):
            i = SHARES[m]
            ve.wait_ge(sem["y"], m + 1)
            at = yacc[:, 2 * i:2 * i + 2, :].rearrange("p t n -> p (t n)")
            nc.vector.tensor_tensor(at, at, YB[m % 2][:], ALU.add).then_inc(sem["yadd"], 1)

        with nc.Fori(0, PAIRS) as pr:
            with nc.Block() as block:
                @block.sync
                def _(sp):
                    load_pair(sp, (pr + 1) % PAIRS, sem["next"])
                    sp.dma_start(wo_raw[:], ins["wo1"][bass.ds(pr, 1)].rearrange("o p k n -> (o p) k n"))\
                      .then_inc(sem["load"], 16)
                    sp.wait_ge(sem["next"], 16)

                @block.scalar
                def _(a):
                    a.wait_ge(sem["sneg"], 1)
                    for h in range(2):
                        s = small[:, h, 0:1]
                        nc.scalar.activation(dmask[:, h, :], steps[:, 0, :], ACT.Exp, scale=s)
                        nc.scalar.activation(qdec[:, h, :], steps[:, 2, :], ACT.Exp, scale=s)
                        last = nc.scalar.activation(kbdec[:, h, :], steps[:, 3, 0:2], ACT.Exp, scale=s)
                    last.then_inc(sem["dec"], 1)

                    def drain(some):
                        for item in some:
                            kind, h, j = item
                            i = nth[item]
                            if item == ("k", 1, 0):
                                a.wait_ge(sem["ktr"], GROUPS)
                                a.wait_ge(sem["sc"], GROUPS)
                            if item == ("q", 1, 0):
                                a.wait_ge(sem["qd"], GROUPS)
                            n = h * GROUPS + j
                            if kind == "g" and n >= 2:
                                a.wait_ge(sem["og"], n - 1)
                            a.wait_ge(sem["proj"], i + 1)
                            src = PROJ[i % 2][:]
                            if kind == "v":
                                dst = v[:, j:j + 2, :].rearrange("p t n -> p (t n)")
                            else:
                                at = slice(j * GN, (j + 1) * GN)
                                dst = {"q": qT[:, at], "k": kT[:, at], "g": gT[:, n % 2, :]}[kind]
                            f, scale = (ACT.Tanh, 0.5) if kind == "g" else (ACT.Silu, 1.0)
                            nc.scalar.activation(dst, src, f, scale=scale).then_inc(sem["evac"], 1)

                    def head(h):
                        for j in range(GROUPS + 2):
                            if j < GROUPS:
                                drain([("g", h, j)])
                            if 1 <= j <= GROUPS:
                                n = h * GROUPS + j - 1
                                a.wait_ge(sem["o"], n + 1)
                                if n >= 2:
                                    a.wait_ge(sem["og"], n - 1)
                                nc.scalar.copy(oT[:, n % 2, :], OB[n % 2][:]).then_inc(sem["oT"], 1)
                                if n >= 2:
                                    a.wait_ge(sem["ssum"], n - 1)
                                a.wait_ge(sem["oT"], n + 1)
                                nc.scalar.activation(sq[:, n % 2, :], oT[:, n % 2, :], ACT.Square).then_inc(sem["sq"], 1)
                            if h and j == GROUPS:
                                split_weights("g", a=a)
                            if h == 0 and j >= GROUPS:
                                drain([("k", 1, j - GROUPS)])
                            if j >= 2:
                                n = h * GROUPS + j - 2
                                a.wait_ge(sem["og"], n + 1)
                                if n == 0:
                                    a.wait_ge(sem["y"], LATE)
                                nc.scalar.copy(ogs[0][:, h, (j - 2) * GN:(j - 1) * GN],
                                               og[:, n % 2, :]).then_inc(sem["ogh"], 1)

                    drain(wide("k", 0) + wide("q", 0) + values)
                    a.wait_ge(sem["next"], 16)
                    split_weights("v", a=a)
                    head(0)
                    drain(wide("k", 1)[2:] + wide("q", 1))
                    split_weights("qk", a=a)
                    a.wait_ge(sem["load"], 16)
                    nc.scalar.copy(wo[0][:], wo_raw[:]).then_inc(sem["woh"], 1)
                    head(1)

                @block.tensor
                def _(pe):
                    def project(item):
                        kind, h, j = item
                        i = nth[item]
                        if i >= 2:
                            pe.wait_ge(sem["evac"], i - 1)
                        out = PROJ[i % 2]
                        if kind == "v":
                            for t in range(2):
                                for k in range(KD):
                                    last = product(nc, out[:, t * 2 * D1:(t + 1) * 2 * D1],
                                                   [part[:, k, (j + t) * P:(j + t + 1) * P] for part in hT],
                                                   [part[:, k, 6 * D1:8 * D1] for part in w], k == 0, k == KD - 1)
                        else:
                            at = (column[kind] + h) * D1
                            for k in range(KD):
                                last = product(nc, out[:], [part[:, k, at:at + D1] for part in w],
                                               [part[:, k, j * GN:(j + 1) * GN] for part in hT], k == 0, k == KD - 1)
                        last.then_inc(sem["proj"], 1)

                    def turn_keys(h, j):
                        n = h * GROUPS + j
                        pe.wait_ge(sem["evac"], nth[("k", h, j)] + 1)
                        if n:
                            pe.wait_ge(sem["ktok"], n)
                        if h and j == 0:
                            pe.wait_ge(sem["oT"], GROUPS)
                        for t in range(GT):
                            b = j * GT + t
                            last = nc.tensor.transpose(KTR[:, t * P:(t + 1) * P], kT[:, b * P:(b + 1) * P], ident[:])
                        last.then_inc(sem["ktr"], 1)

                    def block_scores(h, j):
                        n = h * GROUPS + j
                        pe.wait_ge(sem["evac"], nth[("q", h, j)] + 1)
                        if n:
                            pe.wait_ge(sem["sm"], n)
                        for t in range(GT):
                            b = j * GT + t
                            last = nc.tensor.matmul(SC[:, t * P:(t + 1) * P], kT[:, b * P:(b + 1) * P],
                                                    qT[:, b * P:(b + 1) * P], start=True, stop=True)
                        last.then_inc(sem["sc"], 1)

                    def deltas(h, j):
                        n = h * GROUPS + j
                        pe.wait_ge(sem["ktok"], n + 1)
                        pe.wait_ge(sem["evac"], nth[values[-1]] + 1)
                        if n:
                            pe.wait_ge(sem["st"], h * (TILES - 1) + j * GT)
                        for b in range(j * GT, min(j * GT + GT, TILES - 1)):
                            t = b % GT
                            last = nc.tensor.matmul(DL[:, t * P:(t + 1) * P], ktok[:, b, :],
                                                    v[:, b, h * D1:(h + 1) * D1], start=True, stop=True)
                        last.then_inc(sem["dl"], 1)

                    def attend(h, j):
                        n = h * GROUPS + j
                        pe.wait_ge(sem["sm"], n + 1)
                        pe.wait_ge(sem["st"], h * (TILES - 1) + j * GT + GT - 1)
                        pe.wait_ge(sem["qd"], n + 1)
                        if n >= 2:
                            pe.wait_ge(sem["oT"], n - 1)
                        for t in range(GT):
                            b = j * GT + t
                            out = OB[n % 2][:, t * P:(t + 1) * P]
                            last = nc.tensor.matmul(out, v[:, b, h * D1:(h + 1) * D1], smask[:, n % 2, t, :],
                                                    start=True, stop=(b == 0))
                            if b:
                                last = nc.tensor.matmul(out, state[:, b, :], qd[:, b * P:(b + 1) * P],
                                                        start=False, stop=True)
                        last.then_inc(sem["o"], 1)

                    def head(h):
                        for j in range(GROUPS + 1):
                            if j < GROUPS:
                                deltas(h, j)
                                block_scores(h, j)
                                project(("g", h, j))
                            if j:
                                attend(h, j - 1)

                    before = share(pe, range(LATE))
                    for item in wide("k", 0) + wide("q", 0):
                        project(item)
                        next(before, None)
                    for i, item in enumerate(values):
                        project(item)
                        if i % 2:
                            turn_keys(0, i // 2)
                    head(0)
                    for item in wide("k", 1):
                        project(item)
                    for j, item in enumerate(wide("q", 1)):
                        project(item)
                        turn_keys(1, j)
                    head(1)
                    pe.wait_ge(sem["wol"], 1)
                    for m in range(LATE, TILES // 2):
                        pe.wait_ge(sem["ogl"], GROUPS + (2 * SHARES[m] + 1) // GT + 1)
                        for _ in share(pe, (m,)):
                            pass

                @block.gpsimd
                def _(gp):
                    nc.gpsimd.tensor_copy(small[:, :, 0], slope[:, bass.ds(pr * 2, 2)])
                    nc.gpsimd.tensor_copy(small[:, :, 1], nw[:, bass.ds(pr * 2, 2)]).then_inc(sem["small"], 1)

                    def decay_queries(h):
                        gp.wait_ge(sem["dec"], 1)
                        for j in range(GROUPS):
                            gp.wait_ge(sem["evac"], nth[("q", h, j)] + 1)
                            if h:
                                gp.wait_ge(sem["o"], j + 1)
                            at = slice(j * GN, (j + 1) * GN)
                            nc.gpsimd.tensor_tensor(qd[:, at].rearrange("p (b m) -> p b m", m=P),
                                                    qT[:, at].rearrange("p (b m) -> p b m", m=P),
                                                    qdec[:, h, :].unsqueeze(1).to_broadcast([P, GT, P]),
                                                    ALU.mult).then_inc(sem["qd"], 1)

                    def outs(h):
                        for j in range(GROUPS):
                            n = h * GROUPS + j
                            at = slice(j * GN, (j + 1) * GN)
                            if n < 2 * GROUPS - 1:
                                if n >= GROUPS:
                                    gp.wait_ge(sem["ssum"], n - GROUPS + 1)
                                add_squares(n, gp, nc.gpsimd)
                            gp.wait_ge(sem["ogh"], n + 1)
                            nc.gpsimd.tensor_tensor(ogs[1][:, h, at], og[:, n % 2, :], ogs[0][:, h, at].bitcast(F32),
                                                    ALU.subtract).then_inc(sem["ogl"], 1)

                    decay_queries(0)
                    split_weights("v", gp=gp)
                    outs(0)
                    decay_queries(1)
                    split_weights("qk", gp=gp)
                    gp.wait_ge(sem["woh"], 1)
                    gp.wait_ge(sem["y"], LATE)
                    nc.gpsimd.tensor_tensor(wo[1][:], wo_raw[:], wo[0][:].bitcast(F32),
                                            ALU.subtract).then_inc(sem["wol"], 1)
                    outs(1)

                @block.vector
                def _(ve):
                    chain = Chain(ve, sem["vec"])
                    ve.wait_ge(sem["small"], 1)
                    chain.did(nc.vector.tensor_scalar(small[:, :, 1], small[:, :, 1], 0.5, None, ALU.mult))
                    nc.vector.tensor_scalar(small[:, :, 0], small[:, :, 0], -1.0, None, ALU.mult).then_inc(sem["sneg"], 1)
                    ve.wait_ge(sem["dec"], 1)
                    chain.link(nc.vector.tensor_tensor(dmask[:], dmask[:],
                                                       steps[:, 1:2, :].to_broadcast([P, 2, P]), ALU.mult))

                    def take_keys(h):
                        for j in range(GROUPS):
                            n = h * GROUPS + j
                            ve.wait_ge(sem["ktr"], n + 1)
                            if h and j == 0:
                                ve.wait_ge(sem["dl"], GROUPS)
                            nc.vector.tensor_scalar(ktok[:, j * GT:(j + 1) * GT, :].rearrange("p t d -> p (t d)"),
                                                    KTR[:], kbdec[:, h, 1:2], None, ALU.mult).then_inc(sem["ktok"], 1)

                    def states(h, j):
                        ve.wait_ge(sem["dl"], h * GROUPS + j + 1)
                        if h and j == 0:
                            ve.wait_ge(sem["o"], GROUPS)
                        for b in range(j * GT, min(j * GT + GT, TILES - 1)):
                            if b:
                                ve.wait_ge(sem["st"], h * (TILES - 1) + b)
                            nc.vector.scalar_tensor_tensor(state[:, b + 1, :], state[:, b, :], kbdec[:, h, 0:1],
                                                           DL[:, (b % GT) * P:(b % GT + 1) * P], ALU.mult,
                                                           ALU.add).then_inc(sem["st"], 1)

                    def mask_scores(h, j):
                        n = h * GROUPS + j
                        ve.wait_ge(sem["sc"], n + 1)
                        if n >= 2:
                            ve.wait_ge(sem["o"], n - 1)
                        nc.vector.tensor_tensor(smask[:, n % 2], SC[:].rearrange("p (t m) -> p t m", t=GT),
                                                dmask[:, h, :].unsqueeze(1).to_broadcast([P, GT, P]),
                                                ALU.mult).then_inc(sem["sm"], 1)

                    def weigh_gate(h, j):
                        n = h * GROUPS + j
                        ve.wait_ge(sem["evac"], nth[("g", h, j)] + 1)
                        at = gT[:, n % 2, :]
                        nc.vector.tensor_scalar(at, at, 1.0, small[:, h, 1:2], ALU.add, ALU.mult).then_inc(sem["g"], 1)

                    def gate(h, j):
                        n = h * GROUPS + j
                        ve.wait_ge(sem["g"], n + 1)
                        ve.wait_ge(sem["oT"], n + 1)
                        if n >= 2:
                            ve.wait_ge(sem["ogl"], n - 1)
                        nc.vector.tensor_tensor(og[:, n % 2, :], oT[:, n % 2, :], gT[:, n % 2, :],
                                                ALU.mult).then_inc(sem["og"], 1)

                    for m in range(LATE):
                        add_share(ve, m)
                    for h in range(2):
                        take_keys(h)
                        for j in range(GROUPS + 1):
                            if j < GROUPS:
                                states(h, j)
                                mask_scores(h, j)
                                weigh_gate(h, j)
                            if j:
                                gate(h, j - 1)
                    add_share(ve, LATE)
                    split_weights("g", ve=ve)
                    add_share(ve, LATE + 1)
                    ve.wait_ge(sem["ssum"], 2 * GROUPS - 1)
                    add_squares(2 * GROUPS - 1, ve, nc.vector)
                    for m in range(LATE + 2, TILES // 2):
                        add_share(ve, m)
            sem.clear()

        ORDER = [*range(LATE, TILES // 2), *range(LATE)]
        POOL_ADDS = 5

        def add_saved(ops, m):
            at = slice(2 * SHARES[m], 2 * SHARES[m] + 2)
            ops.tensor_tensor(x[:, at, :], yacc[:, at, :], v[:, at, :], ALU.add)

        with nc.Block() as block:
            @block.tensor
            def _(pe):
                for t in range(TILES):
                    last = nc.tensor.matmul(bank[0][:, t:t + 1], ssum[:, t * P:(t + 1) * P], ones[:], start=True, stop=True)
                last.then_inc(sem["ss"], 1)
                for _ in share(pe, range(LATE)):
                    pass

            @block.sync
            def _(sp):
                sp.dma_start(v[:], x_dram).then_inc(sem["load"], 16)

            @block.scalar
            def _(a):
                a.wait_ge(sem["ss"], 1)
                nc.scalar.activation(rms[:, 0, :], bank[0][:, 0:TILES], ACT.Sqrt, bias=reps[:],
                                     scale=1.0 / F1).then_inc(sem["rstd"], 1)

            @block.vector
            def _(ve):
                chain = Chain(ve, sem["vec"])
                ve.wait_ge(sem["rstd"], 1)
                chain.link(nc.vector.reciprocal(rms[:, 1, :], rms[:, 0, :]))
                for m in ORDER:
                    if m < LATE:
                        add_share(ve, m)
                        ve.wait_ge(sem["yadd"], m + 1)
                    for t in (2 * SHARES[m], 2 * SHARES[m] + 1):
                        nc.vector.scalar_tensor_tensor(yacc[:, t, :], yacc[:, t, :], rms[:, 1, t:t + 1],
                                                       gates[:, 1, 0, :], ALU.mult, ALU.mult).then_inc(sem["g"], 1)
                ve.wait_ge(sem["load"], 16)
                ve.wait_ge(sem["g"], TILES)
                for m in ORDER[POOL_ADDS:]:
                    add_saved(nc.vector, m)

            @block.gpsimd
            def _(gp):
                gp.wait_ge(sem["load"], 16)
                for i, m in enumerate(ORDER[:POOL_ADDS]):
                    gp.wait_ge(sem["g"], 2 * i + 2)
                    add_saved(nc.gpsimd, m)
        sem.clear()


def ternary_ffn(nc, bank, x, ident, eps, mods, gates, ins, out):
    with ExitStack() as c:
        sb = lambda n, s, dt=F32: c.enter_context(nc.sbuf_tensor(f"tf_{n}", s, dt))
        norm = Norm(nc, c, "tf", ident, eps, bank[0:2])
        h = sb("h", [P, KD, GN])
        hT = [sb("hh", [P, KD, S], F32R), sb("hl", [P, KD, S], F32R)]
        raw = sb("raw", [P, 3, KD * DE])
        low = sb("low", [P, 3, KD * DE])
        junk = sb("junk", [P, KD * DE])
        tern = sb("tern", [P, 3, KD * DE], F32R)
        asum = sb("asum", [P, 3])
        ones = sb("ones", [P, P])
        scale = sb("scale", [P, 3])
        half = sb("half", [P, 2, 3])
        hid = sb("hid", [P, 2, GN])
        hids = [sb("hidh", [P, KE, GN], F32R), sb("hidl", [P, KE, GN], F32R)]
        act = sb("act", [P, 2, GN])
        upd = sb("upd", [P, GT, D])
        sem = Stage(nc, c, "tf", *LN_SEMS, "load", "load2", "load3", "abs", "ones", "sum", "half", "wd", "up", "gate", "silu",
                    "hid", "hidh", "hidl", "store", "xdone")
        wu = tern[:, 0, :].rearrange("p (k n) -> p k n", k=KD)
        wg = tern[:, 1, :].rearrange("p (k n) -> p k n", k=KD)
        wd = tern[:, 2, :].rearrange("p (k n) -> p k n", k=KE)
        loaded = ("load", "load2", "load3")
        rows = lambda g: x[:, bass.ds(g * GT, GT), :]
        parts = lambda g: [part[:, :, bass.ds(g * GN, GN)] for part in hT]
        factor, shift = mods[:, 1, 1, 1, :], mods[:, 1, 1, 0, :]

        def round_weights(v, i):
            return nc.vector.scalar_tensor_tensor(tern[:, i, :], raw[:, i, :], half[:, 0, i:i + 1], low[:, i, :],
                                                  ALU.is_gt, ALU.subtract)

        with nc.Block() as block:
            @block.sync
            def _(sp):
                for i, name in enumerate(("wup", "wgate", "wdown")):
                    sp.dma_start(raw[:, i, :], ins[name]).then_inc(sem[loaded[i]], 16)

            @block.scalar
            def _(a):
                norm.scalar_std(nc, a, sem)
                for i in range(3):
                    a.wait_ge(sem[loaded[i]], 16)
                    nc.scalar.activation(junk[:], raw[:, i, :], ACT.Abs, accum_out=asum[:, i:i + 1])\
                      .then_inc(sem["abs"], 1)
                    a.wait_ge(sem["abs"], i + 1)
                    if i == 0:
                        norm.modulate(nc, a, None, sem, h, factor, shift)
                        norm.split(nc, a, None, sem, h, *parts(0))

            @block.vector
            def _(v):
                chain = Chain(v, sem["vec"])
                nc.vector.memset(ones[:], 1.0).then_inc(sem["ones"], 1)
                norm.vector(nc, v, chain, sem, rows(0))
                norm.modulate(nc, None, v, sem, h, factor, shift)
                norm.split(nc, None, v, sem, h, *parts(0))
                for i in range(3):
                    one = slice(i, i + 1)
                    v.wait_ge(sem["sum"], i + 1)
                    chain.link(nc.vector.tensor_scalar(scale[:, one], bank[2 + i][:, 0:1], 1.0 / (D * DE), 1e-8,
                                                       ALU.mult, ALU.add))
                    nc.vector.tensor_scalar(half[:, 0, one], scale[:, one], 0.5, None, ALU.mult).then_inc(sem["half"], 1)
                    nc.vector.tensor_scalar(half[:, 1, one], scale[:, one], -0.5, None, ALU.mult).then_inc(sem["half"], 1)
                    v.wait_ge(sem["half"], 2 * i + 2)
                    chain.link(nc.vector.tensor_scalar(low[:, i, :], raw[:, i, :], half[:, 1, one], None, ALU.is_lt))
                    if i < 2:
                        round_weights(v, i)

            @block.tensor
            def _(pe):
                norm.tensor(nc, pe, sem)
                pe.wait_ge(sem["ones"], 1)
                for i in range(3):
                    pe.wait_ge(sem["abs"], i + 1)
                    nc.tensor.matmul(bank[2 + i][:, 0:1], ones[:], asum[:, i:i + 1], start=True, stop=True)\
                      .then_inc(sem["sum"], 1)
        sem.clear()

        def finish(v, chain, g, some=range(GT // 2)):
            for i in some:
                y = bank[6 + i][:].rearrange("p (t n) -> p t n", t=2)
                to = x[:, bass.ds(g * GT + 2 * i, 2), :]
                chain.link(nc.vector.scalar_tensor_tensor(
                    upd[:, 2 * i:2 * i + 2, :], y, scale[:, 2:3],
                    gates[:, 1, 1:2, :].to_broadcast([P, 2, D]), ALU.mult, ALU.mult))
                nc.vector.tensor_tensor(to, to, upd[:, 2 * i:2 * i + 2, :], ALU.add).then_inc(sem["xdone"], 1)

        def store(sp, g):
            for i in range(GT // 2):
                sp.wait_ge(sem["xdone"], i + 1)
                at = bass.ds(g * GT + 2 * i, 2)
                sp.dma_start(out[:, at, :], x[:, at, :]).then_inc(sem["store"], 16)
            sp.wait_ge(sem["store"], 32)

        def turn(g, first=False, last=False):
            with nc.Block() as block:
                @block.tensor
                def _(pe):
                    high, low_ = parts(g)
                    for e in range(KE):
                        for w, banks, done, used in ((wu, bank[2:4], "up", "silu"), (wg, bank[4:6], "gate", "hid")):
                            if e >= 2:
                                pe.wait_ge(sem[used], e - 1)
                            for k in range(KD):
                                nc.tensor.matmul(banks[e % 2][:], w[:, k, e * P:(e + 1) * P], high[:, k, :],
                                                 start=(k == 0), stop=False)
                                mm = nc.tensor.matmul(banks[e % 2][:], w[:, k, e * P:(e + 1) * P], low_[:, k, :],
                                                      start=False, stop=(k == KD - 1))
                            mm.then_inc(sem[done], 1)
                    if first:
                        pe.wait_ge(sem["wd"], 1)
                    else:
                        pe.wait_ge(sem["xdone"], GT // 2)
                    for n, (t, some) in enumerate(((0, range(KE - 1)), (2, range(KE - 1)),
                                                   (0, (KE - 1,)), (2, (KE - 1,)),
                                                   (1, range(KE)), (3, range(KE)))):
                        if n == 4 and not last:
                            norm.tensor(nc, pe, sem)
                        at = bank[6 + t // 2][:, (t % 2) * D:(t % 2 + 1) * D]
                        for e in some:
                            if t == 0:
                                pe.wait_ge(sem["hidh"], e + 1)
                                pe.wait_ge(sem["hidl"], e + 1)
                            for p, part in enumerate(hids):
                                mm = nc.tensor.matmul(at, part[:, e, t * P:(t + 1) * P], wd[:, e, :],
                                                      start=(e == 0 and p == 0), stop=(e == KE - 1 and p == 1))

                @block.scalar
                def _(a):
                    for e in range(KE + 1):
                        if e < KE:
                            a.wait_ge(sem["up"], e + 1)
                            if e >= 2:
                                a.wait_ge(sem["hid"], e - 1)
                            nc.scalar.activation(act[:, e % 2, :], bank[2 + e % 2][:], ACT.Silu,
                                                 scale=scale[:, 0:1]).then_inc(sem["silu"], 1)
                        if e:
                            a.wait_ge(sem["hid"], e)
                            nc.scalar.copy(hids[0][:, e - 1, :], hid[:, (e - 1) % 2, :]).then_inc(sem["hidh"], 1)
                    if not last:
                        norm.scalar_std(nc, a, sem)
                        norm.modulate(nc, a, None, sem, h, factor, shift)
                        norm.split(nc, a, None, sem, h, *parts(g + 1))

                @block.gpsimd
                def _(gp):
                    for e in range(KE):
                        gp.wait_ge(sem["hidh"], e + 1)
                        nc.gpsimd.tensor_tensor(hids[1][:, e, :], hid[:, e % 2, :], hids[0][:, e, :].bitcast(F32),
                                                ALU.subtract).then_inc(sem["hidl"], 1)

                @block.vector
                def _(v):
                    chain = Chain(v, sem["vec"])
                    for e in range(KE):
                        v.wait_ge(sem["silu"], e + 1)
                        v.wait_ge(sem["gate"], e + 1)
                        if e >= 2:
                            v.wait_ge(sem["hidl"], e - 1)
                        nc.vector.scalar_tensor_tensor(hid[:, e % 2, :], bank[4 + e % 2][:], scale[:, 1:2],
                                                       act[:, e % 2, :], ALU.mult, ALU.mult).then_inc(sem["hid"], 1)
                        if e in (1, 3) and not first:
                            finish(v, chain, g - 1, (e // 2,))
                        if e == 5 and not last:
                            norm.moments(nc, v, chain, sem, rows(g + 1))
                        if e == 3 and first:
                            round_weights(v, 2).then_inc(sem["wd"], 1)
                    if not last:
                        norm.normalize(nc, v, chain, sem, rows(g + 1))
                        norm.modulate(nc, None, v, sem, h, factor, shift)
                        norm.split(nc, None, v, sem, h, *parts(g + 1))

                if not first:
                    @block.sync
                    def _(sp):
                        store(sp, g - 1)
            sem.clear()

        turn(0, first=True)
        with nc.Fori(1, GROUPS - 1) as g:
            turn(g)
        turn(GROUPS - 1, last=True)
        with nc.Block() as block:
            @block.vector
            def _(v):
                finish(v, Chain(v, sem["vec"]), GROUPS - 1)

            @block.sync
            def _(sp):
                store(sp, GROUPS - 1)
        sem.clear()


class Banks:

    def __init__(self, whole):
        self.whole = whole
        self.each = [whole[:, i, :] for i in range(8)]

    def __getitem__(self, i):
        return self.each[i]


def build(nc, ins, out, keep=99):
    parts_dram = nc.dram_tensor("qk_parts", [2, 3, D, S], BF16, kind="Internal").ap()
    x_dram = nc.dram_tensor("x_saved", [P, TILES, D], F32, kind="Internal").ap()
    with ExitStack() as ctx:
        sb = lambda n, s, dt=F32: ctx.enter_context(nc.sbuf_tensor(n, s, dt))
        bank = Banks(ctx.enter_context(nc.psum_tensor("psum", [P, 8, 512], F32)))
        x = sb("x", [P, TILES, D])
        ident = sb("ident", [P, P])
        eps = sb("eps", [P, 1])
        mods = sb("mods", [P, 2, 2, 2, KD])
        gates = sb("gates", [P, 2, 2, D])
        modulation(nc, bank, x, ident, eps, mods, gates, ins)
        with ExitStack() as c0:
            attn = c0.enter_context(nc.sbuf_tensor("attn", [P, TILES, D], F32))
            with nc.sbuf_tensor("v_all", [P, TILES, D], F32) as v_all:
                rope_front(nc, bank, x, v_all, ident, eps, mods, parts_dram, ins)
                rope_attention(nc, bank, v_all, attn, ident, parts_dram, ins)
            routed_ffn(nc, bank, x, attn, ident, eps, mods, gates, ins)
        with nc.sbuf_tensor("h1h", [P, KD, S], F32R) as high, nc.sbuf_tensor("h1l", [P, KD, S], F32R) as low:
            with ExitStack() as c1:
                one = lambda n, s: c1.enter_context(nc.sbuf_tensor(f"first_{n}", s, F32))
                first = (one("raw", [P, KD, 8 * D1]),
                         one("nw", [P, H1]), one("slope", [P, H1]),
                         one("steps", [P, 4, P]))
                decay_front(nc, bank, x, (high, low), first, ident, eps, mods, x_dram, ins)
                decay_attention(nc, bank, x, (high, low), first, ident, gates, x_dram, ins)
        ternary_ffn(nc, bank, x, ident, eps, mods, gates, ins, out)


def lay_out(i, np):
    kp = lambda a: np.ascontiguousarray(a.reshape(-1, P, a.shape[-1]).transpose(1, 0, 2))
    o = {}
    o["x"] = i["L0_attn_x"].reshape(TILES, P, D).transpose(1, 0, 2)
    o["ident"] = np.eye(P, dtype=np.float32)
    for l in range(2):
        o[f"c{l}"] = i[f"L{l}_c"].reshape(KD, P).T
        o[f"wmod{l}"] = kp(i[f"L{l}_wmod"])
    o["wqk"] = kp(np.concatenate([i["L0_attn_wq"].T, i["L0_attn_wk"].T], axis=1))
    o["wv"] = kp(i["L0_attn_wv"].T)
    pos = np.arange(S, dtype=np.float32)[:, None]
    inv = np.float32(10000.0) ** (-(np.arange(0, DK, 2, dtype=np.float32) / np.float32(DK)))
    ang = (pos * inv.astype(np.float32)).astype(np.float32)
    cos, sin = np.cos(ang), np.sin(ang)
    cos = np.stack([cos, cos], -1).reshape(TILES, P, DK)
    sin = np.stack([-sin, sin], -1).reshape(TILES, P, DK)
    o["cos"] = cos.transpose(1, 0, 2).astype(np.float32)
    o["sin"] = sin.transpose(1, 0, 2).astype(np.float32)
    r = np.arange(P)
    later = r[None, :] > r[:, None]
    o["mask"] = np.where(later, np.float32(-1e30), np.float32(0))
    o["wo"] = kp(i["L0_attn_wo"].T)
    a = i["L0_ffn_A"].reshape(D, D)
    o["wbase"] = kp(np.concatenate([i["L0_ffn_W"].T, a.T], axis=1))
    o["wexp"] = kp(i["L0_ffn_B"].transpose(0, 2, 1).reshape(D, D))
    o["rw1"] = kp(i["L0_ffn_rw1"].T)
    o["rw2"] = i["L0_ffn_rw2"][:EXPERTS].T
    o["rb1"] = i["L0_ffn_rb1"].reshape(RHID, 1)
    o["rows"] = np.stack([i["L0_ffn_rb2"][:EXPERTS], i["L0_ffn_gates"]]).reshape(1, 2, EXPERTS)
    o["bias"] = i["L0_ffn_bias"].reshape(1, D)
    o["iota"] = np.tile(np.arange(EXPERTS, dtype=np.float32), (P, 1))
    w = i["L1_attn_Wqkv"].reshape(PAIRS, 2, 3, D1, D)
    wg = i["L1_attn_Wg"].reshape(PAIRS, 2, D1, D)
    each = np.stack([w[:, 0, 0], w[:, 1, 0], w[:, 0, 1], w[:, 1, 1], wg[:, 0], wg[:, 1], w[:, 0, 2], w[:, 1, 2]], 1)
    each = each.reshape(PAIRS, 8 * D1, KD, P)
    o["wpair"] = each.transpose(0, 3, 2, 1)
    o["wo1"] = i["L1_attn_Wo"].reshape(D, PAIRS, 2, D1).transpose(1, 3, 2, 0)
    o["nw"] = i["L1_attn_norm_w"].reshape(H1, D1).T
    o["slope"] = np.tile(i["L1_attn_slope_rate"].reshape(1, H1), (P, 1))
    m, n = r[None, :], r[:, None]
    last = np.zeros((P, P), np.float32)
    last[:, 0] = P
    last[:, 1] = P - 1 - r
    o["steps"] = np.stack([np.maximum(m - n, 0), m >= n, np.broadcast_to(m + 1, (P, P)), last], 1).astype(np.float32)
    o["wup"] = kp(i["L1_ffn_W_up"].T).reshape(P, KD * DE)
    o["wgate"] = kp(i["L1_ffn_W_gate"].T).reshape(P, KD * DE)
    o["wdown"] = kp(i["L1_ffn_W_down"].T).reshape(P, KE * D)
    return {k: np.ascontiguousarray(a) for k, a in o.items()}


def kernel(**inputs):
    import numpy as np
    import concourse.bacc as bacc
    from concourse.bass_utils import run_bass_kernel_spmd

    arrays = lay_out({k: np.asarray(a) for k, a in inputs.items()}, np)
    nc = bacc.Bacc("TRN2", target_bir_lowering=False, num_devices=1)
    ins = {k: nc.dram_tensor(f"in_{k}", a.shape, mybir.dt.from_np(a.dtype), kind="ExternalInput").ap()
           for k, a in arrays.items()}
    out = nc.dram_tensor("out", [P, TILES, D], F32, kind="ExternalOutput").ap()
    build(nc, ins, out)
    r = run_bass_kernel_spmd(nc, [{f"in_{k}": a for k, a in arrays.items()}], core_ids=[0])
    return r.results[0]["out"].transpose(1, 0, 2).reshape(1, S, D)
```
